# Optimizing a Trainium2 kernel written in Bass

```python
import numpy as np
import jax
import jax.numpy as jnp

def _softmax(x, axis=-1):
    return jax.nn.softmax(x, axis=axis)

def _gelu(x):
    return jax.nn.gelu(x, approximate=True)

def _silu(x):
    return jax.nn.silu(x)

def _sigmoid(x):
    return jax.nn.sigmoid(x)

def _layernorm(x, axis=-1, eps=1e-05):
    m = jnp.mean(x, axis=axis, keepdims=True)
    v = jnp.var(x, axis=axis, keepdims=True)
    return (x - m) / jnp.sqrt(v + eps)

def _scatter_add(tgt, idx, src, axis=0):
    return tgt.at[idx].add(src)

def _segment_sum(src, seg, n):
    return jax.ops.segment_sum(src, seg, n)
kernel_name = 'mk_adj_resnorm_d4_adj_r2_6e0825'

def setup_inputs(seed: int=0):
    np.random.seed(seed)
    _w = jnp.asarray

    def _rec_inputs():
        import jax
        import jax.numpy as jnp
        _gk = jax.random.key(seed)
        x = -0.000929 + 1 * jax.random.normal(jax.random.fold_in(_gk, 1), (8, 1024, 64), jnp.float32)
        _w = (1.0 + jnp.arange(1024, dtype=jnp.float32)) ** (-0.5)
        _w = _w / _w.mean()
        _pij = jnp.clip(0.00390625 * _w[:, None] * _w[None, :], 0.0, 1.0)
        _a = jax.random.uniform(jax.random.fold_in(_gk, 2), (1024, 1024)) < _pij
        _a = jnp.logical_or(_a, jnp.eye(1024, dtype=bool))
        _af = _a.astype(jnp.float32)
        adj = _af
        return (x, adj)
    x, adj = _rec_inputs()

    def _L0_gnn_setup():
        import jax, jax.numpy as jnp
        import numpy as np
        NEG = -1000000000.0
        key = jax.random.key(seed)
        ks = jax.random.split(key, 14)
        B, N, E, NF, NH = (8, 1024, 64, 64, 64)
        x = jax.random.normal(ks[0], (B, N, NF), dtype=jnp.float32)
        base = jax.nn.one_hot(jax.random.randint(ks[1], (N,), 0, E), E, dtype=jnp.float32)
        extra = (jax.random.uniform(ks[2], (N, E)) < 0.03).astype(jnp.float32)
        H = jnp.clip(base + extra, 0.0, 1.0)
        adj = (jax.random.uniform(ks[3], (N, N)) < 0.01).astype(jnp.float32)
        adj = jnp.clip(adj + jnp.eye(N, dtype=jnp.float32), 0.0, 1.0)
        s_in = 1.0 / np.sqrt(NF)
        s_h = 1.0 / np.sqrt(NH)
        W = jax.random.normal(ks[4], (NF, NH), dtype=jnp.float32) * s_in
        W_ind = jax.random.normal(ks[5], (NF, NH), dtype=jnp.float32) * s_in
        a_node = jax.random.normal(ks[6], (NH,), dtype=jnp.float32) * s_h
        a_gn = jax.random.normal(ks[7], (NH,), dtype=jnp.float32) * s_h
        a_ge = jax.random.normal(ks[8], (NH,), dtype=jnp.float32) * s_h
        fcW = jax.random.normal(ks[9], (NH, 2 * NH), dtype=jnp.float32) * s_h
        fcb = jnp.zeros((2 * NH,), dtype=jnp.float32)
        av = jax.random.normal(ks[10], (2 * NH,), dtype=jnp.float32) / np.sqrt(2 * NH)
        return {'x': x, 'H': H, 'adj': adj, 'nhid': NH, 'W': W, 'W_ind': W_ind, 'a_node': a_node, 'a_gn': a_gn, 'a_ge': a_ge, 'fcW': fcW, 'fcb': fcb, 'av': av}
    _L0_gnn_all = _L0_gnn_setup()
    _L0_gnn_in = {k: v for k, v in _L0_gnn_all.items() if k in ('H', 'W', 'W_ind', 'a_node', 'a_gn', 'a_ge', 'fcW', 'fcb', 'av')}
    del _L0_gnn_all

    def _L1_gnn_setup():
        import jax, jax.numpy as jnp
        import numpy as np
        NEG_INF = -1e+16

        def gat_layer(x, graph, W, b):
            h = x @ W
            s = jnp.einsum('bnd,bmd->bnm', h, h) * graph
            s = jnp.where(s == 0.0, NEG_INF, s)
            a = jax.nn.softmax(s, axis=2)
            return jnp.einsum('bnm,bmd->bnd', a, h) + b
        key = jax.random.key(seed)
        k1, k2, k3, k4, k5, k6 = jax.random.split(key, 6)
        B, N, C_IN, HID, HEADS, C_OUT = (16, 512, 64, 128, 8, 64)
        flow_x = jax.random.normal(k1, (B, N, C_IN), dtype=jnp.float32)
        graph = jax.random.randint(k2, (N, N), 0, 2).astype(jnp.float32)
        Wh = jax.random.normal(k3, (HEADS, C_IN, HID), dtype=jnp.float32)
        bh = jax.random.normal(k4, (HEADS, HID), dtype=jnp.float32)
        W_out = jax.random.normal(k5, (HID * HEADS, C_OUT), dtype=jnp.float32)
        b_out = jax.random.normal(k6, (C_OUT,), dtype=jnp.float32)
        return {'flow_x': flow_x, 'graph': graph, 'Wh': Wh, 'bh': bh, 'W_out': W_out, 'b_out': b_out}
    _L1_gnn_all = _L1_gnn_setup()
    _L1_gnn_in = {k: v for k, v in _L1_gnn_all.items() if k in ('Wh', 'bh', 'W_out', 'b_out')}
    del _L1_gnn_all

    def _L2_gnn_setup():
        import jax, jax.numpy as jnp
        import numpy as np
        MAX_STEPS = 3
        key = jax.random.key(seed)
        ks = jax.random.split(key, 7)
        B, N, D = (1, 4096, 64)
        return {'causal_vars': jax.random.normal(ks[0], (B, N, D), dtype=jnp.float32), 'adj_matrix': jax.random.uniform(ks[1], (N, N), dtype=jnp.float32), 'intervention_value': jax.random.normal(ks[2], (B, D), dtype=jnp.float32), 'W1': jax.random.normal(ks[3], (D, 2 * D), dtype=jnp.float32) * (1.0 / np.sqrt(2 * D)), 'b1': jax.random.normal(ks[4], (D,), dtype=jnp.float32) * 0.01, 'W2': jax.random.normal(ks[5], (D, D), dtype=jnp.float32) * (1.0 / np.sqrt(D)), 'b2': jax.random.normal(ks[6], (D,), dtype=jnp.float32) * 0.01, 'intervention_idx': 0}
    _L2_gnn_all = _L2_gnn_setup()
    _L2_gnn_in = {k: v for k, v in _L2_gnn_all.items() if k in ('intervention_value', 'W1', 'b1', 'W2', 'b2')}
    del _L2_gnn_all

    def _L3_gnn_setup():
        import jax, jax.numpy as jnp
        import numpy as np
        B, N, F_IN, F_OUT = (8, 1024, 64, 64)
        ALPHA = 0.2
        NEG = -9000000000000000.0
        key = jax.random.key(seed)
        k1, k2, k3, k4 = jax.random.split(key, 4)
        h = jax.random.normal(k1, (B, N, F_IN), dtype=jnp.float32)
        adj = jax.random.randint(k2, (N, N), 0, 2).astype(jnp.float32)
        W = jax.random.normal(k3, (F_OUT, F_IN), dtype=jnp.float32) * 0.05
        a = jax.random.normal(k4, (2 * F_OUT,), dtype=jnp.float32) * 0.05
        return {'h': h, 'adj': adj, 'W': W, 'a': a}
    _L3_gnn_all = _L3_gnn_setup()
    _L3_gnn_in = {k: v for k, v in _L3_gnn_all.items() if k in ('W', 'a')}
    del _L3_gnn_all
    return {'x': x, 'adj': adj, 'L0_gnn_H': _L0_gnn_in['H'], 'L0_gnn_W': _L0_gnn_in['W'], 'L0_gnn_W_ind': _L0_gnn_in['W_ind'], 'L0_gnn_a_node': _L0_gnn_in['a_node'], 'L0_gnn_a_gn': _L0_gnn_in['a_gn'], 'L0_gnn_a_ge': _L0_gnn_in['a_ge'], 'L0_gnn_fcW': _L0_gnn_in['fcW'], 'L0_gnn_fcb': _L0_gnn_in['fcb'], 'L0_gnn_av': _L0_gnn_in['av'], 'L1_gnn_Wh': _L1_gnn_in['Wh'], 'L1_gnn_bh': _L1_gnn_in['bh'], 'L1_gnn_W_out': _L1_gnn_in['W_out'], 'L1_gnn_b_out': _L1_gnn_in['b_out'], 'L2_gnn_intervention_value': _L2_gnn_in['intervention_value'], 'L2_gnn_W1': _L2_gnn_in['W1'], 'L2_gnn_b1': _L2_gnn_in['b1'], 'L2_gnn_W2': _L2_gnn_in['W2'], 'L2_gnn_b2': _L2_gnn_in['b2'], 'L3_gnn_W': _L3_gnn_in['W'], 'L3_gnn_a': _L3_gnn_in['a']}

def reference(x, adj, L0_gnn_H, L0_gnn_W, L0_gnn_W_ind, L0_gnn_a_node, L0_gnn_a_gn, L0_gnn_a_ge, L0_gnn_fcW, L0_gnn_fcb, L0_gnn_av, L1_gnn_Wh, L1_gnn_bh, L1_gnn_W_out, L1_gnn_b_out, L2_gnn_intervention_value, L2_gnn_W1, L2_gnn_b1, L2_gnn_W2, L2_gnn_b2, L3_gnn_W, L3_gnn_a):
    import jax
    import jax.numpy as jnp

    def _L0_gnn_ref(x, H, adj, nhid, W, W_ind, a_node, a_gn, a_ge, fcW, fcb, av):
        import jax, jax.numpy as jnp
        import numpy as np
        NEG = -1000000000.0
        h = x @ W
        maskEN = H.T
        s = jax.nn.leaky_relu(h @ a_node, 0.2)
        logits = jnp.where(maskEN[None, :, :] > 0, s[:, None, :], NEG)
        alpha = jax.nn.softmax(logits, axis=-1)
        agg = jnp.einsum('ben,bnf->bef', alpha, h)
        beta = jax.nn.sigmoid((h @ a_gn)[:, None, :] + (agg @ a_ge)[:, :, None])
        all_he = beta[..., None] * h[:, None, :, :] + (1.0 - beta[..., None]) * agg[:, :, None, :]
        deg = jnp.maximum(adj.sum(-1), 1.0)[:, None]
        industry = jnp.einsum('nm,bmf->bnf', adj / deg, x @ W_ind)
        all_he = jax.nn.elu(all_he)
        he = jax.nn.elu(agg)

        def attn_scores(f):
            return jnp.tanh(f @ fcW + fcb) @ av
        se = attn_scores(he)
        logits2 = jnp.where(H[None, :, :] > 0, se[:, None, :], NEG)
        coefs1 = jax.nn.softmax(logits2, axis=-1)
        g = jnp.einsum('bne,benf->bnf', coefs1, all_he)
        pair = jnp.stack([industry, g], axis=2)
        coefs2 = jax.nn.softmax(attn_scores(pair), axis=-1)
        out = jnp.einsum('bnk,bnkf->bnf', coefs2, pair)
        return out

    def _L1_gnn_ref(flow_x, graph, Wh, bh, W_out, b_out):
        import jax, jax.numpy as jnp
        import numpy as np
        NEG_INF = -1e+16

        def gat_layer(x, graph, W, b):
            h = x @ W
            s = jnp.einsum('bnd,bmd->bnm', h, h) * graph
            s = jnp.where(s == 0.0, NEG_INF, s)
            a = jax.nn.softmax(s, axis=2)
            return jnp.einsum('bnm,bmd->bnd', a, h) + b
        heads = jax.vmap(lambda W, b: gat_layer(flow_x, graph, W, b))(Wh, bh)
        H, B, N, D = heads.shape
        cat = jnp.moveaxis(heads, 0, 2).reshape(B, N, H * D)
        x = jax.nn.leaky_relu(cat, negative_slope=0.01)
        out = gat_layer(x, graph, W_out, b_out)
        return jax.nn.leaky_relu(out, negative_slope=0.01)

    def _L2_gnn_ref(causal_vars, adj_matrix, intervention_value, W1, b1, W2, b2, intervention_idx):
        import jax, jax.numpy as jnp
        import numpy as np
        MAX_STEPS = 3
        v = causal_vars.at[:, intervention_idx].set(intervention_value)
        for _ in range(MAX_STEPS):
            effects = jnp.einsum('nm,bmd->bnd', adj_matrix, v)
            h = jnp.concatenate([v, effects], axis=-1)
            h = jax.nn.relu(jnp.einsum('bnk,dk->bnd', h, W1) + b1)
            v = jnp.einsum('bnk,dk->bnd', h, W2) + b2
        return v

    def _L3_gnn_ref(h, adj, W, a):
        import jax, jax.numpy as jnp
        import numpy as np
        B, N, F_IN, F_OUT = (8, 1024, 64, 64)
        ALPHA = 0.2
        NEG = -9000000000000000.0
        Wh = jnp.einsum('bnf,of->bno', h, W)
        e1 = Wh @ a[:F_OUT]
        e2 = Wh @ a[F_OUT:]
        e = jax.nn.leaky_relu(e1[:, :, None] + e2[:, None, :], negative_slope=ALPHA)
        att = jnp.where(adj[None, :, :] > 0, e, NEG)
        att = jax.nn.softmax(att, axis=-1)
        h_prime = jnp.einsum('bij,bjo->bio', att, Wh)
        return jax.nn.elu(h_prime)
    x = _layernorm(x + _L0_gnn_ref(x, L0_gnn_H, adj, 64, L0_gnn_W, L0_gnn_W_ind, L0_gnn_a_node, L0_gnn_a_gn, L0_gnn_a_ge, L0_gnn_fcW, L0_gnn_fcb, L0_gnn_av), axis=-1)
    x = _layernorm(x + _L1_gnn_ref(x, adj, L1_gnn_Wh, L1_gnn_bh, L1_gnn_W_out, L1_gnn_b_out), axis=-1)
    x = _layernorm(x + _L2_gnn_ref(x, adj, L2_gnn_intervention_value, L2_gnn_W1, L2_gnn_b1, L2_gnn_W2, L2_gnn_b2, 0), axis=-1)
    x = _layernorm(x + _L3_gnn_ref(x, adj, L3_gnn_W, L3_gnn_a), axis=-1)
    return x

_drawn_inputs = setup_inputs


def setup_inputs(seed=0):
    import zlib

    import numpy as np

    out = dict(_drawn_inputs(seed))
    spreads = {'L0_gnn_fcb': (0.0, 2.0)}
    factors = {'L0_gnn_H': 12.73,
     'L0_gnn_a_ge': 8.0,
     'L1_gnn_b_out': 7.207,
     'L2_gnn_intervention_value': 3.984,
     'L2_gnn_b1': 8.0,
     'L2_gnn_b2': 8.0,
     'L3_gnn_a': 8.0}
    for name, (base, spread) in spreads.items():
        noise = np.random.default_rng([zlib.crc32(name.encode()), seed]).standard_normal(out[name].shape)
        drawn = base * np.exp(spread * noise) if base else spread * noise
        out[name] = jnp.asarray(drawn.astype(out[name].dtype))
    for name, factor in factors.items():
        out[name] = (out[name] * factor).astype(out[name].dtype)
    return out
```

```python
from contextlib import ExitStack

import numpy as np

import concourse.bass as bass
from concourse import mybir

F32 = mybir.dt.float32
F16 = mybir.dt.float16
BF16 = mybir.dt.bfloat16
I32 = mybir.dt.int32
ACT = mybir.ActivationFunctionType
ALU = mybir.AluOpType
AX = mybir.AxisListType

P = 128
B, N, D = 8, 1024, 64
NT = N // P
HEADS, HID = 8, 128
E = 64
HALF = 512
NEG = -1.0e30
LOWEST = -3.0e38
SPLIT = 4096.0
LN_PEAK = 10.397207708
EPS = 1e-5
FREE = 1


class Mem:

    def __init__(self, nc, ctx, tag=""):
        self.nc, self.ctx, self.tag, self.sems = nc, ctx, tag, []

    def sb(self, name, shape, dt=F32):
        return self.ctx.enter_context(self.nc.sbuf_tensor(self.tag + name, shape, dt))

    def ps(self, name, shape, dt=F32):
        return self.ctx.enter_context(self.nc.psum_tensor(self.tag + name, shape, dt))

    def sem(self, name):
        if not self.sems:
            self.ctx.callback(self.clear)
        self.sems.append(self.nc.alloc_semaphore(self.tag + name))
        return self.sems[-1]

    def clear(self):
        self.nc.clear_and_free_semaphores(self.sems)
        self.nc.all_engine_barrier()


def cols(i, width=P):
    return slice(i * width, (i + 1) * width)


def apart(eng, c):
    eng.sem_inc(c["passed"], 1)


def make_constants(nc, c):
    with ExitStack() as ctx:
        m = Mem(nc, ctx)
        zeroed = m.sem("ident_zeroed")
        built = c["built"]
        with nc.Block() as block:

            @block.gpsimd
            def _(pool):
                pool.memset(c["ident"][:, :], 0.0).then_inc(zeroed, 1)
                pool.wait_ge(zeroed, 1)
                pool.affine_select(out=c["ident"][:, :], in_=c["ident"][:, :], compare_op=ALU.not_equal, fill=1.0,
                                   base=0, pattern=[[-1, P]], channel_multiplier=1).then_inc(built, 1)
                pool.wait_ge(built, 1)
                pool.tensor_copy(c["ident16"][:, :], c["ident"][:, :]).then_inc(built, 1)
                pool.wait_ge(built, 2)


def load(nc, pairs, tag):
    with ExitStack() as ctx:
        loaded = Mem(nc, ctx).sem("loaded_" + tag)
        with nc.Block() as block:

            @block.sync
            def _(sp):
                for dst, src in pairs:
                    sp.dma_start(dst, src).then_inc(loaded, 16)
                sp.wait_ge(loaded, 16 * len(pairs))


def layer_norm(nc, X, tag):
    with ExitStack() as ctx:
        m = Mem(nc, ctx)
        G = NT * B
        sq = m.sb("sq" + tag, [P, G, D])
        mean = m.sb("mean" + tag, [P, G])
        var = m.sb("var" + tag, [P, G])
        step = m.sem("ln_step" + tag)
        centred = m.sem("ln_centred" + tag)
        squared = m.sem("ln_squared" + tag)
        var_ready = m.sem("ln_var" + tag)
        std_ready = m.sem("ln_std" + tag)
        x = X[:, :, :, :].rearrange("p t b f -> p (t b) f")
        with nc.Block() as block:

            @block.vector
            def _(dve):
                dve.tensor_reduce(out=mean[:, :], in_=x, axis=AX.X, op=ALU.add).then_inc(step, 1)
                dve.wait_ge(step, 1)
                dve.tensor_scalar(out=mean[:, :], in0=mean[:, :], scalar1=1.0 / D, scalar2=None,
                                  op0=ALU.mult).then_inc(step, 1)
                dve.wait_ge(step, 2)
                dve.tensor_tensor(out=x, in0=x, in1=mean[:, :].unsqueeze(2).broadcast_to([P, G, D]),
                                  op=ALU.subtract).then_inc(centred, 1)
                dve.wait_ge(squared, 1)
                dve.tensor_reduce(out=var[:, :], in_=sq[:, :, :], axis=AX.X, op=ALU.add).then_inc(step, 1)
                dve.wait_ge(step, 3)
                dve.tensor_scalar(out=var[:, :], in0=var[:, :], scalar1=1.0 / D, scalar2=EPS,
                                  op0=ALU.mult, op1=ALU.add).then_inc(var_ready, 1)
                dve.wait_ge(std_ready, 1)
                dve.reciprocal(var[:, :], mean[:, :]).then_inc(step, 1)
                dve.wait_ge(step, 4)
                dve.tensor_tensor(out=x, in0=x, in1=var[:, :].unsqueeze(2).broadcast_to([P, G, D]),
                                  op=ALU.mult).then_inc(step, 1)
                dve.wait_ge(step, 5)

            @block.scalar
            def _(act):
                act.wait_ge(centred, 1)
                act.activation(sq[:, :, :], x, ACT.Square).then_inc(squared, 1)
                act.wait_ge(var_ready, 1)
                act.activation(mean[:, :], var[:, :], ACT.Sqrt).then_inc(std_ready, 1)



def l0_prepare(nc, w, X, st):
    with ExitStack() as ctx:
        m = Mem(nc, ctx)
        xb = m.sb("xT_batch", [D, N])
        W2 = m.sb("W2", [D, 2 * D])
        WT2 = m.sb("WT2", [D, 2 * D])
        wvec = m.sb("wvec", [D, 3])
        ones = m.sb("ones0", [P, P])
        avec = m.sb("avec", [D, 2, P])
        Lnode = m.sb("Lnode", [D, P])
        Lgate = m.sb("Lgate", [D, P])
        hT_neg = m.sb("hT_neg", [P, N])
        h_neg = m.sb("h_neg", [P, NT, E])
        avb = m.sb("avb", [P, P])
        lg = m.sb("lg", [P, N])
        al = m.sb("al", [P, N])
        alT = m.sb("alT", [P, NT, E])
        hN = m.sb("hN", [P, NT, 2 * D])
        small = m.sb("small0", [P, 8])
        agT = m.sb("agT", [P, 2, E])
        ex = m.sb("ex", [P, E])
        he = m.sb("he", [P, E])
        Tse = m.sb("Tse", [P, E])
        b32 = m.sb("b32", [P, N])
        lgc = m.sb("lgc", [P, NT, E])
        cst = m.sb("cst", [P, 2, NT])
        cdup = m.sb("cdup", [P, NT, 2, E])
        psN = m.ps("psN", [P, N])
        psG = m.ps("psG", [P, N])
        psH = m.ps("psH", [P, N])
        psC = m.ps("psC", [P, NT, 2 * D])
        loaded = m.sem("l0_loaded")
        xb_loaded = m.sem("l0_xb_loaded")
        pro = {k: m.sem("l0_" + k) for k in ("avec", "L_ps", "masks", "avb")}
        S = {k: m.sem("l0_" + k) for k in (
            "projected", "slope", "lrelu", "h_copied", "masked", "nmax", "alpha_exp", "alpha_inv", "alpha", "alphaT_ps",
            "alphaT", "agg_ps", "agg", "agg_exp", "agg_relu", "he", "edge_ps", "q", "Tse", "beta_t", "beta32",
            "beta_hi", "beta", "se_ps", "c_lg", "c_max", "c_sub", "c_exp", "c_sum", "c_inv", "c_inv2", "c_ready",
            "cT_ps", "cT_hi", "batch")}
        with nc.Block() as block:

            @block.sync
            def _(sp):
                n = 0
                for dst, src in ((W2[:, 0:D], w["W0"]), (W2[:, D:2 * D], w["W0"]),
                                 (WT2[:, 0:D], w["W0T"]), (WT2[:, D:2 * D], w["W0T"]),
                                 (wvec[:, 0:1], w["a_node"]), (wvec[:, 1:2], w["a_gn"]), (wvec[:, 2:3], w["a_ge"]),
                                 (hT_neg[0:E, :], w["HT"]), (hT_neg[E:P, :], w["HT"]),
                                 (h_neg[:, :, :], w["H"]), (st["fcW"][:, :], w["fcW"]), (st["fcb"][:, :], w["fcb"]),
                                 (st["av"][:, 0:1], w["av"])):
                    sp.dma_start(dst, src).then_inc(loaded, 16)
                    n += 1
                assert n == 13
                with sp.Fori(0, B) as b:
                    sp.wait_ge(S["projected"], b + FREE)
                    sp.dma_start(xb[:, :], w["xT"][:, bass.ds(b, 1), :].squeeze(1)).then_inc(xb_loaded, 16)

            @block.vector
            def _(dve):
                dve.sem_inc(S["batch"], FREE)
                dve.memset(ones[:, :], 1.0).then_inc(pro["avb"], 1)
                dve.wait_ge(loaded, 16 * 13)
                dve.wait_ge(pro["avb"], 1)
                dve.tensor_scalar(out=avec[:, 0, :], in0=ones[0:D, :], scalar1=wvec[:, 0:1], scalar2=None,
                                  op0=ALU.mult).then_inc(pro["avec"], 1)
                dve.tensor_scalar(out=avec[:, 1, :], in0=ones[0:D, :], scalar1=wvec[:, 1:2], scalar2=None,
                                  op0=ALU.mult).then_inc(pro["avec"], 1)
                dve.tensor_scalar(out=avb[:, :], in0=ones[:, :], scalar1=st["av"][:, 0:1], scalar2=None,
                                  op0=ALU.mult).then_inc(pro["avb"], 1)
                dve.tensor_scalar(out=st["av"][:, 1:2], in0=st["av"][:, 0:1], scalar1=-1.0, scalar2=None,
                                  op0=ALU.mult).then_inc(pro["avb"], 1)
                dve.tensor_scalar(out=hT_neg[:, :], in0=hT_neg[:, :], scalar1=0.0, scalar2=NEG,
                                  op0=ALU.is_le, op1=ALU.mult).then_inc(pro["masks"], 1)
                dve.tensor_scalar(out=h_neg[:, :, :], in0=h_neg[:, :, :], scalar1=0.0, scalar2=NEG,
                                  op0=ALU.is_le, op1=ALU.mult).then_inc(pro["masks"], 1)
                dve.wait_ge(pro["L_ps"], 1)
                dve.tensor_copy(Lnode[:, :], psN[0:D, 0:P]).then_inc(pro["masks"], 1)
                dve.tensor_copy(Lgate[:, :], psN[0:D, P:2 * P]).then_inc(pro["masks"], 1)
                dve.wait_ge(pro["masks"], 4)
                with dve.Fori(0, B) as b:
                    dve.wait_ge(S["slope"], b + 1)
                    dve.tensor_tensor(out=lg[:, :], in0=psN[:, :], in1=lg[:, :], op=ALU.max).then_inc(S["lrelu"], 1)
                    dve.wait_ge(S["lrelu"], b + 1)
                    apart(dve, st)
                    dve.tensor_tensor_reduce(out=al[:, :], in0=lg[:, :], in1=hT_neg[:, :], scale=1.0, scalar=LOWEST,
                                             op0=ALU.add, op1=ALU.max, accum_out=small[:, 0:1])\
                        .then_inc(S["masked"], 1)
                    dve.wait_ge(S["masked"], b + 1)
                    dve.tensor_scalar(out=small[:, 1:2], in0=small[:, 0:1], scalar1=-1.0, scalar2=None,
                                      op0=ALU.mult).then_inc(S["nmax"], 1)
                    dve.wait_ge(S["alpha_exp"], b + 1)
                    dve.reciprocal(small[:, 3:4], small[:, 2:3]).then_inc(S["alpha_inv"], 1)
                    dve.wait_ge(S["alpha_inv"], b + 1)
                    dve.tensor_scalar(out=al[:, :], in0=al[:, :], scalar1=small[:, 3:4], scalar2=None,
                                      op0=ALU.mult).then_inc(S["alpha"], 1)
                    dve.wait_ge(S["agg_ps"], b + 1)
                    dve.tensor_copy(agT[:, 0, :], psN[:, HALF:HALF + E]).then_inc(S["agg"], 1)
                    dve.tensor_copy(agT[:, 1, :], psN[:, HALF:HALF + E]).then_inc(S["agg"], 1)
                    pairs = psN[:, HALF:HALF + E].rearrange("p (j i) -> p j i", i=2)
                    dve.tensor_copy(st["aggP"][0:D, bass.ds(b, 1), :], pairs[0:D, :, 0].unsqueeze(1)).then_inc(S["agg"], 1)
                    dve.tensor_copy(st["aggP"][D:P, bass.ds(b, 1), :], pairs[D:P, :, 1].unsqueeze(1)).then_inc(S["agg"], 1)
                    dve.wait_ge(S["agg"], 4 * b + 4)
                    dve.tensor_scalar(out=he[:, :], in0=agT[:, 0, :], scalar1=0.0, scalar2=None,
                                      op0=ALU.max).then_inc(S["agg_relu"], 1)
                    dve.wait_ge(S["agg_relu"], b + 1)
                    dve.wait_ge(S["agg_exp"], b + 1)
                    dve.scalar_tensor_tensor(out=he[:, :], in0=ex[:, :], scalar=-1.0, in1=he[:, :],
                                             op0=ALU.add, op1=ALU.min).then_inc(S["he"], 1)
                    dve.wait_ge(S["beta_t"], b + 1)
                    dve.tensor_scalar(out=b32[:, :], in0=b32[:, :], scalar1=SPLIT / 2, scalar2=SPLIT / 2,
                                      op0=ALU.mult, op1=ALU.add).then_inc(S["beta32"], 1)
                    dve.wait_ge(S["beta32"], b + 1)
                    bs = st["BS"][:, bass.ds(b, 1), :].squeeze(1)
                    dve.tensor_copy(bs, b32[:, :]).then_inc(S["beta_hi"], 1)
                    dve.wait_ge(S["beta_hi"], b + 1)
                    bs_lo = st["BS"][E:P, bass.ds(b, 1), :].squeeze(1)
                    dve.tensor_tensor(out=bs_lo, in0=b32[E:P, :], in1=bs_lo, op=ALU.subtract).then_inc(S["beta"], 1)
                    dve.wait_ge(S["se_ps"], b + 1)
                    dve.tensor_tensor(out=lgc[:, :, :], in0=h_neg[:, :, :],
                                      in1=psN[:, 0:E].unsqueeze(1).broadcast_to([P, NT, E]),
                                      op=ALU.add).then_inc(S["c_lg"], 1)
                    dve.wait_ge(S["c_lg"], b + 1)
                    dve.tensor_reduce(out=cst[:, 0, :], in_=lgc[:, :, :], axis=AX.X, op=ALU.max)\
                        .then_inc(S["c_max"], 1)
                    dve.wait_ge(S["c_max"], b + 1)
                    dve.tensor_tensor(out=lgc[:, :, :], in0=lgc[:, :, :],
                                      in1=cst[:, 0, :].unsqueeze(2).broadcast_to([P, NT, E]),
                                      op=ALU.subtract).then_inc(S["c_sub"], 1)
                    dve.wait_ge(S["c_exp"], b + 1)
                    dve.tensor_reduce(out=cst[:, 0, :], in_=lgc[:, :, :], axis=AX.X, op=ALU.add)\
                        .then_inc(S["c_sum"], 1)
                    dve.wait_ge(S["c_sum"], b + 1)
                    dve.reciprocal(cst[:, 1, :], cst[:, 0, :]).then_inc(S["c_inv"], 1)
                    dve.wait_ge(S["c_inv"], b + 1)
                    dve.tensor_scalar(out=cst[:, 1, :], in0=cst[:, 1, :], scalar1=SPLIT, scalar2=None,
                                      op0=ALU.mult).then_inc(S["c_inv2"], 1)
                    dve.wait_ge(S["c_inv2"], b + 1)
                    for k in range(2):
                        dve.tensor_tensor(out=cdup[:, :, k, :], in0=lgc[:, :, :],
                                          in1=cst[:, 1, :].unsqueeze(2).broadcast_to([P, NT, E]),
                                          op=ALU.mult).then_inc(S["c_ready"], 1)
                    dve.wait_ge(S["cT_hi"], b + 1)
                    cs_lo = st["CS"][E:P, bass.ds(b, 1), :].squeeze(1)
                    dve.tensor_tensor(out=cs_lo, in0=psN[E:P, :], in1=cs_lo, op=ALU.subtract).then_inc(S["batch"], 1)

            @block.scalar
            def _(act):
                with act.Fori(0, B) as b:
                    act.wait_ge(S["projected"], b + 1 + FREE)
                    act.activation(lg[:, :], psN[:, :], ACT.Copy, scale=0.2).then_inc(S["slope"], 1)
                    act.activation(st["hT"][:, bass.ds(b, 1), :].squeeze(1), psH[:, :], ACT.Copy).then_inc(S["h_copied"], 1)
                    act.activation(hN[:, :, :], psC[:, :, :], ACT.Copy).then_inc(S["h_copied"], 1)
                    act.wait_ge(S["nmax"], b + 1)
                    act.activation(al[:, :], al[:, :], ACT.Exp, bias=small[:, 1:2], accum_out=small[:, 2:3])\
                        .then_inc(S["alpha_exp"], 1)
                    act.wait_ge(S["alphaT_ps"], b + 1)
                    act.activation(alT[:, :, :], psN[:, 0:HALF].rearrange("p (t e) -> p t e", e=E), ACT.Copy)\
                        .then_inc(S["alphaT"], 1)
                    act.wait_ge(S["agg"], 4 * b + 4)
                    act.activation(ex[:, :], agT[:, 0, :], ACT.Exp).then_inc(S["agg_exp"], 1)
                    act.wait_ge(S["edge_ps"], b + 1)
                    act.activation(small[:, 4:5], psN[:, 0:1], ACT.Copy, scale=0.5).then_inc(S["q"], 1)
                    act.activation(Tse[:, :], psN[:, E:2 * E], ACT.Tanh, bias=st["fcb"][:, 0:1])\
                        .then_inc(S["Tse"], 1)
                    act.wait_ge(S["q"], b + 1)
                    act.activation(b32[:, :], psG[:, :], ACT.Tanh, bias=small[:, 4:5], scale=0.5)\
                        .then_inc(S["beta_t"], 1)
                    act.wait_ge(S["c_sub"], b + 1)
                    act.activation(lgc[:, :, :], lgc[:, :, :], ACT.Exp).then_inc(S["c_exp"], 1)
                    act.wait_ge(S["cT_ps"], b + 1)
                    act.activation(st["CS"][:, bass.ds(b, 1), :].squeeze(1), psN[:, :], ACT.Copy).then_inc(S["cT_hi"], 1)

            @block.tensor
            def _(pe):
                pe.sem_inc(S["projected"], FREE)
                ident = st["ident"]
                pe.wait_ge(pro["avec"], 2)
                for k in range(2):
                    last = pe.matmul(psN[0:D, cols(k)], WT2[:, 0:D], avec[:, k, :], start=True, stop=True)
                last.then_inc(pro["L_ps"], 1)
                pe.wait_ge(pro["masks"], 4)
                pe.wait_ge(pro["avb"], 3)
                with pe.Fori(0, B) as b:
                    pe.wait_ge(S["batch"], b + FREE)
                    pe.wait_ge(xb_loaded, 16 * b + 16)
                    for hf in range(2):
                        pe.matmul(psN[:, cols(hf, HALF)], Lnode[:, :], xb[:, cols(hf, HALF)], start=True, stop=True)
                        pe.matmul(psG[:, cols(hf, HALF)], Lgate[:, :], xb[:, cols(hf, HALF)], start=True, stop=True)
                        pe.matmul(psH[:, cols(hf, HALF)], W2[:, :], xb[:, cols(hf, HALF)], start=True, stop=True)
                    for t in range(NT):
                        last = pe.matmul(psC[:, t, :], xb[:, cols(t)], W2[:, :], start=True, stop=True)
                    last.then_inc(S["projected"], 1)
                    pe.wait_ge(S["alpha"], b + 1)
                    apart(pe, st)
                    for t in range(NT):
                        last = pe.transpose(psN[:, cols(t, E)], al[0:E, cols(t)], ident[0:E, 0:E])
                    last.then_inc(S["alphaT_ps"], 1)
                    pe.wait_ge(S["alphaT"], b + 1)
                    pe.wait_ge(S["h_copied"], 2 * b + 2)
                    for t in range(NT):
                        last = pe.matmul(psN[:, HALF:HALF + E], hN[:, t, :], alT[:, t, :],
                                         start=(t == 0), stop=(t == NT - 1))
                    last.then_inc(S["agg_ps"], 1)
                    pe.wait_ge(S["he"], b + 1)
                    pe.matmul(psN[:, 0:1], agT[0:D, :, :], wvec[:, 2:3], start=True, stop=True)
                    pe.matmul(psN[:, E:2 * E], st["fcW"][:, :], he[0:D, :], start=True, stop=True)\
                        .then_inc(S["edge_ps"], 1)
                    pe.wait_ge(S["Tse"], b + 1)
                    pe.matmul(psN[:, 0:E], avb[:, :], Tse[:, :], start=True, stop=True).then_inc(S["se_ps"], 1)
                    pe.wait_ge(S["c_ready"], 2 * b + 2)
                    for t in range(NT):
                        last = pe.transpose(psN[:, cols(t)], cdup[:, t, :, :].rearrange("p k e -> p (k e)"), ident[:, :])
                    last.then_inc(S["cT_ps"], 1)


def l0_industry(nc, w, st, adjT, IND):
    with ExitStack() as ctx:
        m = Mem(nc, ctx)
        xT = m.sb("xTi", [D, B, N])
        Wi = m.sb("Wi", [D, D])
        Y = m.sb("Yi", [P, NT, B, D])
        adj = m.sb("adjn", [P, 2, N])
        deg = m.sb("deg", [P, NT])
        rdeg = m.sb("rdeg", [P, NT])
        psY = [m.ps(f"psY{i}", [P, NT, D]) for i in range(2)]
        psI = [m.ps(f"psI{i}", [P, B, D]) for i in range(2)]
        loaded, adj_loaded = m.sem("ind_loaded"), [m.sem("adjrow_loaded0"), m.sem("adjrow_loaded1")]
        adjT_loaded = m.sem("adjT_loaded")
        y_ps, y_ready, ind_ps, ind_ready = (m.sem("ind_" + k) for k in ("y_ps", "y", "ps", "ready"))
        deg_part, deg_ready = m.sem("deg_part"), m.sem("deg_ready")
        with nc.Block() as block:

            @block.sync
            def _(sp):
                sp.dma_start(xT[:, :, :], w["xT"]).then_inc(loaded, 16)
                sp.dma_start(Wi[:, :], w["Wind"]).then_inc(loaded, 16)
                sp.dma_start(adjT[:, :, :], w["adjT"]).then_inc(adjT_loaded, 16)
                for t in range(NT):
                    if t >= 2:
                        sp.wait_ge(deg_part, 2 * t - 2)
                    sp.dma_start(adj[:, t % 2, :], w["adj"][:, t, :]).then_inc(adj_loaded[t % 2], 16)

            @block.vector
            def _(dve):
                for t in range(NT):
                    dve.wait_ge(adj_loaded[t % 2], 16 * (t // 2 + 1))
                    dve.tensor_scalar(out=st["neg"][:, t, :], in0=adj[:, t % 2, :], scalar1=0.0, scalar2=NEG,
                                      op0=ALU.is_equal, op1=ALU.mult).then_inc(deg_part, 1)
                    dve.tensor_reduce(out=deg[:, t:t + 1], in_=adj[:, t % 2, :], axis=AX.X, op=ALU.add)\
                        .then_inc(deg_part, 1)
                dve.wait_ge(deg_part, 2 * NT)
                dve.tensor_scalar(out=deg[:, :], in0=deg[:, :], scalar1=1.0, scalar2=None, op0=ALU.max)\
                    .then_inc(deg_part, 1)
                dve.wait_ge(deg_part, 2 * NT + 1)
                dve.reciprocal(rdeg[:, :], deg[:, :]).then_inc(deg_ready, 1)

            @block.tensor
            def _(pe):
                pe.wait_ge(loaded, 32)
                for b in range(B):
                    if b >= 2:
                        pe.wait_ge(y_ready, b - 1)
                    for t in range(NT):
                        last = pe.matmul(psY[b % 2][:, t, :], xT[:, b, cols(t)], Wi[:, :], start=True, stop=True)
                    last.then_inc(y_ps, 1)
                pe.wait_ge(adjT_loaded, 16)
                pe.wait_ge(y_ready, B)
                for t in range(NT):
                    if t >= 2:
                        pe.wait_ge(ind_ready, t - 1)
                    for j in range(NT):
                        last = pe.matmul(psI[t % 2][:, :, :], adjT[:, j, cols(t)], Y[:, j, :, :],
                                         start=(j == 0), stop=(j == NT - 1))
                    last.then_inc(ind_ps, 1)

            @block.scalar
            def _(act):
                for b in range(B):
                    act.wait_ge(y_ps, b + 1)
                    act.activation(Y[:, :, b, :], psY[b % 2][:, :, :], ACT.Copy).then_inc(y_ready, 1)
                act.wait_ge(deg_ready, 1)
                for t in range(NT):
                    act.wait_ge(ind_ps, t + 1)
                    act.activation(IND[:, t, :, :], psI[t % 2][:, :, :], ACT.Copy, scale=rdeg[:, t:t + 1])\
                        .then_inc(ind_ready, 1)


def l0_edges(nc, st, gT):
    J = E // 2
    with ExitStack() as ctx:
        m = Mem(nc, ctx)
        SEL = m.sb("SEL", [P, E, D], F16)
        SUM = m.sb("SUM", [P, D])
        v = m.sb("v", [P, 2, N])
        ex = m.sb("exv", [P, 2, N])
        r = m.sb("rv", [P, 2, N])
        y = m.sb("yv", [P, 2, N])
        psB = [m.ps(f"psB{i}", [P, N]) for i in range(2)]
        psC = m.ps("psCe", [P, N])
        psA = m.ps("psA", [D, N])
        sel = m.sem("sel_step")
        S = {k: m.sem("edge_" + k) for k in ("beta", "coef", "v", "exp", "relu", "elu", "y", "summed", "g")}
        with nc.Block() as block:

            @block.gpsimd
            def _(pool):
                pool.memset(SEL[:, :, :], 0.0).then_inc(sel, 1)
                pool.memset(SUM[:, :], 0.0).then_inc(sel, 1)
                pool.wait_ge(sel, 2)
                for k in range(2):
                    pool.affine_select(out=SEL[:, :, :], in_=SEL[:, :, :], compare_op=ALU.not_equal, fill=1.0 / SPLIT,
                                       base=-E * k, pattern=[[-1, E], [0, D]], channel_multiplier=1).then_inc(sel, 1)
                    pool.affine_select(out=SUM[:, :], in_=SUM[:, :], compare_op=ALU.not_equal, fill=1.0,
                                       base=-D * k, pattern=[[-1, D]], channel_multiplier=1).then_inc(sel, 1)
                    pool.wait_ge(sel, 4 + 2 * k)

            @block.tensor
            def _(pe):
                pe.wait_ge(sel, 6)

                def gates(b, j, i):
                    for hf in range(2):
                        last = pe.matmul(psB[i][:, cols(hf, HALF)], SEL[:, bass.ds(2 * j, 2), :],
                                         st["BS"][:, b, cols(hf, HALF)], start=True, stop=True)
                    last.then_inc(S["beta"], 1)

                def coefs(b, j):
                    for hf in range(2):
                        last = pe.matmul(psC[:, cols(hf, HALF)], SEL[:, bass.ds(2 * j, 2), :],
                                         st["CS"][:, b, cols(hf, HALF)], start=True, stop=True)
                    last.then_inc(S["coef"], 1)

                def add_up(i, first=False, final=False):
                    for hf in range(2):
                        last = pe.matmul(psA[:, cols(hf, HALF)], SUM[:, :], y[:, i, cols(hf, HALF)],
                                         start=first, stop=final)
                    last.then_inc(S["summed"], 1)

                with pe.Fori(0, B) as b:
                    pe.wait_ge(S["v"], b * J + FREE)
                    gates(b, 0, 0)
                    gates(b, 1, 1)
                    pe.wait_ge(S["y"], b * J + FREE)
                    coefs(b, 0)
                    pe.wait_ge(S["v"], b * J + 1 + FREE)
                    gates(b, 2, 0)
                    pe.wait_ge(S["y"], b * J + 1 + FREE)
                    coefs(b, 1)
                    pe.wait_ge(S["g"], b + FREE)
                    add_up(0, first=True)
                    with pe.Fori(0, J // 2 - 2) as jj:
                        j = 2 * jj + 1
                        for i in range(2):
                            pe.wait_ge(S["v"], b * J + j + i + 1 + FREE)
                            gates(b, j + i + 2, 1 - i)
                            pe.wait_ge(S["y"], b * J + j + i + 1 + FREE)
                            coefs(b, j + i + 1)
                            add_up(1 - i)
                    pe.wait_ge(S["v"], b * J + J - 2 + FREE)
                    gates(b, J - 1, 1)
                    for j in (J - 3, J - 2):
                        pe.wait_ge(S["y"], b * J + j + 1 + FREE)
                        coefs(b, j + 1)
                        add_up(j % 2)
                    pe.wait_ge(S["y"], b * J + J + FREE)
                    add_up(1, final=True)

            @block.vector
            def _(dve):
                dve.sem_inc(S["v"], FREE)
                dve.sem_inc(S["y"], FREE)
                dve.sem_inc(S["g"], FREE)
                def gate(b, j, i):
                    s = b * J + j
                    dve.wait_ge(S["beta"], s + 1)
                    dve.scalar_tensor_tensor(out=v[:, i, :], in0=st["hT"][:, b, :],
                                             scalar=st["aggP"][:, b, bass.ds(j, 1)], in1=psB[i][:, :],
                                             op0=ALU.subtract, op1=ALU.mult).then_inc(S["v"], 1)

                def weigh(b, j, i):
                    s = b * J + j
                    dve.wait_ge(S["relu"], s + 1)
                    dve.scalar_tensor_tensor(out=ex[:, i, :], in0=ex[:, i, :], scalar=-1.0, in1=r[:, i, :],
                                             op0=ALU.add, op1=ALU.min).then_inc(S["elu"], 1)
                    dve.wait_ge(S["elu"], s + 1)
                    dve.wait_ge(S["coef"], s + 1)
                    dve.tensor_tensor(out=y[:, i, :], in0=ex[:, i, :], in1=psC[:, :], op=ALU.mult)\
                        .then_inc(S["y"], 1)

                with dve.Fori(0, B) as b:
                    gate(b, 0, 0)
                    with dve.Fori(0, J // 2 - 1) as jj:
                        j = 2 * jj
                        for i in range(2):
                            gate(b, j + i + 1, 1 - i)
                            weigh(b, j + i, i)
                    gate(b, J - 1, 1)
                    weigh(b, J - 2, 0)
                    weigh(b, J - 1, 1)
                    dve.wait_ge(S["summed"], b * J + J)
                    dve.tensor_copy(gT[:, bass.ds(b, 1), :].squeeze(1), psA[:, :]).then_inc(S["g"], 1)

            @block.scalar
            def _(act):
                with act.Fori(0, B) as b:
                    with act.Fori(0, J // 2) as jj:
                        j = 2 * jj
                        for i in range(2):
                            s = b * J + j + i
                            act.wait_ge(S["v"], s + 1 + FREE)
                            agg = st["aggP"][:, b, bass.ds(j + i, 1)]
                            act.activation(ex[:, i, :], v[:, i, :], ACT.Exp, bias=agg).then_inc(S["exp"], 1)
                            act.activation(r[:, i, :], v[:, i, :], ACT.Relu, bias=agg).then_inc(S["relu"], 1)


def l0_combine(nc, st, X, IND, gT):
    with ExitStack() as ctx:
        m = Mem(nc, ctx)
        indb = m.sb("indb", [P, NT, D])
        gb = m.sb("gb", [D, N])
        indT = m.sb("indT", [D, N])
        T1 = m.sb("T1", [P, N])
        T2 = m.sb("T2", [P, N])
        gN = m.sb("gN", [P, NT, D])
        d = m.sb("dmix", [P, NT, D])
        wt = m.sb("wt", [P, NT])
        psT = m.ps("psT0", [D, N])
        psGn = m.ps("psGn", [P, NT, D])
        psF = [m.ps(f"psF{i}", [P, N]) for i in range(2)]
        psD = m.ps("psD", [P, NT])
        S = {k: m.sem("comb_" + k) for k in ("staged", "tr", "indT", "fc", "tanh", "diff", "w", "w1", "gN", "d", "d2", "d3", "x")}
        with nc.Block() as block:

            @block.gpsimd
            def _(pool):
                with pool.Fori(0, B) as b:
                    pool.wait_ge(S["x"], b + FREE)
                    pool.tensor_copy(indb[:, :, :], IND[:, :, b, :]).then_inc(S["staged"], 1)
                    pool.tensor_copy(gb[:, :], gT[:, b, :]).then_inc(S["staged"], 1)

            @block.tensor
            def _(pe):
                with pe.Fori(0, B) as b:
                    pe.wait_ge(S["staged"], 2 * b + 2)
                    apart(pe, st)
                    for t in range(NT):
                        pe.transpose(psT[:, cols(t)], indb[:, t, :], st["ident"][:, :])
                        last = pe.transpose(psGn[:, t, :], gb[:, cols(t)], st["ident"][0:D, 0:D])
                    last.then_inc(S["tr"], 1)
                    for hf in range(2):
                        pe.matmul(psF[1][:, cols(hf, HALF)], st["fcW"][:, :], gb[:, cols(hf, HALF)],
                                  start=True, stop=True)
                    pe.wait_ge(S["indT"], b + 1)
                    for hf in range(2):
                        last = pe.matmul(psF[0][:, cols(hf, HALF)], st["fcW"][:, :], indT[:, cols(hf, HALF)],
                                         start=True, stop=True)
                    last.then_inc(S["fc"], 1)
                    pe.wait_ge(S["tanh"], 2 * b + 2)
                    for t in range(NT):
                        pe.matmul(psD[:, t:t + 1], T1[:, cols(t)], st["av"][:, 0:1], start=True, stop=False)
                        last = pe.matmul(psD[:, t:t + 1], T2[:, cols(t)], st["av"][:, 1:2], start=False, stop=True)
                    last.then_inc(S["diff"], 1)

            @block.scalar
            def _(act):
                with act.Fori(0, B) as b:
                    act.wait_ge(S["tr"], b + 1)
                    act.activation(indT[:, :], psT[:, :], ACT.Copy).then_inc(S["indT"], 1)
                    act.wait_ge(S["fc"], b + 1)
                    act.activation(T1[:, :], psF[0][:, :], ACT.Tanh, bias=st["fcb"][:, 0:1]).then_inc(S["tanh"], 1)
                    act.activation(T2[:, :], psF[1][:, :], ACT.Tanh, bias=st["fcb"][:, 0:1]).then_inc(S["tanh"], 1)
                    act.wait_ge(S["diff"], b + 1)
                    act.activation(wt[:, :], psD[:, :], ACT.Tanh, scale=0.5).then_inc(S["w"], 1)

            @block.vector
            def _(dve):
                dve.sem_inc(S["x"], FREE)
                with dve.Fori(0, B) as b:
                    dve.wait_ge(S["tr"], b + 1)
                    dve.tensor_copy(gN[:, :, :], psGn[:, :, :]).then_inc(S["gN"], 1)
                    dve.wait_ge(S["gN"], b + 1)
                    dve.tensor_tensor(out=d[:, :, :], in0=indb[:, :, :], in1=gN[:, :, :], op=ALU.subtract)\
                        .then_inc(S["d"], 1)
                    dve.wait_ge(S["w"], b + 1)
                    dve.tensor_scalar(out=wt[:, :], in0=wt[:, :], scalar1=0.5, scalar2=0.5, op0=ALU.mult, op1=ALU.add)\
                        .then_inc(S["w1"], 1)
                    dve.wait_ge(S["w1"], b + 1)
                    dve.tensor_tensor(out=d[:, :, :], in0=d[:, :, :], in1=wt[:, :].unsqueeze(2).broadcast_to([P, NT, D]),
                                      op=ALU.mult).then_inc(S["d2"], 1)
                    dve.wait_ge(S["d2"], b + 1)
                    dve.tensor_tensor(out=d[:, :, :], in0=d[:, :, :], in1=gN[:, :, :], op=ALU.add).then_inc(S["d3"], 1)
                    dve.wait_ge(S["d3"], b + 1)
                    dve.tensor_tensor(out=X[:, :, b, :], in0=X[:, :, b, :], in1=d[:, :, :], op=ALU.add)\
                        .then_inc(S["x"], 1)


def layer0(nc, w, c, X):
    with ExitStack() as ctx:
        m = Mem(nc, ctx)
        IND = m.sb("IND", [P, NT, B, D])
        st = dict(c)
        with ExitStack() as inner:
            mi = Mem(nc, inner)
            adjT = mi.sb("adjT0", [P, NT, N])
            l0_industry(nc, w, st, adjT, IND)
        st["fcW"] = m.sb("fcW", [D, P])
        st["fcb"] = m.sb("fcb", [P, 1])
        st["av"] = m.sb("av", [P, 2])
        gT = m.sb("gT", [D, B, N])
        st["hT"] = m.sb("hT", [P, B, N])
        st["BS"] = m.sb("BS", [P, B, N], F16)
        st["CS"] = m.sb("CS", [P, B, N], F16)
        st["aggP"] = m.sb("aggP", [P, B, E // 2])
        l0_prepare(nc, w, X, st)
        l0_edges(nc, st, gT)
        l0_combine(nc, st, X, IND, gT)



TAB = HID + 3 + D
BIAS, SCALE_P, SCALE_N, WOUT = HID, HID + 1, HID + 2, HID + 3


def l1_prepare(nc, w, c, X, st):
    with ExitStack() as ctx:
        m = Mem(nc, ctx)
        WhT = m.sb("WhT", [P, HEADS, 2, D])
        Ms = m.sb("Ms", [P, HEADS, D])
        bh = m.sb("bh", [P, HEADS])
        top = m.sb("top", [P, 4, HEADS])
        psM = m.ps("psM", [P, HEADS, D])
        psX = [m.ps(f"psX{i}", [P, N], F16) for i in range(2)]
        loaded = m.sem("l1_loaded")
        S = {k: m.sem("l1p_" + k) for k in ("x_hi", "x_lo", "m_ps", "m_abs", "m_max", "pow2", "inv", "scale", "ms",
                                            "m_hi", "m_lo", "mask", "xt_ps", "xt_act", "xt_dve")}
        XP, M12, tab = st["XP"], st["M12"], st["tab"]
        with nc.Block() as block:

            @block.sync
            def _(sp):
                for k in range(2):
                    sp.dma_start(WhT[:, :, k, :], w["WhT"]).then_inc(loaded, 16)
                    sp.dma_start(tab[k * D:k * D + D, :, 0:HID], w["Wh"]).then_inc(loaded, 16)
                sp.dma_start(tab[:, :, WOUT:WOUT + D], w["Wout"]).then_inc(loaded, 16)
                sp.dma_start(bh[:, :], w["bh"]).then_inc(loaded, 16)

            @block.vector
            def _(dve):
                x = X[:, :, :, :].rearrange("p t b f -> p (t b) f")
                xp = XP[:, :, :, :].rearrange("p t b f -> p (t b) f")
                dve.tensor_scalar(out=xp[:, :, 0:D], in0=x, scalar1=SPLIT, scalar2=None, op0=ALU.mult)\
                    .then_inc(S["x_hi"], 1)
                dve.wait_ge(S["x_hi"], 1)
                dve.scalar_tensor_tensor(out=xp[:, :, D:2 * D], in0=x, scalar=SPLIT, in1=xp[:, :, 0:D],
                                         op0=ALU.mult, op1=ALU.subtract).then_inc(S["x_lo"], 1)
                dve.wait_ge(S["m_abs"], 1)
                dve.tensor_reduce(out=top[:, 0, :], in_=Ms[:, :, :], axis=AX.X, op=ALU.max).then_inc(S["m_abs"], 1)
                dve.wait_ge(S["m_max"], 1)
                dve.tensor_scalar(out=top[:, 1, :], in0=top[:, 1, :], scalar1=2.0 ** -100, scalar2=None, op0=ALU.max)\
                    .then_inc(S["pow2"], 1)
                dve.wait_ge(S["pow2"], 1)
                dve.tensor_scalar(out=top[:, 2, :].bitcast(I32), in0=top[:, 1, :].bitcast(I32), scalar1=0x7F800000,
                                  scalar2=None, op0=ALU.bitwise_and).then_inc(S["pow2"], 1)
                dve.wait_ge(S["pow2"], 2)
                dve.reciprocal(top[:, 3, :], top[:, 2, :]).then_inc(S["inv"], 1)
                dve.wait_ge(loaded, 16 * 6)
                dve.tensor_copy(tab[:, :, BIAS], bh[:, :]).then_inc(S["scale"], 1)
                dve.tensor_scalar(out=tab[:, :, SCALE_P], in0=top[:, 2, :], scalar1=2.0 ** -20, scalar2=None,
                                  op0=ALU.mult).then_inc(S["scale"], 1)
                dve.tensor_scalar(out=tab[:, :, SCALE_N], in0=top[:, 2, :], scalar1=-(2.0 ** -20), scalar2=None,
                                  op0=ALU.mult).then_inc(S["scale"], 1)
                dve.wait_ge(S["inv"], 1)
                dve.tensor_scalar(out=top[:, 3, :], in0=top[:, 3, :], scalar1=256.0, scalar2=None, op0=ALU.mult)\
                    .then_inc(S["inv"], 1)
                dve.wait_ge(S["inv"], 2)
                dve.tensor_tensor(out=Ms[:, :, :], in0=psM[:, :, :],
                                  in1=top[:, 3, :].unsqueeze(2).broadcast_to([P, HEADS, D]), op=ALU.mult)\
                    .then_inc(S["ms"], 1)
                dve.wait_ge(S["ms"], 1)
                dve.tensor_copy(M12[:, :, :], Ms[:, :, :]).then_inc(S["m_hi"], 1)
                dve.wait_ge(S["m_hi"], 1)
                dve.tensor_tensor(out=M12[D:P, :, :], in0=Ms[D:P, :, :], in1=M12[D:P, :, :], op=ALU.subtract)\
                    .then_inc(S["m_lo"], 1)
                for b in range(B):
                    dve.wait_ge(S["xt_ps"], b + 1)
                    dve.tensor_copy(st["XT2"][D:P, b, :], psX[b % 2][D:P, :]).then_inc(S["xt_dve"], 1)
                    dve.tensor_copy(st["XT2"][0:D, b, :], psX[b % 2][D:P, :]).then_inc(S["xt_dve"], 1)

            @block.gpsimd
            def _(pool):
                pool.memset(st["H2"][:, :, :, :], 0.0).then_inc(S["mask"], 1)
                pool.wait_ge(S["m_abs"], 2)
                pool.partition_all_reduce(top[:, 1, :], top[:, 0, :], P, bass.bass_isa.ReduceOp.max)\
                    .then_inc(S["m_max"], 1)

            @block.tensor
            def _(pe):
                pe.wait_ge(loaded, 16 * 6)
                for h in range(HEADS):
                    last = pe.matmul(psM[:, h, :], WhT[:, h, :, :].rearrange("p k f -> p (k f)"), WhT[:, h, 0, :],
                                     start=True, stop=True)
                last.then_inc(S["m_ps"], 1)
                pe.wait_ge(S["x_lo"], 1)
                for b in range(B):
                    if b >= 2:
                        pe.wait_ge(S["xt_act"], 2 * (b - 1))
                        pe.wait_ge(S["xt_dve"], 2 * (b - 1))
                    for t in range(NT):
                        last = pe.transpose(psX[b % 2][:, cols(t)], XP[:, t, b, :], c["ident16"][:, :])
                    last.then_inc(S["xt_ps"], 1)

            @block.scalar
            def _(act):
                act.wait_ge(S["m_ps"], 1)
                act.activation(Ms[:, :, :], psM[:, :, :], ACT.Abs).then_inc(S["m_abs"], 1)
                for b in range(B):
                    act.wait_ge(S["xt_ps"], b + 1)
                    act.activation(st["XT1"][D:P, b, :], psX[b % 2][0:D, :], ACT.Copy).then_inc(S["xt_act"], 1)
                    act.activation(st["XT1"][0:D, b, :], psX[b % 2][0:D, :], ACT.Copy).then_inc(S["xt_act"], 1)


def l1_heads(nc, c, st):
    U = B * HEADS
    with ExitStack() as ctx:
        m = Mem(nc, ctx)
        XT1, XT2, XP, M12, H2, tab, ident = (st[k] for k in ("XT1", "XT2", "XP", "M12", "H2", "tab", "ident"))
        neg = c["neg"]
        TQ = [m.sb(f"TQ{q}", [P, TAB]) for q in range(2)]
        GT = [m.sb(f"GT{q}", [P, N], F16) for q in range(2)]
        gg = m.sb("gg", [P, NT, P], F16)
        Z = m.sb("Z1", [P, 4, N])
        mx = m.sb("mx1", [P, 4])
        nb = m.sb("nb1", [P, 4])
        rs = [m.sb(f"rs{q}", [P, NT]) for q in range(2)]
        rinv = m.sb("rinv", [P, 4])
        EH = [m.sb(f"EH{k}", [P, NT, HALF], F16) for k in range(2)]
        EL = [m.sb(f"EL{k}", [P, NT, HALF], F16) for k in range(2)]
        Rs = m.sb("Rs", [P, HALF])
        OT = m.sb("OT", [P, HALF])
        yb = m.sb("yb", [P, HALF])
        yr = m.sb("yr", [P, HALF])
        psS = [m.ps(f"psS{i}", [P, N]) for i in range(2)]
        psE = [m.ps(f"psE{i}", [P, HALF]) for i in range(2)]
        psA = m.ps("psAtt", [P, HALF])
        psB = m.ps("psBank", [P, HALF])
        psB16 = psB[:, :].bitcast(F16)
        S = {k: m.sem("l1_" + k) for k in (
            "table", "g_ps", "g_hi", "g_lo", "gt_ps", "gt", "scores", "masked", "bias", "exps", "transposed", "hi", "lo",
            "o_ps", "rinv", "r_ps", "r_copied", "o_scaled", "y_ps", "y_biased", "y", "h2_ps", "h2")}

        def bh(u):
            return (u // HEADS, u % HEADS)

        with nc.Block() as block:

            @block.gpsimd
            def _(pool):
                def stage(u, q):
                    pool.tensor_copy(TQ[q][:, :], tab[:, u % HEADS, :]).then_inc(S["table"], 1)

                def unit(u, q, first=False, last=False):
                    if not first:
                        pool.wait_ge(S["h2_ps"], 2 * u)
                    if not last:
                        stage(u + 1, 1 - q)

                stage(0, 0)
                unit(0, 0, first=True)
                with pool.Fori(0, U // 2 - 1) as i:
                    unit(2 * i + 1, 1)
                    unit(2 * i + 2, 0)

            @block.tensor
            def _(pe):
                def g_product(u):
                    b, h = bh(u)
                    for t in range(NT):
                        pe.matmul(psB[:, cols(t, D)], XT1[:, b, cols(t)], M12[:, h, :], start=True, stop=False)
                        last = pe.matmul(psB[:, cols(t, D)], XT2[:, b, cols(t)], M12[:, h, :], start=False, stop=True)
                    last.then_inc(S["g_ps"], 1)

                def g_transpose(u):
                    pe.wait_ge(S["g_lo"], u + 1)
                    for t in range(NT):
                        last = pe.transpose(psB16[:, cols(t)], gg[:, t, :], c["ident16"][:, :])
                    last.then_inc(S["gt_ps"], 1)

                def scores(u, q, t):
                    b, _ = bh(u)
                    for xt, first in ((XT1, True), (XT2, False)):
                        for hf in range(2):
                            last = pe.matmul(psS[t % 2][:, cols(hf, HALF)], GT[q][:, cols(t)], xt[:, b, cols(hf, HALF)],
                                             start=first, stop=not first)
                    last.then_inc(S["scores"], 1)

                def transpose(u, t, first=False):
                    g = NT * u + t
                    pe.wait_ge(S["exps"], g + 1)
                    for k in range(2):
                        if not (first and t == 0):
                            pe.wait_ge(S["lo"], 2 * g - 1 + k)
                        for j in range(4):
                            last = pe.transpose(psE[k][:, cols(j)], Z[:, t % 4, cols(4 * k + j)], ident[:, :])
                        last.then_inc(S["transposed"], 1)

                def attend(u, half, j0):
                    b, _ = bh(u)
                    for j in range(j0, j0 + 4):
                        pe.matmul(psA[:, :], XP[:, j, b, :], EH[half][:, j, :], start=(j == 0), stop=False)
                        last = pe.matmul(psA[:, :], XP[:, j, b, :], EL[half][:, j, :], start=False, stop=(j == NT - 1))
                    if j0:
                        last.then_inc(S["o_ps"], 1)

                def spread_sums(i):
                    pe.wait_ge(S["rinv"], i + 1)
                    for t in range(4):
                        last = pe.matmul(psB[:, cols(t)], rinv[:, t:t + 1].broadcast_to([P, P]), ident[:, :],
                                         start=True, stop=True)
                    last.then_inc(S["r_ps"], 1)

                def times_w(i, q):
                    pe.wait_ge(S["o_scaled"], i + 1)
                    pe.matmul(psA[:, :], TQ[q][:, 0:HID], OT[:, :], start=True, stop=True).then_inc(S["y_ps"], 1)

                def times_wout(i, q):
                    pe.wait_ge(S["y"], i + 1)
                    for t in range(4):
                        last = pe.matmul(psB[:, cols(t, D)], yr[:, cols(t)], TQ[q][:, WOUT:WOUT + D],
                                         start=True, stop=True)
                    last.then_inc(S["h2_ps"], 1)

                def unit(u, q, first=False, last=False):
                    for t in range(NT):
                        if t < NT - 2:
                            pe.wait_ge(S["masked"], NT * u + t + 1)
                            scores(u, q, t + 2)
                        elif not last:
                            if t == NT - 2:
                                pe.wait_ge(S["gt"], u + 2)
                            pe.wait_ge(S["masked"], NT * u + t + 1)
                            scores(u + 1, 1 - q, t - NT + 2)
                        transpose(u, t, first)
                        if t == 0 and not first:
                            pe.wait_ge(S["lo"], 16 * u)
                            pe.wait_ge(S["y_biased"], 2 * u - 1)
                            attend(u - 1, 1, 0)
                            times_wout(2 * u - 2, 1 - q)
                        if t == 1:
                            if not first:
                                attend(u - 1, 1, 4)
                                pe.wait_ge(S["h2"], 2 * u - 1)
                            if not last:
                                g_product(u + 1)
                        if t == 2 and not first:
                            if not last:
                                pe.wait_ge(S["g_lo"], u + 2)
                            else:
                                pe.wait_ge(S["h2"], 2 * u - 1)
                            spread_sums(2 * u - 1)
                        if t == 3:
                            if not first:
                                times_w(2 * u - 1, 1 - q)
                                pe.wait_ge(S["r_copied"], 2 * u)
                            if not last:
                                g_transpose(u + 1)
                        if t == 4 and not first:
                            if not last:
                                pe.wait_ge(S["gt"], u + 2)
                            times_wout(2 * u - 1, 1 - q)
                        if t == 5:
                            if not first:
                                pe.wait_ge(S["y_biased"], 2 * u)
                            pe.wait_ge(S["lo"], 16 * u + 8)
                            attend(u, 0, 0)
                        if t == 6:
                            attend(u, 0, 4)
                            if not first:
                                pe.wait_ge(S["h2"], 2 * u)
                            else:
                                pe.wait_ge(S["gt"], u + 2)
                            spread_sums(2 * u)
                        if t == 7:
                            times_w(2 * u, q)

                g_product(0)
                g_transpose(0)
                pe.wait_ge(S["gt"], 1)
                scores(0, 0, 0)
                scores(0, 0, 1)
                unit(0, 0, first=True)
                with pe.Fori(0, U // 2 - 1) as i:
                    unit(2 * i + 1, 1)
                    unit(2 * i + 2, 0)
                unit(U - 1, 1, last=True)
                times_wout(2 * U - 2, 1)
                pe.wait_ge(S["lo"], 16 * U)
                attend(U - 1, 1, 0)
                attend(U - 1, 1, 4)
                pe.wait_ge(S["h2"], 2 * U - 1)
                spread_sums(2 * U - 1)
                times_w(2 * U - 1, 1)
                times_wout(2 * U - 1, 1)

            @block.scalar
            def _(act):
                def exps(u, q, t):
                    act.wait_ge(S["bias"], NT * u + t + 1)
                    act.activation(Z[:, t % 4, :], Z[:, t % 4, :], ACT.Exp, bias=nb[:, t % 4:t % 4 + 1],
                                   scale=TQ[q][:, SCALE_P:SCALE_P + 1], accum_out=rs[q][:, t:t + 1])\
                        .then_inc(S["exps"], 1)

                def high(u, t, first=False):
                    g = NT * u + t
                    half = t // 4
                    if t % 4 == 0 and not first:
                        act.wait_ge(S["o_ps"], 2 * u + half - 1)
                    for k in range(2):
                        act.wait_ge(S["transposed"], 2 * g + k + 1)
                        act.activation(EH[half][:, 4 * k:4 * k + 4, cols(t % 4)],
                                       psE[k][:, :].rearrange("p (j n) -> p j n", n=P), ACT.Copy).then_inc(S["hi"], 1)

                def g_high(u):
                    act.wait_ge(S["g_ps"], u + 1)
                    act.activation(gg[:, :, 0:D], psB[:, :].rearrange("p (t f) -> p t f", f=D), ACT.Copy,
                                   scale=1.0 / SPLIT).then_inc(S["g_hi"], 1)

                def g_copy(u, q):
                    act.wait_ge(S["gt_ps"], u + 1)
                    act.activation(GT[q][:, :], psB16, ACT.Copy).then_inc(S["gt"], 1)

                def copy_sums(i):
                    act.wait_ge(S["r_ps"], i + 1)
                    act.activation(Rs[:, :], psB[:, :], ACT.Copy, scale=1.0 / SPLIT).then_inc(S["r_copied"], 1)

                def add_bias(i, q):
                    act.wait_ge(S["y_ps"], i + 1)
                    act.activation(yb[:, :], psA[:, :], ACT.Identity, bias=TQ[q][:, BIAS:BIAS + 1])\
                        .then_inc(S["y_biased"], 1)

                def unit(u, q, first=False, last=False):
                    for t in range(NT):
                        if t < NT - 1:
                            exps(u, q, t + 1)
                        elif not last:
                            exps(u + 1, 1 - q, 0)
                        high(u, t, first)
                        if t == 1 and not last:
                            g_high(u + 1)
                        if t == 2 and not first:
                            copy_sums(2 * u - 1)
                        if t == 3:
                            if not first:
                                add_bias(2 * u - 1, 1 - q)
                            if not last:
                                g_copy(u + 1, 1 - q)
                        if t == 6:
                            copy_sums(2 * u)
                        if t == 7:
                            add_bias(2 * u, q)

                g_high(0)
                g_copy(0, 0)
                exps(0, 0, 0)
                unit(0, 0, first=True)
                with act.Fori(0, U // 2 - 1) as i:
                    unit(2 * i + 1, 1)
                    unit(2 * i + 2, 0)
                unit(U - 1, 1, last=True)
                copy_sums(2 * U - 1)
                add_bias(2 * U - 1, 1)

            @block.vector
            def _(dve):
                def mask(u, q, t):
                    g = NT * u + t
                    dve.wait_ge(S["scores"], g + 1)
                    apart(dve, c)
                    dve.tensor_tensor_reduce(out=Z[:, t % 4, :], in0=psS[t % 2][:, :], in1=neg[:, t, :], scale=1.0,
                                             scalar=LOWEST, op0=ALU.add, op1=ALU.max,
                                             accum_out=mx[:, t % 4:t % 4 + 1]).then_inc(S["masked"], 1)
                    if t == 0:
                        dve.wait_ge(S["table"], u + 1)
                    dve.wait_ge(S["masked"], g + 1)
                    dve.tensor_scalar(out=nb[:, t % 4:t % 4 + 1], in0=mx[:, t % 4:t % 4 + 1],
                                      scalar1=TQ[q][:, SCALE_N:SCALE_N + 1], scalar2=LN_PEAK,
                                      op0=ALU.mult, op1=ALU.add).then_inc(S["bias"], 1)

                def low(u, t):
                    g = NT * u + t
                    half = t // 4
                    for k in range(2):
                        dve.wait_ge(S["hi"], 2 * g + k + 1)
                        dve.tensor_tensor(out=EL[half][:, 4 * k:4 * k + 4, cols(t % 4)],
                                          in0=psE[k][:, :].rearrange("p (j n) -> p j n", n=P),
                                          in1=EH[half][:, 4 * k:4 * k + 4, cols(t % 4)],
                                          op=ALU.subtract).then_inc(S["lo"], 1)

                def g_low(u):
                    dve.wait_ge(S["g_hi"], u + 1)
                    dve.scalar_tensor_tensor(out=gg[:, :, D:P], in0=psB[:, :].rearrange("p (t f) -> p t f", f=D),
                                             scalar=1.0 / SPLIT, in1=gg[:, :, 0:D], op0=ALU.mult, op1=ALU.subtract)\
                        .then_inc(S["g_lo"], 1)

                def invert(i, q, half):
                    dve.wait_ge(S["exps"], 4 * i + 4)
                    dve.reciprocal(rinv[:, :], rs[q][:, 4 * half:4 * half + 4]).then_inc(S["rinv"], 1)

                def scale(i):
                    dve.wait_ge(S["r_copied"], i + 1)
                    dve.wait_ge(S["o_ps"], i + 1)
                    dve.tensor_tensor(out=OT[:, :], in0=psA[:, :], in1=Rs[:, :], op=ALU.mult).then_inc(S["o_scaled"], 1)

                def lrelu(i):
                    dve.wait_ge(S["y_biased"], i + 1)
                    dve.scalar_tensor_tensor(out=yr[:, :], in0=yb[:, :], scalar=0.01, in1=yb[:, :],
                                             op0=ALU.mult, op1=ALU.max).then_inc(S["y"], 1)

                def add_h2(i, u, half):
                    b = u // HEADS
                    dst = H2[:, 4 * half:4 * half + 4, b, :]
                    dve.wait_ge(S["h2_ps"], i + 1)
                    dve.tensor_tensor(out=dst, in0=dst, in1=psB[:, 0:4 * D].rearrange("p (t f) -> p t f", f=D),
                                      op=ALU.add).then_inc(S["h2"], 1)

                def unit(u, q, first=False, last=False):
                    for t in range(NT):
                        if t < NT - 2:
                            mask(u, q, t + 2)
                        elif not last:
                            mask(u + 1, 1 - q, t - NT + 2)
                        low(u, t)
                        if t == 0 and not first:
                            add_h2(2 * u - 2, u - 1, 0)
                            invert(2 * u - 1, 1 - q, 1)
                        if t == 1 and not last:
                            g_low(u + 1)
                        if t == 2 and not first:
                            scale(2 * u - 1)
                        if t == 3 and not first:
                            lrelu(2 * u - 1)
                        if t == 4 and not first:
                            add_h2(2 * u - 1, u - 1, 1)
                        if t == 5:
                            invert(2 * u, q, 0)
                        if t == 6:
                            scale(2 * u)
                        if t == 7:
                            lrelu(2 * u)

                g_low(0)
                mask(0, 0, 0)
                mask(0, 0, 1)
                unit(0, 0, first=True)
                with dve.Fori(0, U // 2 - 1) as i:
                    unit(2 * i + 1, 1)
                    unit(2 * i + 2, 0)
                unit(U - 1, 1, last=True)
                add_h2(2 * U - 2, U - 1, 0)
                invert(2 * U - 1, 1, 1)
                scale(2 * U - 1)
                lrelu(2 * U - 1)
                add_h2(2 * U - 1, U - 1, 1)


def attention(nc, c, X, kind, src, wts):
    dot = kind == "dot"
    with ExitStack() as ctx:
        m = Mem(nc, ctx, kind + "_")
        neg, ident = c["neg"], c["ident"]
        Xb = m.sb("Xb", [P, NT, D])
        Tb = m.sb("Tb", [D, N])
        Hb = m.sb("Hb", [P, NT, D])
        Z = m.sb("Z2", [P, 4, N])
        L = None if dot else m.sb("L2s", [P, 2, N])
        mx = m.sb("mx2", [P, 4])
        na = m.sb("na2", [P, 4])
        nb = m.sb("nb2", [P, 4])
        rs = m.sb("rs2", [P, 2, NT])
        e1 = m.sb("e1", [P, 2, NT])
        ET = m.sb("ET", [P, 2, NT, P])
        o = m.sb("o2", [P, NT, D])
        o2 = m.sb("o2b", [P, NT, D])
        psS = [m.ps(f"psT{i}", [P, N]) for i in range(2)]
        psE = [m.ps(f"psU{i}", [P, HALF]) for i in range(2)]
        psO = m.ps("psO", [P, NT, D])
        psV = m.ps("psV", [P, HALF])
        S = {k: m.sem("at_" + k) for k in (
            "staged", "t_ps", "t", "v_ps", "v", "e1", "scores", "masked", "na", "slope", "lrelu", "bias", "exps",
            "transposed", "ev0", "ev1", "o_ps", "rinv", "o1", "o2", "oexp", "o3", "x")}
        with nc.Block() as block:

            @block.gpsimd
            def _(pool):
                with pool.Fori(0, B) as b:
                    pool.wait_ge(S["o_ps"], NT * b + FREE)
                    pool.tensor_copy(Xb[:, :, :], src[:, :, b, :]).then_inc(S["staged"], 1)

            @block.tensor
            def _(pe):
                pe.sem_inc(S["o_ps"], FREE)
                with pe.Fori(0, B) as b:
                    pe.wait_ge(S["staged"], b + 1)
                    pe.wait_ge(S["masked"], NT * b + FREE)
                    apart(pe, c)
                    for t in range(NT):
                        last = pe.transpose(psS[0][0:D, cols(t)], Xb[:, t, :], ident[:, :])
                    last.then_inc(S["t_ps"], 1)
                    pe.wait_ge(S["t"], b + 1)
                    if not dot:
                        pe.wait_ge(S["v"], b + FREE)
                        for t in range(NT):
                            last = pe.matmul(psV[:, cols(t, D)], Tb[:, cols(t)], wts["W3T"][:, :], start=True, stop=True)
                        last.then_inc(S["v_ps"], 1)
                        for t in range(NT):
                            last = pe.matmul(psS[1][:, t:t + 1], Tb[:, cols(t)], wts["A"][0][:, 0:1], start=True, stop=True)
                        last.then_inc(S["scores"], 1)
                        for hf in range(2):
                            last = pe.matmul(psS[0][:, cols(hf, HALF)], wts["A"][1][:, :], Tb[:, cols(hf, HALF)],
                                             start=True, stop=True)
                        last.then_inc(S["scores"], 1)

                    def scores(t):
                        for hf in range(2):
                            last = pe.matmul(psS[t % 2][:, cols(hf, HALF)], Tb[:, cols(t)], Tb[:, cols(hf, HALF)],
                                             start=True, stop=True)
                        last.then_inc(S["scores"], 1)

                    def attend(t):
                        g = NT * b + t
                        pe.wait_ge(S["ev0"], g + 1 + FREE)
                        pe.wait_ge(S["ev1"], g + 1 + FREE)
                        if t == 0:
                            pe.wait_ge(S["o1"], b + FREE)
                            pe.wait_ge(S["v"], b + 1 + FREE)
                        for j in range(NT):
                            last = pe.matmul(psO[:, t, :], ET[:, t % 2, j, :], Hb[:, j, :],
                                             start=(j == 0), stop=(j == NT - 1))
                        last.then_inc(S["o_ps"], 1)

                    if dot:
                        scores(0)
                        scores(1)
                    for t in range(NT):
                        g = NT * b + t
                        if dot and t + 2 < NT:
                            pe.wait_ge(S["masked"], g + 1 + FREE)
                            scores(t + 2)
                        pe.wait_ge(S["exps"], g + 1)
                        for k in range(2):
                            pe.wait_ge(S[f"ev{k}"], g + FREE)
                            for j in range(4):
                                last = pe.transpose(psE[k][:, cols(j)], Z[:, t % 4, cols(4 * k + j)], ident[:, :])
                            last.then_inc(S["transposed"], 1)
                        if t:
                            attend(t - 1)
                    attend(NT - 1)

            @block.scalar
            def _(act):
                act.sem_inc(S["v"], FREE)
                act.sem_inc(S["ev0"], FREE)
                with act.Fori(0, B) as b:
                    act.wait_ge(S["t_ps"], b + 1)
                    act.activation(Tb[:, :], psS[0][0:D, :], ACT.Copy).then_inc(S["t"], 1)
                    if dot:
                        act.wait_ge(S["o_ps"], NT * b + FREE)
                        act.activation(Hb[:, :, :], Xb[:, :, :], ACT.Copy).then_inc(S["v"], 1)
                    else:
                        act.wait_ge(S["v_ps"], b + 1)
                        act.wait_ge(S["o_ps"], NT * b + FREE)
                        act.activation(Hb[:, :, :], psV[:, :].rearrange("p (t f) -> p t f", f=D), ACT.Copy)\
                            .then_inc(S["v"], 1)

                    def exps(t):
                        g = NT * b + t
                        if not dot:
                            if t == 0:
                                act.wait_ge(S["e1"], 2 * b + 2)
                            act.wait_ge(S["masked"], g + 1 + FREE)
                            act.activation(L[:, t % 2, :], Z[:, t % 4, :], ACT.Identity, scale=0.2,
                                           bias=e1[:, 1, t:t + 1]).then_inc(S["slope"], 1)
                            act.wait_ge(S["lrelu"], g + 1)
                        act.wait_ge(S["bias"], g + 1)
                        act.activation(Z[:, t % 4, :], Z[:, t % 4, :], ACT.Exp, bias=nb[:, t % 4:t % 4 + 1],
                                       accum_out=rs[:, 0, t:t + 1]).then_inc(S["exps"], 1)

                    exps(0)
                    for t in range(NT):
                        g = NT * b + t
                        if t + 1 < NT:
                            exps(t + 1)
                        act.wait_ge(S["transposed"], 2 * g + 1)
                        if t >= 2:
                            act.wait_ge(S["o_ps"], g - 1 + FREE)
                        act.activation(ET[:, t % 2, 0:4, :], psE[0][:, :].rearrange("p (j n) -> p j n", n=P), ACT.Copy)\
                            .then_inc(S["ev0"], 1)
                    if not dot:
                        act.wait_ge(S["o1"], b + 1 + FREE)
                        act.activation(o2[:, :, :], o[:, :, :], ACT.Exp).then_inc(S["oexp"], 1)

            @block.vector
            def _(dve):
                dve.sem_inc(S["masked"], FREE)
                dve.sem_inc(S["o1"], FREE)
                dve.sem_inc(S["ev1"], FREE)
                with dve.Fori(0, B) as b:
                    if not dot:
                        dve.wait_ge(S["scores"], 2 * b + 2)
                        dve.tensor_copy(e1[:, 0, :], psS[1][:, 0:NT]).then_inc(S["e1"], 1)
                        dve.tensor_scalar(out=e1[:, 1, :], in0=psS[1][:, 0:NT], scalar1=0.2, scalar2=None, op0=ALU.mult)\
                            .then_inc(S["e1"], 1)
                        dve.wait_ge(S["e1"], 2 * b + 2)

                    def mask(t):
                        g = NT * b + t
                        r = slice(t % 4, t % 4 + 1)
                        if dot:
                            dve.wait_ge(S["scores"], g + 1)
                        apart(dve, c)
                        dve.tensor_tensor_reduce(out=Z[:, t % 4, :], in0=psS[t % 2 if dot else 0][:, :],
                                                 in1=neg[:, t, :], scale=1.0, scalar=LOWEST, op0=ALU.add, op1=ALU.max,
                                                 accum_out=mx[:, r]).then_inc(S["masked"], 1)
                        dve.wait_ge(S["masked"], g + 1 + FREE)
                        if dot:
                            dve.tensor_scalar(out=nb[:, r], in0=mx[:, r], scalar1=-1.0, scalar2=None, op0=ALU.mult)\
                                .then_inc(S["bias"], 1)
                            return
                        dve.tensor_scalar(out=na[:, r], in0=mx[:, r], scalar1=e1[:, 0, t:t + 1], scalar2=-1.0,
                                          op0=ALU.add, op1=ALU.mult).then_inc(S["na"], 1)
                        dve.wait_ge(S["na"], g + 1)
                        dve.scalar_tensor_tensor(out=nb[:, r], in0=na[:, r], scalar=0.2, in1=na[:, r],
                                                 op0=ALU.mult, op1=ALU.min).then_inc(S["bias"], 1)

                    def lrelu(t):
                        g = NT * b + t
                        dve.wait_ge(S["slope"], g + 1)
                        dve.scalar_tensor_tensor(out=Z[:, t % 4, :], in0=Z[:, t % 4, :], scalar=e1[:, 0, t:t + 1],
                                                 in1=L[:, t % 2, :], op0=ALU.add, op1=ALU.max).then_inc(S["lrelu"], 1)

                    mask(0)
                    mask(1)
                    if not dot:
                        lrelu(0)
                    for t in range(NT):
                        g = NT * b + t
                        if t + 2 < NT:
                            mask(t + 2)
                        if not dot and t + 1 < NT:
                            lrelu(t + 1)
                        dve.wait_ge(S["transposed"], 2 * g + 2)
                        if t >= 2:
                            dve.wait_ge(S["o_ps"], g - 1 + FREE)
                        dve.tensor_copy(ET[:, t % 2, 4:8, :], psE[1][:, :].rearrange("p (j n) -> p j n", n=P))\
                            .then_inc(S["ev1"], 1)
                    dve.wait_ge(S["exps"], NT * b + NT)
                    dve.reciprocal(rs[:, 1, :], rs[:, 0, :]).then_inc(S["rinv"], 1)
                    dve.wait_ge(S["rinv"], b + 1)
                    dve.wait_ge(S["o_ps"], NT * b + NT + FREE)
                    dve.tensor_tensor(out=o[:, :, :], in0=psO[:, :, :],
                                      in1=rs[:, 1, :].unsqueeze(2).broadcast_to([P, NT, D]), op=ALU.mult)\
                        .then_inc(S["o1"], 1)
                    dve.wait_ge(S["o1"], b + 1 + FREE)
                    if dot:
                        dve.tensor_tensor(out=o[:, :, :], in0=o[:, :, :],
                                          in1=wts["bout"][:, :].unsqueeze(1).broadcast_to([P, NT, D]), op=ALU.add)\
                            .then_inc(S["o2"], 1)
                        dve.wait_ge(S["o2"], b + 1)
                        dve.scalar_tensor_tensor(out=o2[:, :, :], in0=o[:, :, :], scalar=0.01, in1=o[:, :, :],
                                                 op0=ALU.mult, op1=ALU.max).then_inc(S["o3"], 1)
                    else:
                        dve.wait_ge(S["oexp"], b + 1)
                        dve.tensor_scalar(out=o[:, :, :], in0=o[:, :, :], scalar1=0.0, scalar2=None, op0=ALU.max)\
                            .then_inc(S["o2"], 1)
                        dve.wait_ge(S["o2"], b + 1)
                        dve.scalar_tensor_tensor(out=o2[:, :, :], in0=o2[:, :, :], scalar=-1.0, in1=o[:, :, :],
                                                 op0=ALU.add, op1=ALU.min).then_inc(S["o3"], 1)
                    dve.wait_ge(S["o3"], b + 1)
                    dve.tensor_tensor(out=X[:, :, b, :], in0=X[:, :, b, :], in1=o2[:, :, :], op=ALU.add)\
                        .then_inc(S["x"], 1)


def layer1(nc, w, c, X):
    with ExitStack() as ctx:
        m = Mem(nc, ctx)
        H2 = m.sb("H2", [P, NT, B, D])
        bout = m.sb("bout", [P, D])
        with ExitStack() as inner:
            mi = Mem(nc, inner)
            st = dict(c, H2=H2, XT1=mi.sb("XT1", [P, B, N], F16), XT2=mi.sb("XT2", [P, B, N], F16),
                      XP=mi.sb("XP", [P, NT, B, 2 * D], F16), M12=mi.sb("M12", [P, HEADS, D], F16),
                      tab=mi.sb("tab", [P, HEADS, TAB]))
            l1_prepare(nc, w, c, X, st)
            l1_heads(nc, c, st)
        load(nc, [(bout[:, :], w["bout"].partition_broadcast(P))], "bout")
        attention(nc, c, X, "dot", H2, {"bout": bout})



def layer2(nc, w, c, X):
    STEPS, PAIRS = 3, B // 2
    with ExitStack() as ctx:
        m = Mem(nc, ctx)
        adjT = m.sb("adjT2", [P, NT, N])
        V = m.sb("V", [P, NT, B, D])
        VT = m.sb("VT", [P, PAIRS, N])
        W1a, W1b, W2 = (m.sb(k, [P, P]) for k in ("W1a", "W1b", "W2b"))
        b1, b2 = m.sb("b1", [P, 1]), m.sb("b2", [P, 1])
        b2r = m.sb("b2r", [P, 2, D])
        EF = m.sb("EF", [P, N])
        HT = m.sb("HT", [P, N])
        psE, psH, psT, psN = (m.ps(k, [P, N]) for k in ("psE2", "psH2", "psT2", "psN2"))
        zeroed, copied, loaded = m.sem("l2_zeroed"), m.sem("l2_copied"), m.sem("l2_loaded")
        adj_loaded = m.sem("l2_adj_loaded")
        S = {k: m.sem("l2_" + k) for k in ("vt0_ps", "vt0", "eff_ps", "eff", "h_ps", "h", "v_ps", "vt", "v")}
        with nc.Block() as block:

            @block.gpsimd
            def _(pool):
                for k in (W1a, W1b, W2):
                    pool.memset(k[:, :], 0.0).then_inc(zeroed, 1)

            @block.sync
            def _(sp):
                sp.dma_start(adjT[:, :, :], w["adjT"]).then_inc(adj_loaded, 16)
                sp.wait_ge(zeroed, 3)
                sp.wait_ge(copied, 1)
                n = 0
                for k in range(2):
                    blk = slice(k * D, k * D + D)
                    for dst, src in ((W1a[blk, blk], w["W1T"][0:D, :]), (W1b[blk, blk], w["W1T"][D:2 * D, :]),
                                     (W2[blk, blk], w["W2T"]), (b1[blk, :], w["b1"]), (b2[blk, :], w["b2"]),
                                     (b2r[:, k, :], w["b2row"].partition_broadcast(P))):
                        sp.dma_start(dst, src).then_inc(loaded, 16)
                        n += 1
                for b in range(B):
                    sp.dma_start(V[0:1, 0, b, :], w["iv"]).then_inc(loaded, 16)
                    n += 1
                assert n == 20

            @block.vector
            def _(dve):
                dve.sem_inc(S["v"], FREE)
                dve.tensor_copy(V[:, :, :, :], X[:, :, :, :]).then_inc(copied, 1)
                dve.wait_ge(loaded, 16 * 20)
                for p in range(PAIRS):
                    dve.wait_ge(S["vt0_ps"], p + 1)
                    dve.tensor_copy(VT[:, p, :], (psE, psH, psT, psN)[p][:, :]).then_inc(S["vt0"], 1)
                with dve.Fori(0, STEPS) as s:
                    for p in range(PAIRS):
                        i = PAIRS * s + p
                        dve.wait_ge(S["v_ps"], i + 1 + FREE)
                        dve.tensor_scalar(out=VT[:, p, :], in0=psT[:, :], scalar1=b2[:, 0:1], scalar2=None, op0=ALU.add)\
                            .then_inc(S["vt"], 1)
                        dve.tensor_tensor(out=V[:, :, 2 * p:2 * p + 2, :].rearrange("p t b f -> p t (b f)"),
                                          in0=psN[:, :].rearrange("p (t c) -> p t c", c=P),
                                          in1=b2r[:, :, :].rearrange("p b f -> p (b f)").unsqueeze(1)
                                          .broadcast_to([P, NT, P]), op=ALU.add).then_inc(S["v"], 1)
                dve.wait_ge(S["v"], STEPS * PAIRS + FREE)
                dve.tensor_tensor(out=X[:, :, :, :].rearrange("p t b f -> p (t b f)"),
                                  in0=X[:, :, :, :].rearrange("p t b f -> p (t b f)"),
                                  in1=V[:, :, :, :].rearrange("p t b f -> p (t b f)"), op=ALU.add).then_inc(copied, 1)

            @block.tensor
            def _(pe):
                pe.sem_inc(S["v_ps"], FREE)
                pe.wait_ge(loaded, 16 * 20)
                for p in range(PAIRS):
                    for t in range(NT):
                        last = pe.transpose((psE, psH, psT, psN)[p][:, cols(t)],
                                            V[:, t, 2 * p:2 * p + 2, :].rearrange("p b f -> p (b f)"), c["ident"][:, :])
                    last.then_inc(S["vt0_ps"], 1)
                pe.wait_ge(adj_loaded, 16)
                pe.wait_ge(S["vt0"], PAIRS)

                def effects(s, p):
                    i = PAIRS * s + p
                    pe.wait_ge(S["eff"], i + FREE)
                    for j in range(NT):
                        for hf in range(2):
                            last = pe.matmul(psE[:, cols(hf, HALF)],
                                             V[:, j, 2 * p:2 * p + 2, :].rearrange("p b f -> p (b f)"),
                                             adjT[:, j, cols(hf, HALF)], start=(j == 0), stop=(j == NT - 1))
                    last.then_inc(S["eff_ps"], 1)

                def update(s, p):
                    i = PAIRS * s + p
                    pe.wait_ge(S["eff"], i + 1 + FREE)
                    for hf in range(2):
                        pe.matmul(psH[:, cols(hf, HALF)], W1a[:, :], VT[:, p, cols(hf, HALF)], start=True, stop=False)
                        last = pe.matmul(psH[:, cols(hf, HALF)], W1b[:, :], EF[:, cols(hf, HALF)], start=False, stop=True)
                    last.then_inc(S["h_ps"], 1)

                def output(s, p):
                    i = PAIRS * s + p
                    pe.wait_ge(S["h"], i + 1)
                    pe.wait_ge(S["v"], i + FREE)
                    for hf in range(2):
                        pe.matmul(psT[:, cols(hf, HALF)], W2[:, :], HT[:, cols(hf, HALF)], start=True, stop=True)
                    for t in range(NT):
                        last = pe.matmul(psN[:, cols(t)], HT[:, cols(t)], W2[:, :], start=True, stop=True)
                    last.then_inc(S["v_ps"], 1)

                with pe.Fori(0, STEPS) as s:
                    pe.wait_ge(S["v"], PAIRS * s + FREE)
                    effects(s, 0)
                    for p in range(PAIRS):
                        update(s, p)
                        if p + 1 < PAIRS:
                            effects(s, p + 1)
                        output(s, p)

            @block.scalar
            def _(act):
                act.sem_inc(S["eff"], FREE)
                with act.Fori(0, STEPS) as s:
                    for p in range(PAIRS):
                        i = PAIRS * s + p
                        act.wait_ge(S["eff_ps"], i + 1)
                        act.activation(EF[:, :], psE[:, :], ACT.Copy).then_inc(S["eff"], 1)
                        act.wait_ge(S["h_ps"], i + 1)
                        act.wait_ge(S["v_ps"], i + FREE)
                        act.activation(HT[:, :], psH[:, :], ACT.Relu, bias=b1[:, 0:1]).then_inc(S["h"], 1)



def layer3(nc, w, c, X):
    with ExitStack() as ctx:
        m = Mem(nc, ctx)
        W3T, W3 = m.sb("W3T", [D, D]), m.sb("W3", [D, D])
        a3 = m.sb("a3", [D, 2])
        a3b = m.sb("a3b", [D, 2, P])
        A = [m.sb(f"A{k}", [D, P]) for k in range(2)]
        with ExitStack() as inner:
            mi = Mem(nc, inner)
            psA = mi.ps("psA3", [D, 2, P])
            loaded, ones, rep, a_ps, done = (mi.sem("l3_" + k) for k in ("loaded", "ones", "rep", "a_ps", "a"))
            with nc.Block() as block:

                @block.sync
                def _(sp):
                    for dst, src in ((W3T[:, :], w["W3T"]), (W3[:, :], w["W3"]), (a3[:, :], w["a3"])):
                        sp.dma_start(dst, src).then_inc(loaded, 16)

                @block.vector
                def _(dve):
                    dve.memset(a3b[:, :, :], 1.0).then_inc(ones, 1)
                    dve.wait_ge(ones, 1)
                    dve.wait_ge(loaded, 48)
                    for k in range(2):
                        dve.tensor_scalar(out=a3b[:, k, :], in0=a3b[:, k, :], scalar1=a3[:, k:k + 1], scalar2=None,
                                          op0=ALU.mult).then_inc(rep, 1)
                    dve.wait_ge(a_ps, 1)
                    for k in range(2):
                        dve.tensor_copy(A[k][:, :], psA[:, k, :]).then_inc(done, 1)

                @block.tensor
                def _(pe):
                    pe.wait_ge(rep, 2)
                    for k in range(2):
                        last = pe.matmul(psA[:, k, :], W3[:, :], a3b[:, k, :], start=True, stop=True)
                    last.then_inc(a_ps, 1)

        attention(nc, c, X, "add", X, {"W3T": W3T, "A": A})


LAYERS = {0: layer0, 1: layer1, 2: layer2, 3: layer3}


def build(nc, w, out, layers=(0, 1, 2, 3)):
    with ExitStack() as ctx:
        m = Mem(nc, ctx)
        X = m.sb("X", [P, NT, B, D])
        c = {"ident": m.sb("ident", [P, P]), "ident16": m.sb("ident16", [P, P], F16),
             "built": m.sem("ident_built"), "passed": m.sem("passed"),
             "neg": m.sb("neg", [P, NT, N], BF16)}
        make_constants(nc, c)
        load(nc, [(X[:, :, :, :], w["x"])], "x")
        for n in layers:
            LAYERS[n](nc, w, c, X)
            layer_norm(nc, X, f"_{n}")
        stored = m.sem("stored")
        with nc.Block() as block:

            @block.sync
            def _(sp):
                sp.dma_start(out, X[:, :, :, :]).then_inc(stored, 16)
                sp.wait_ge(stored, 16)


def host_layout(v):
    x, adj, H = v["x"], v["adj"], v["L0_gnn_H"]
    tiles = lambda a: a.reshape(NT, P, *a.shape[1:])
    return {
        "x": tiles(x.transpose(1, 0, 2)).transpose(1, 0, 2, 3),
        "xT": x.transpose(2, 0, 1),
        "adj": tiles(adj).transpose(1, 0, 2),
        "adjT": tiles(adj.T).transpose(1, 0, 2),
        "H": tiles(H).transpose(1, 0, 2),
        "HT": H.T,
        "W0": v["L0_gnn_W"], "W0T": v["L0_gnn_W"].T, "Wind": v["L0_gnn_W_ind"],
        "a_node": v["L0_gnn_a_node"][:, None], "a_gn": v["L0_gnn_a_gn"][:, None], "a_ge": v["L0_gnn_a_ge"][:, None],
        "fcW": v["L0_gnn_fcW"], "fcb": v["L0_gnn_fcb"][:, None], "av": v["L0_gnn_av"][:, None],
        "Wh": v["L1_gnn_Wh"].transpose(1, 0, 2),
        "WhT": v["L1_gnn_Wh"].transpose(2, 0, 1),
        "bh": v["L1_gnn_bh"].T,
        "Wout": v["L1_gnn_W_out"].reshape(HEADS, HID, D).transpose(1, 0, 2),
        "bout": v["L1_gnn_b_out"][None, :],
        "iv": v["L2_gnn_intervention_value"],
        "W1T": v["L2_gnn_W1"].T, "b1": v["L2_gnn_b1"][:, None],
        "W2T": v["L2_gnn_W2"].T, "b2": v["L2_gnn_b2"][:, None], "b2row": v["L2_gnn_b2"][None, :],
        "W3": v["L3_gnn_W"], "W3T": v["L3_gnn_W"].T, "a3": v["L3_gnn_a"].reshape(2, D).T,
    }


def kernel(**inputs):
    import concourse.bacc as bacc
    from concourse.bass_utils import run_bass_kernel_spmd

    nc = bacc.Bacc("TRN2", target_bir_lowering=False, num_devices=1)
    arrays, w = {}, {}
    for name, a in host_layout({k: np.asarray(v) for k, v in inputs.items()}).items():
        a = np.ascontiguousarray(a)
        arrays["in_" + name] = a
        w[name] = nc.dram_tensor("in_" + name, a.shape, mybir.dt.from_np(a.dtype), kind="ExternalInput").ap()
    out = nc.dram_tensor("out_x", [P, NT, B, D], F32, kind="ExternalOutput").ap()
    build(nc, w, out)
    r = run_bass_kernel_spmd(nc, [arrays], core_ids=[0])
    got = np.asarray(r.results[0]["out_x"])
    return np.ascontiguousarray(got.transpose(2, 1, 0, 3).reshape(B, N, D))
```

```python
from contextlib import ExitStack

import numpy as np

import concourse.bass as bass
from concourse import mybir

F32 = mybir.dt.float32
F16 = mybir.dt.float16
BF16 = mybir.dt.bfloat16
I32 = mybir.dt.int32
ACT = mybir.ActivationFunctionType
ALU = mybir.AluOpType
AX = mybir.AxisListType

P = 128
B, N, D = 8, 1024, 64
NT = N // P
HEADS, HID = 8, 128
E = 64
HALF = 512
NEG = -1.0e30
LOWEST = -3.0e38
SPLIT = 4096.0
LN_PEAK = 10.397207708
EPS = 1e-5
KEEP = 2
FREE = 1


class Mem:

    def __init__(self, nc, ctx, tag=""):
        self.nc, self.ctx, self.tag, self.sems = nc, ctx, tag, []

    def sb(self, name, shape, dt=F32):
        return self.ctx.enter_context(self.nc.sbuf_tensor(self.tag + name, shape, dt))

    def ps(self, name, shape, dt=F32):
        return self.ctx.enter_context(self.nc.psum_tensor(self.tag + name, shape, dt))

    def sem(self, name):
        if not self.sems:
            self.ctx.callback(self.clear)
        self.sems.append(self.nc.alloc_semaphore(self.tag + name))
        return self.sems[-1]

    def clear(self):
        self.nc.clear_and_free_semaphores(self.sems)
        self.nc.all_engine_barrier()


def cols(i, width=P):
    return slice(i * width, (i + 1) * width)


def apart(eng, c):
    eng.sem_inc(c["passed"], 1)


def make_constants(nc, c):
    with ExitStack() as ctx:
        m = Mem(nc, ctx)
        zeroed = m.sem("ident_zeroed")
        built = c["built"]
        with nc.Block() as block:

            @block.gpsimd
            def _(pool):
                pool.memset(c["ident"][:, :], 0.0).then_inc(zeroed, 1)
                pool.wait_ge(zeroed, 1)
                pool.affine_select(out=c["ident"][:, :], in_=c["ident"][:, :], compare_op=ALU.not_equal, fill=1.0,
                                   base=0, pattern=[[-1, P]], channel_multiplier=1).then_inc(built, 1)
                pool.wait_ge(built, 1)
                pool.tensor_copy(c["ident16"][:, :], c["ident"][:, :]).then_inc(built, 1)
                pool.wait_ge(built, 2)


def load(nc, pairs, tag):
    with ExitStack() as ctx:
        loaded = Mem(nc, ctx).sem("loaded_" + tag)
        with nc.Block() as block:

            @block.sync
            def _(sp):
                for dst, src in pairs:
                    sp.dma_start(dst, src).then_inc(loaded, 16)
                sp.wait_ge(loaded, 16 * len(pairs))


def layer_norm(nc, X, tag):
    with ExitStack() as ctx:
        m = Mem(nc, ctx)
        G = NT * B
        sq = m.sb("sq" + tag, [P, G, D])
        mean = m.sb("mean" + tag, [P, G])
        var = m.sb("var" + tag, [P, G])
        step = m.sem("ln_step" + tag)
        centred = m.sem("ln_centred" + tag)
        squared = m.sem("ln_squared" + tag)
        var_ready = m.sem("ln_var" + tag)
        std_ready = m.sem("ln_std" + tag)
        x = X[:, :, :, :].rearrange("p t b f -> p (t b) f")
        with nc.Block() as block:

            @block.vector
            def _(dve):
                dve.tensor_reduce(out=mean[:, :], in_=x, axis=AX.X, op=ALU.add).then_inc(step, 1)
                dve.wait_ge(step, 1)
                dve.tensor_scalar(out=mean[:, :], in0=mean[:, :], scalar1=1.0 / D, scalar2=None,
                                  op0=ALU.mult).then_inc(step, 1)
                dve.wait_ge(step, 2)
                dve.tensor_tensor(out=x, in0=x, in1=mean[:, :].unsqueeze(2).broadcast_to([P, G, D]),
                                  op=ALU.subtract).then_inc(centred, 1)
                dve.wait_ge(squared, 1)
                dve.tensor_reduce(out=var[:, :], in_=sq[:, :, :], axis=AX.X, op=ALU.add).then_inc(step, 1)
                dve.wait_ge(step, 3)
                dve.tensor_scalar(out=var[:, :], in0=var[:, :], scalar1=1.0 / D, scalar2=EPS,
                                  op0=ALU.mult, op1=ALU.add).then_inc(var_ready, 1)
                dve.wait_ge(std_ready, 1)
                dve.reciprocal(var[:, :], mean[:, :]).then_inc(step, 1)
                dve.wait_ge(step, 4)
                dve.tensor_tensor(out=x, in0=x, in1=var[:, :].unsqueeze(2).broadcast_to([P, G, D]),
                                  op=ALU.mult).then_inc(step, 1)
                dve.wait_ge(step, 5)

            @block.scalar
            def _(act):
                act.wait_ge(centred, 1)
                act.activation(sq[:, :, :], x, ACT.Square).then_inc(squared, 1)
                act.wait_ge(var_ready, 1)
                act.activation(mean[:, :], var[:, :], ACT.Sqrt).then_inc(std_ready, 1)



def l0_prepare(nc, w, X, st):
    LANES = 2
    with ExitStack() as ctx:
        m = Mem(nc, ctx)
        W2 = m.sb("W2", [D, 2 * D])
        WT2 = m.sb("WT2", [D, 2 * D])
        wvec = m.sb("wvec", [D, 3])
        ones = m.sb("ones0", [P, P])
        avec = m.sb("avec", [D, 2, P])
        Lnode = m.sb("Lnode", [D, P])
        Lgate = m.sb("Lgate", [D, P])
        hT_neg = m.sb("hT_neg", [P, N])
        h_neg = m.sb("h_neg", [P, NT, E])
        avb = m.sb("avb", [P, P])

        def lanes(name, shape):
            return [m.sb(f"{name}{l}", shape) for l in range(LANES)]

        xb_ = lanes("xT_batch", [D, N])
        lg_ = lanes("lg", [P, N])
        al_ = lanes("al", [P, N])
        alT_ = lanes("alT", [P, NT, E])
        hN_ = lanes("hN", [P, NT, 2 * D])
        small_ = lanes("small0", [P, 8])
        agT_ = lanes("agT", [P, 2, E])
        ex_ = lanes("ex", [P, E])
        he_ = lanes("he", [P, E])
        Tse_ = lanes("Tse", [P, E])
        cst_ = lanes("cst", [P, 2, NT])
        psN_ = [m.ps(f"psN{l}", [P, N]) for l in range(LANES)]
        psP_ = [m.ps(f"psP{l}", [P, N]) for l in range(LANES)]

        def each_lane(eng, steps):
            with eng.Fori(0, B // LANES) as i:
                for step in steps:
                    for l in range(LANES):
                        step(LANES * i + l, l)

        loaded = m.sem("l0_loaded")
        xb_loaded = [m.sem(f"l0_xb_loaded{l}") for l in range(LANES)]
        pro = {k: m.sem("l0_" + k) for k in ("avec", "L_ps", "masks", "avb")}
        S = {k: m.sem("l0_" + k) for k in (
            "projected", "projected_c", "projected_g", "ht_copied", "slope", "lrelu", "h_copied", "masked", "nmax", "alpha_exp", "alpha_inv", "alpha", "alphaT_ps",
            "alphaT", "agg_ps", "agg", "agg_exp", "agg_relu", "he", "edge_ps", "q", "Tse", "beta_t", "beta32",
            "beta_hi", "beta", "se_ps", "c_lg", "c_max", "c_sub", "c_exp", "c_sum", "c_inv", "c_inv2", "c_ready",
            "cT_ps", "cT_hi", "batch")}
        with nc.Block() as block:

            @block.sync
            def _(sp):
                n = 0
                for dst, src in ((W2[:, 0:D], w["W0"]), (W2[:, D:2 * D], w["W0"]),
                                 (WT2[:, 0:D], w["W0T"]), (WT2[:, D:2 * D], w["W0T"]),
                                 (wvec[:, 0:1], w["a_node"]), (wvec[:, 1:2], w["a_gn"]), (wvec[:, 2:3], w["a_ge"]),
                                 (hT_neg[0:E, :], w["HT"]), (hT_neg[E:P, :], w["HT"]),
                                 (h_neg[:, :, :], w["H"]), (st["fcW"][:, :], w["fcW"]), (st["fcb"][:, :], w["fcb"]),
                                 (st["av"][:, 0:1], w["av"])):
                    sp.dma_start(dst, src).then_inc(loaded, 16)
                    n += 1
                assert n == 13

                def load_x(b, l):
                    sp.wait_ge(S["projected_g"], b + 1)
                    sp.dma_start(xb_[l][:, :], w["xT"][:, bass.ds(b, 1), :].squeeze(1))\
                        .then_inc(xb_loaded[l], 16)

                each_lane(sp, [load_x])

            @block.vector
            def _(dve):
                dve.sem_inc(S["batch"], LANES)
                dve.memset(ones[:, :], 1.0).then_inc(pro["avb"], 1)
                dve.wait_ge(loaded, 16 * 13)
                dve.wait_ge(pro["avb"], 1)
                dve.tensor_scalar(out=avec[:, 0, :], in0=ones[0:D, :], scalar1=wvec[:, 0:1], scalar2=None,
                                  op0=ALU.mult).then_inc(pro["avec"], 1)
                dve.tensor_scalar(out=avec[:, 1, :], in0=ones[0:D, :], scalar1=wvec[:, 1:2], scalar2=None,
                                  op0=ALU.mult).then_inc(pro["avec"], 1)
                dve.tensor_scalar(out=avb[:, :], in0=ones[:, :], scalar1=st["av"][:, 0:1], scalar2=None,
                                  op0=ALU.mult).then_inc(pro["avb"], 1)
                dve.tensor_scalar(out=st["av"][:, 1:2], in0=st["av"][:, 0:1], scalar1=-1.0, scalar2=None,
                                  op0=ALU.mult).then_inc(pro["avb"], 1)
                dve.tensor_scalar(out=hT_neg[:, :], in0=hT_neg[:, :], scalar1=0.0, scalar2=NEG,
                                  op0=ALU.is_le, op1=ALU.mult).then_inc(pro["masks"], 1)
                dve.tensor_scalar(out=h_neg[:, :, :], in0=h_neg[:, :, :], scalar1=0.0, scalar2=NEG,
                                  op0=ALU.is_le, op1=ALU.mult).then_inc(pro["masks"], 1)
                dve.wait_ge(pro["L_ps"], 1)
                dve.tensor_copy(Lnode[:, :], psN_[0][0:D, 0:P]).then_inc(pro["masks"], 1)
                dve.tensor_copy(Lgate[:, :], psN_[0][0:D, P:2 * P]).then_inc(pro["masks"], 1)
                dve.wait_ge(pro["masks"], 4)

                def mask_nodes(b, l):
                    dve.wait_ge(S["slope"], b + 1)
                    dve.tensor_tensor(out=lg_[l][:, :], in0=psN_[l][:, :], in1=lg_[l][:, :], op=ALU.max)\
                        .then_inc(S["lrelu"], 1)
                    dve.wait_ge(S["lrelu"], b + 1)
                    apart(dve, st)
                    dve.tensor_tensor_reduce(out=al_[l][:, :], in0=lg_[l][:, :], in1=hT_neg[:, :], scale=1.0,
                                             scalar=LOWEST, op0=ALU.add, op1=ALU.max, accum_out=small_[l][:, 0:1])\
                        .then_inc(S["masked"], 1)
                    dve.wait_ge(S["masked"], b + 1)
                    dve.tensor_scalar(out=small_[l][:, 1:2], in0=small_[l][:, 0:1], scalar1=-1.0, scalar2=None,
                                      op0=ALU.mult).then_inc(S["nmax"], 1)

                def alpha(b, l):
                    dve.wait_ge(S["alpha_exp"], b + 1)
                    dve.reciprocal(small_[l][:, 3:4], small_[l][:, 2:3]).then_inc(S["alpha_inv"], 1)
                    dve.wait_ge(S["alpha_inv"], b + 1)
                    dve.tensor_scalar(out=al_[l][:, :], in0=al_[l][:, :], scalar1=small_[l][:, 3:4], scalar2=None,
                                      op0=ALU.mult).then_inc(S["alpha"], 1)

                def agg(b, l):
                    dve.wait_ge(S["agg_ps"], b + 1)
                    dve.tensor_copy(agT_[l][:, 0, :], psN_[l][:, HALF:HALF + E]).then_inc(S["agg"], 1)
                    dve.tensor_copy(agT_[l][:, 1, :], psN_[l][:, HALF:HALF + E]).then_inc(S["agg"], 1)
                    pairs = psN_[l][:, HALF:HALF + E].rearrange("p (j i) -> p j i", i=2)
                    dve.tensor_copy(st["aggP"][0:D, bass.ds(b, 1), :], pairs[0:D, :, 0].unsqueeze(1)).then_inc(S["agg"], 1)
                    dve.tensor_copy(st["aggP"][D:P, bass.ds(b, 1), :], pairs[D:P, :, 1].unsqueeze(1)).then_inc(S["agg"], 1)

                def edge_elu(b, l):
                    dve.wait_ge(S["agg"], 4 * b + 4)
                    dve.tensor_scalar(out=he_[l][:, :], in0=agT_[l][:, 0, :], scalar1=0.0, scalar2=None,
                                      op0=ALU.max).then_inc(S["agg_relu"], 1)
                    dve.wait_ge(S["agg_relu"], b + 1)
                    dve.wait_ge(S["agg_exp"], b + 1)
                    dve.scalar_tensor_tensor(out=he_[l][:, :], in0=ex_[l][:, :], scalar=-1.0, in1=he_[l][:, :],
                                             op0=ALU.add, op1=ALU.min).then_inc(S["he"], 1)

                def beta(b, l):
                    dve.wait_ge(S["beta_t"], b + 1)
                    dve.tensor_scalar(out=al_[l][:, :], in0=al_[l][:, :], scalar1=SPLIT / 2, scalar2=SPLIT / 2,
                                      op0=ALU.mult, op1=ALU.add).then_inc(S["beta32"], 1)
                    dve.wait_ge(S["beta32"], b + 1)
                    bs = st["BS"][:, bass.ds(b, 1), :].squeeze(1)
                    dve.tensor_copy(bs, al_[l][:, :]).then_inc(S["beta_hi"], 1)
                    dve.wait_ge(S["beta_hi"], b + 1)
                    bs_lo = st["BS"][E:P, bass.ds(b, 1), :].squeeze(1)
                    dve.tensor_tensor(out=bs_lo, in0=al_[l][E:P, :], in1=bs_lo, op=ALU.subtract).then_inc(S["beta"], 1)

                def coef_logits(b, l):
                    dve.wait_ge(S["se_ps"], b + 1)
                    dve.tensor_tensor(out=alT_[l][:, :, :], in0=h_neg[:, :, :],
                                      in1=psN_[l][:, 0:E].unsqueeze(1).broadcast_to([P, NT, E]),
                                      op=ALU.add).then_inc(S["c_lg"], 1)
                    dve.wait_ge(S["c_lg"], b + 1)
                    dve.tensor_reduce(out=cst_[l][:, 0, :], in_=alT_[l][:, :, :], axis=AX.X, op=ALU.max)\
                        .then_inc(S["c_max"], 1)
                    dve.wait_ge(S["c_max"], b + 1)
                    dve.tensor_tensor(out=alT_[l][:, :, :], in0=alT_[l][:, :, :],
                                      in1=cst_[l][:, 0, :].unsqueeze(2).broadcast_to([P, NT, E]),
                                      op=ALU.subtract).then_inc(S["c_sub"], 1)

                def coef_scale(b, l):
                    dve.wait_ge(S["c_exp"], b + 1)
                    dve.tensor_reduce(out=cst_[l][:, 0, :], in_=alT_[l][:, :, :], axis=AX.X, op=ALU.add)\
                        .then_inc(S["c_sum"], 1)
                    dve.wait_ge(S["c_sum"], b + 1)
                    dve.reciprocal(cst_[l][:, 1, :], cst_[l][:, 0, :]).then_inc(S["c_inv"], 1)
                    dve.wait_ge(S["c_inv"], b + 1)
                    dve.tensor_scalar(out=cst_[l][:, 1, :], in0=cst_[l][:, 1, :], scalar1=SPLIT, scalar2=None,
                                      op0=ALU.mult).then_inc(S["c_inv2"], 1)
                    dve.wait_ge(S["c_inv2"], b + 1)
                    twice = lg_[l][:, :].rearrange("p (t k e) -> p t k e", k=2, e=E)
                    for k in range(2):
                        dve.tensor_tensor(out=twice[:, :, k, :], in0=alT_[l][:, :, :],
                                          in1=cst_[l][:, 1, :].unsqueeze(2).broadcast_to([P, NT, E]),
                                          op=ALU.mult).then_inc(S["c_ready"], 1)

                def coef_low(b, l):
                    dve.wait_ge(S["cT_hi"], b + 1)
                    cs_lo = st["CS"][E:P, bass.ds(b, 1), :].squeeze(1)
                    dve.tensor_tensor(out=cs_lo, in0=psN_[l][E:P, :], in1=cs_lo, op=ALU.subtract).then_inc(S["batch"], 1)

                each_lane(dve, [mask_nodes, alpha, agg, edge_elu, beta, coef_logits, coef_scale, coef_low])

            @block.scalar
            def _(act):
                def copy_ht(b, l):
                    act.wait_ge(S["projected"], b + 1)
                    act.activation(lg_[l][:, :], psN_[l][:, :], ACT.Copy, scale=0.2).then_inc(S["slope"], 1)
                    act.activation(st["hT"][:, bass.ds(b, 1), :].squeeze(1), psP_[l][:, :], ACT.Copy)\
                        .then_inc(S["ht_copied"], 1)

                def copy_h(b, l):
                    act.wait_ge(S["projected_c"], b + 1)
                    act.activation(hN_[l][:, :, :], psP_[l][:, :].rearrange("p (t f) -> p t f", f=2 * D), ACT.Copy)\
                        .then_inc(S["h_copied"], 1)

                def alpha(b, l):
                    act.wait_ge(S["nmax"], b + 1)
                    act.activation(al_[l][:, :], al_[l][:, :], ACT.Exp, bias=small_[l][:, 1:2], accum_out=small_[l][:, 2:3])\
                        .then_inc(S["alpha_exp"], 1)

                def copy_alpha(b, l):
                    act.wait_ge(S["alphaT_ps"], b + 1)
                    act.activation(alT_[l][:, :, :], psN_[l][:, 0:HALF].rearrange("p (t e) -> p t e", e=E), ACT.Copy)\
                        .then_inc(S["alphaT"], 1)

                def edge_exp(b, l):
                    act.wait_ge(S["agg"], 4 * b + 4)
                    act.activation(ex_[l][:, :], agT_[l][:, 0, :], ACT.Exp).then_inc(S["agg_exp"], 1)

                def edge_tanh(b, l):
                    act.wait_ge(S["edge_ps"], b + 1)
                    act.activation(small_[l][:, 4:5], psN_[l][:, 0:1], ACT.Copy, scale=0.5).then_inc(S["q"], 1)
                    act.activation(Tse_[l][:, :], psN_[l][:, E:2 * E], ACT.Tanh, bias=st["fcb"][:, 0:1])\
                        .then_inc(S["Tse"], 1)

                def beta(b, l):
                    act.wait_ge(S["q"], b + 1)
                    act.wait_ge(S["projected_g"], b + 1 + LANES)
                    act.activation(al_[l][:, :], psP_[l][:, :], ACT.Tanh, bias=small_[l][:, 4:5], scale=0.5)\
                        .then_inc(S["beta_t"], 1)

                def coef_exp(b, l):
                    act.wait_ge(S["c_sub"], b + 1)
                    act.activation(alT_[l][:, :, :], alT_[l][:, :, :], ACT.Exp).then_inc(S["c_exp"], 1)

                def coef_high(b, l):
                    act.wait_ge(S["cT_ps"], b + 1)
                    act.activation(st["CS"][:, bass.ds(b, 1), :].squeeze(1), psN_[l][:, :], ACT.Copy).then_inc(S["cT_hi"], 1)

                each_lane(act, [copy_ht, copy_h, alpha, copy_alpha, edge_exp, edge_tanh, beta, coef_exp, coef_high])

            @block.tensor
            def _(pe):
                pe.sem_inc(S["projected_g"], LANES)
                ident = st["ident"]
                pe.wait_ge(pro["avec"], 2)
                for k in range(2):
                    last = pe.matmul(psN_[0][0:D, cols(k)], WT2[:, 0:D], avec[:, k, :], start=True, stop=True)
                last.then_inc(pro["L_ps"], 1)
                pe.wait_ge(pro["masks"], 4)
                pe.wait_ge(pro["avb"], 3)

                def project_ht(b, l):
                    pe.wait_ge(S["batch"], b + 1)
                    pe.wait_ge(xb_loaded[l], 8 * (b - l) + 16)
                    for hf in range(2):
                        pe.matmul(psN_[l][:, cols(hf, HALF)], Lnode[:, :], xb_[l][:, cols(hf, HALF)], start=True, stop=True)
                    for hf in range(2):
                        last = pe.matmul(psP_[l][:, cols(hf, HALF)], W2[:, :], xb_[l][:, cols(hf, HALF)],
                                         start=True, stop=True)
                    last.then_inc(S["projected"], 1)

                def project_h(b, l):
                    pe.wait_ge(S["ht_copied"], b + 1)
                    for t in range(NT):
                        last = pe.matmul(psP_[l][:, cols(t)], xb_[l][:, cols(t)], W2[:, :], start=True, stop=True)
                    last.then_inc(S["projected_c"], 1)

                def project_gate(b, l):
                    pe.wait_ge(S["h_copied"], b + 1)
                    for hf in range(2):
                        last = pe.matmul(psP_[l][:, cols(hf, HALF)], Lgate[:, :], xb_[l][:, cols(hf, HALF)],
                                         start=True, stop=True)
                    last.then_inc(S["projected_g"], 1)

                def alpha(b, l):
                    pe.wait_ge(S["alpha"], b + 1)
                    apart(pe, st)
                    for t in range(NT):
                        last = pe.transpose(psN_[l][:, cols(t, E)], al_[l][0:E, cols(t)], ident[0:E, 0:E])
                    last.then_inc(S["alphaT_ps"], 1)

                def agg(b, l):
                    pe.wait_ge(S["alphaT"], b + 1)
                    for t in range(NT):
                        last = pe.matmul(psN_[l][:, HALF:HALF + E], hN_[l][:, t, :], alT_[l][:, t, :],
                                         start=(t == 0), stop=(t == NT - 1))
                    last.then_inc(S["agg_ps"], 1)

                def edge(b, l):
                    pe.wait_ge(S["he"], b + 1)
                    pe.matmul(psN_[l][:, 0:1], agT_[l][0:D, :, :], wvec[:, 2:3], start=True, stop=True)
                    pe.matmul(psN_[l][:, E:2 * E], st["fcW"][:, :], he_[l][0:D, :], start=True, stop=True)\
                        .then_inc(S["edge_ps"], 1)

                def edge_score(b, l):
                    pe.wait_ge(S["Tse"], b + 1)
                    pe.matmul(psN_[l][:, 0:E], avb[:, :], Tse_[l][:, :], start=True, stop=True).then_inc(S["se_ps"], 1)

                def coefs(b, l):
                    pe.wait_ge(S["c_ready"], 2 * b + 2)
                    for t in range(NT):
                        last = pe.transpose(psN_[l][:, cols(t)], lg_[l][:, cols(t)], ident[:, :])
                    last.then_inc(S["cT_ps"], 1)

                each_lane(pe, [project_ht, project_h, project_gate, alpha, agg, edge, edge_score, coefs])


def l0_industry(nc, w, st, adjT, IND):
    with ExitStack() as ctx:
        m = Mem(nc, ctx)
        xT = m.sb("xTi", [D, B, N])
        Wi = m.sb("Wi", [D, D])
        Y = m.sb("Yi", [P, NT, B, D])
        adj = m.sb("adjn", [P, 2, N])
        deg = m.sb("deg", [P, NT])
        rdeg = m.sb("rdeg", [P, NT])
        psY = [m.ps(f"psY{i}", [P, NT, D]) for i in range(2)]
        psI = [m.ps(f"psI{i}", [P, B, D]) for i in range(2)]
        loaded, adj_loaded = m.sem("ind_loaded"), [m.sem("adjrow_loaded0"), m.sem("adjrow_loaded1")]
        adjT_loaded = m.sem("adjT_loaded")
        y_ps, y_ready, ind_ps, ind_ready = (m.sem("ind_" + k) for k in ("y_ps", "y", "ps", "ready"))
        deg_part, deg_ready = m.sem("deg_part"), m.sem("deg_ready")
        with nc.Block() as block:

            @block.sync
            def _(sp):
                sp.dma_start(xT[:, :, :], w["xT"]).then_inc(loaded, 16)
                sp.dma_start(Wi[:, :], w["Wind"]).then_inc(loaded, 16)
                sp.dma_start(adjT[:, :, :], w["adjT"]).then_inc(adjT_loaded, 16)
                for t in range(NT):
                    if t >= 2:
                        sp.wait_ge(deg_part, 2 * t - 2)
                    sp.dma_start(adj[:, t % 2, :], w["adj"][:, t, :]).then_inc(adj_loaded[t % 2], 16)

            @block.vector
            def _(dve):
                for t in range(NT):
                    dve.wait_ge(adj_loaded[t % 2], 16 * (t // 2 + 1))
                    dve.tensor_scalar(out=st["neg"][:, t, :], in0=adj[:, t % 2, :], scalar1=0.0, scalar2=NEG,
                                      op0=ALU.is_equal, op1=ALU.mult).then_inc(deg_part, 1)
                    dve.tensor_reduce(out=deg[:, t:t + 1], in_=adj[:, t % 2, :], axis=AX.X, op=ALU.add)\
                        .then_inc(deg_part, 1)
                dve.wait_ge(deg_part, 2 * NT)
                dve.tensor_scalar(out=deg[:, :], in0=deg[:, :], scalar1=1.0, scalar2=None, op0=ALU.max)\
                    .then_inc(deg_part, 1)
                dve.wait_ge(deg_part, 2 * NT + 1)
                dve.reciprocal(rdeg[:, :], deg[:, :]).then_inc(deg_ready, 1)

            @block.tensor
            def _(pe):
                pe.wait_ge(loaded, 32)
                for b in range(B):
                    if b >= 2:
                        pe.wait_ge(y_ready, b - 1)
                    for t in range(NT):
                        last = pe.matmul(psY[b % 2][:, t, :], xT[:, b, cols(t)], Wi[:, :], start=True, stop=True)
                    last.then_inc(y_ps, 1)
                pe.wait_ge(adjT_loaded, 16)
                pe.wait_ge(y_ready, B)
                for t in range(NT):
                    if t >= 2:
                        pe.wait_ge(ind_ready, t - 1)
                    for j in range(NT):
                        last = pe.matmul(psI[t % 2][:, :, :], adjT[:, j, cols(t)], Y[:, j, :, :],
                                         start=(j == 0), stop=(j == NT - 1))
                    last.then_inc(ind_ps, 1)

            @block.scalar
            def _(act):
                for b in range(B):
                    act.wait_ge(y_ps, b + 1)
                    act.activation(Y[:, :, b, :], psY[b % 2][:, :, :], ACT.Copy).then_inc(y_ready, 1)
                act.wait_ge(deg_ready, 1)
                for t in range(NT):
                    act.wait_ge(ind_ps, t + 1)
                    act.activation(IND[:, t, :, :], psI[t % 2][:, :, :], ACT.Copy, scale=rdeg[:, t:t + 1])\
                        .then_inc(ind_ready, 1)


def l0_edges(nc, st, gT):
    J = E // 2
    RING = 4
    G = J // RING
    with ExitStack() as ctx:
        m = Mem(nc, ctx)
        SEL = m.sb("SEL", [P, E, D], F16)
        SUM = m.sb("SUM", [P, D])
        v = m.sb("v", [P, RING, N])
        ex = m.sb("exv", [P, RING, N])
        y = m.sb("yv", [P, RING, N])
        cc = m.sb("cc", [P, N])
        psB = [m.ps(f"psB{i}", [P, N]) for i in range(2)]
        psC = m.ps("psCe", [P, N])
        psA = m.ps("psA", [D, N])
        sel = m.sem("sel_step")
        S = {k: m.sem("edge_" + k) for k in ("beta", "coef", "c_copied", "v", "exp", "relu", "elu", "y_even", "y_odd",
                                             "summed", "g")}

        def place(b, g, k):
            if not isinstance(g, int):
                return b, RING * g + k, RING // 2 * g + k // 2
            j = RING * g + k
            if j < 0:
                b, j = b - 1, j + J
            elif j >= J:
                b, j = b + 1, j - J
            return b, j, j // 2

        def count(b, g, k):
            b, j, _ = place(b, g, k)
            return J * b + j + 1

        def halves(b, g, k):
            b, _, h = place(b, g, k)
            return J // 2 * b + h + 1

        def phases(eng, step):
            def batch(b, first=False, last=False):
                for k in range(RING):
                    step(b, 0, k, k if first else RING)
                with eng.Fori(1, G - 1) as g:
                    for k in range(RING):
                        step(b, g, k, RING)
                for k in range(RING):
                    step(b, G - 1, k, RING, last=last)

            batch(0, first=True)
            with eng.Fori(1, B - 1) as b:
                batch(b)
            batch(B - 1, last=True)

        with nc.Block() as block:

            @block.gpsimd
            def _(pool):
                pool.memset(SEL[:, :, :], 0.0).then_inc(sel, 1)
                pool.memset(SUM[:, :], 0.0).then_inc(sel, 1)
                pool.wait_ge(sel, 2)
                for k in range(2):
                    pool.affine_select(out=SEL[:, :, :], in_=SEL[:, :, :], compare_op=ALU.not_equal, fill=1.0 / SPLIT,
                                       base=-E * k, pattern=[[-1, E], [0, D]], channel_multiplier=1).then_inc(sel, 1)
                    pool.affine_select(out=SUM[:, :], in_=SUM[:, :], compare_op=ALU.not_equal, fill=1.0,
                                       base=-D * k, pattern=[[-1, D]], channel_multiplier=1).then_inc(sel, 1)
                    pool.wait_ge(sel, 4 + 2 * k)

                def weigh(g, k, first=False):
                    pool.wait_ge(S["elu"], RING * g + k + 1)
                    pool.wait_ge(S["c_copied"], RING // 2 * g + k // 2 + 1)
                    if not first:
                        pool.wait_ge(S["summed"], RING * (g - 1) + k + 1)
                    pool.tensor_tensor(out=y[:, k, :], in0=ex[:, k, :], in1=cc[:, :], op=ALU.mult)\
                        .then_inc(S["y_odd"], 1)

                weigh(0, 1, True)
                weigh(0, 3, True)
                with pool.Fori(1, B * G) as g:
                    weigh(g, 1)
                    weigh(g, 3)

            @block.tensor
            def _(pe):
                pe.wait_ge(sel, 6)

                def gates(b, g, k):
                    b, j, _ = place(b, g, k)
                    for hf in range(2):
                        last = pe.matmul(psB[k % 2][:, cols(hf, HALF)], SEL[:, bass.ds(2 * j, 2), :],
                                         st["BS"][:, b, cols(hf, HALF)], start=True, stop=True)
                    last.then_inc(S["beta"], 1)

                def coefs(b, g, k):
                    b, j, _ = place(b, g, k)
                    for hf in range(2):
                        last = pe.matmul(psC[:, cols(hf, HALF)], SEL[:, bass.ds(2 * j, 2), :],
                                         st["CS"][:, b, cols(hf, HALF)], start=True, stop=True)
                    last.then_inc(S["coef"], 1)

                def add_up(b, g, k):
                    _, j, _ = place(b, g, k)
                    if k % 2:
                        pe.wait_ge(S["y_odd"], halves(b, g, k))
                    else:
                        pe.wait_ge(S["y_even"], halves(b, g, k))
                    first, final = (isinstance(j, int) and j == x for x in (0, J - 1))
                    for hf in range(2):
                        last = pe.matmul(psA[:, cols(hf, HALF)], SUM[:, :], y[:, k % RING, cols(hf, HALF)],
                                         start=first, stop=final)
                    last.then_inc(S["summed"], 1)

                def step(b, g, k, s, last=False):
                    if not (last and k >= 1):
                        pe.wait_ge(S["v"], count(b, g, k + 1))
                        gates(b, g, k + 3)
                    if k % 2:
                        pe.wait_ge(S["y_even"], halves(b, g, k - 1))
                    elif s > 1:
                        pe.wait_ge(S["c_copied"], halves(b, g, k - 1))
                    coefs(b, g, k)
                    if s >= 3:
                        if isinstance(g, int) and g == 0 and k == 3 and s == RING:
                            pe.wait_ge(S["g"], b)
                        add_up(b, g, k - 3)

                gates(0, 0, 0)
                gates(0, 0, 1)
                pe.wait_ge(S["v"], 1)
                gates(0, 0, 2)
                phases(pe, step)
                for k in (1, 2, 3):
                    add_up(B - 1, G - 1, k)

            @block.vector
            def _(dve):
                def gate(b, g, k):
                    dve.wait_ge(S["beta"], count(b, g, k))
                    b, j, _ = place(b, g, k)
                    dve.scalar_tensor_tensor(out=v[:, k % RING, :], in0=st["hT"][:, b, :],
                                             scalar=st["aggP"][:, b, bass.ds(j, 1)], in1=psB[k % 2][:, :],
                                             op0=ALU.subtract, op1=ALU.mult).then_inc(S["v"], 1)

                def elu(b, g, k):
                    dve.wait_ge(S["relu"], count(b, g, k))
                    dve.scalar_tensor_tensor(out=ex[:, k, :], in0=ex[:, k, :], scalar=-1.0, in1=v[:, k, :],
                                             op0=ALU.add, op1=ALU.min).then_inc(S["elu"], 1)

                def weigh(b, g, k, s):
                    dve.wait_ge(S["elu"], count(b, g, k))
                    dve.wait_ge(S["coef"], count(b, g, k))
                    if s >= RING:
                        dve.wait_ge(S["summed"], count(b, g, k - RING))
                    dve.tensor_tensor(out=y[:, k, :], in0=ex[:, k, :], in1=psC[:, :], op=ALU.mult)\
                        .then_inc(S["y_even"], 1)

                def step(b, g, k, s, last=False):
                    if k % 2:
                        weigh(b, g, k - 1, s)
                    if not (last and k >= 2):
                        gate(b, g, k + 2)
                    elu(b, g, k)

                gate(0, 0, 0)
                gate(0, 0, 1)
                phases(dve, step)

            @block.scalar
            def _(act):
                def exps(b, g, k, early=False):
                    act.wait_ge(S["v"], count(b, g, k))
                    if not early:
                        if k % 2:
                            act.wait_ge(S["y_odd"], halves(b, g, k - RING))
                        else:
                            act.wait_ge(S["y_even"], halves(b, g, k - RING))
                    bb, j, _ = place(b, g, k)
                    agg = st["aggP"][:, bb, bass.ds(j, 1)]
                    act.activation(ex[:, k % RING, :], v[:, k % RING, :], ACT.Exp, bias=agg).then_inc(S["exp"], 1)
                    act.activation(v[:, k % RING, :], v[:, k % RING, :], ACT.Relu, bias=agg).then_inc(S["relu"], 1)

                def copy_sum(b):
                    act.wait_ge(S["summed"], J * b + J)
                    apart(act, st)
                    act.activation(gT[:, bass.ds(b, 1), :].squeeze(1), psA[:, :], ACT.Copy).then_inc(S["g"], 1)

                def step(b, g, k, s, last=False):
                    if k % 2 == 0 and s > 1:
                        act.wait_ge(S["coef"], count(b, g, k - 1))
                        if s >= RING:
                            act.wait_ge(S["y_odd"], halves(b, g, k - 3))
                        act.activation(cc[:, :], psC[:, :], ACT.Copy).then_inc(S["c_copied"], 1)
                    if not (last and k == 3):
                        exps(b, g, k + 1, early=s < 3)
                    if isinstance(g, int) and g == 0 and k == 2 and s == RING:
                        copy_sum(b - 1)

                exps(0, 0, 0, early=True)
                phases(act, step)
                act.wait_ge(S["coef"], B * J)
                act.wait_ge(S["y_odd"], B * J // 2 - 1)
                act.activation(cc[:, :], psC[:, :], ACT.Copy).then_inc(S["c_copied"], 1)
                copy_sum(B - 1)


def l0_combine(nc, st, X, IND, gT):
    LANES = 2
    with ExitStack() as ctx:
        m = Mem(nc, ctx)

        def lanes(name, shape):
            return [m.sb(f"{name}{l}", shape) for l in range(LANES)]

        indb = lanes("indb", [P, NT, D])
        gb = lanes("gb", [D, N])
        indT = lanes("indT", [D, N])
        T1 = lanes("T1", [P, N])
        T2 = lanes("T2", [P, N])
        gN = lanes("gN", [P, NT, D])
        d = lanes("dmix", [P, NT, D])
        wt = lanes("wt", [P, NT])
        psF = [m.ps(f"psF{l}", [P, N]) for l in range(LANES)]
        psGn = [m.ps(f"psGn{l}", [P, NT, D]) for l in range(LANES)]
        psD = [m.ps(f"psD{l}", [P, NT]) for l in range(LANES)]
        S = {k: m.sem("comb_" + k) for k in ("staged", "tr", "indT", "fc1", "fc2", "tanh1", "tanh2", "diff", "w", "w1",
                                             "gN", "d", "d2", "d3", "x")}

        def each_lane(eng, steps):
            with eng.Fori(0, B // LANES) as i:
                for step in steps:
                    for l in range(LANES):
                        step(LANES * i + l, l)

        with nc.Block() as block:

            @block.gpsimd
            def _(pool):
                def stage(b, l):
                    pool.wait_ge(S["d3"], b + 1)
                    pool.tensor_copy(indb[l][:, :, :], IND[:, :, b, :]).then_inc(S["staged"], 1)
                    pool.tensor_copy(gb[l][:, :], gT[:, b, :]).then_inc(S["staged"], 1)

                each_lane(pool, [stage])

            @block.tensor
            def _(pe):
                def fc(l, src):
                    for hf in range(2):
                        last = pe.matmul(psF[l][:, cols(hf, HALF)], st["fcW"][:, :], src[:, cols(hf, HALF)],
                                         start=True, stop=True)
                    return last

                def turn(b, l):
                    pe.wait_ge(S["staged"], 2 * b + 2)
                    pe.wait_ge(S["tanh2"], b + 1)
                    apart(pe, st)
                    for t in range(NT):
                        pe.transpose(psF[l][0:D, cols(t)], indb[l][:, t, :], st["ident"][:, :])
                        last = pe.transpose(psGn[l][:, t, :], gb[l][:, cols(t)], st["ident"][0:D, 0:D])
                    last.then_inc(S["tr"], 1)

                def fc_industry(b, l):
                    pe.wait_ge(S["indT"], b + 1)
                    fc(l, indT[l]).then_inc(S["fc1"], 1)

                def fc_g(b, l):
                    pe.wait_ge(S["tanh1"], b + 1)
                    fc(l, gb[l]).then_inc(S["fc2"], 1)

                def difference(b, l):
                    pe.wait_ge(S["tanh2"], b + 1 + LANES)
                    pe.wait_ge(S["w"], b + 1)
                    for t in range(NT):
                        pe.matmul(psD[l][:, t:t + 1], T1[l][:, cols(t)], st["av"][:, 0:1], start=True, stop=False)
                        last = pe.matmul(psD[l][:, t:t + 1], T2[l][:, cols(t)], st["av"][:, 1:2],
                                         start=False, stop=True)
                    last.then_inc(S["diff"], 1)

                each_lane(pe, [turn, fc_industry, fc_g, difference])

            @block.scalar
            def _(act):
                act.sem_inc(S["tanh2"], LANES)
                act.sem_inc(S["w"], LANES)

                def copy_industry(b, l):
                    act.wait_ge(S["tr"], b + 1)
                    act.activation(indT[l][:, :], psF[l][0:D, :], ACT.Copy).then_inc(S["indT"], 1)

                def tanh_industry(b, l):
                    act.wait_ge(S["fc1"], b + 1)
                    act.activation(T1[l][:, :], psF[l][:, :], ACT.Tanh, bias=st["fcb"][:, 0:1]).then_inc(S["tanh1"], 1)

                def tanh_g(b, l):
                    act.wait_ge(S["fc2"], b + 1)
                    act.activation(T2[l][:, :], psF[l][:, :], ACT.Tanh, bias=st["fcb"][:, 0:1]).then_inc(S["tanh2"], 1)

                def weight(b, l):
                    act.wait_ge(S["diff"], b + 1)
                    act.activation(wt[l][:, :], psD[l][:, :], ACT.Tanh, scale=0.5).then_inc(S["w"], 1)

                each_lane(act, [copy_industry, tanh_industry, tanh_g, weight])

            @block.vector
            def _(dve):
                dve.sem_inc(S["d3"], LANES)

                def copy_g(b, l):
                    dve.wait_ge(S["tr"], b + 1)
                    dve.tensor_copy(gN[l][:, :, :], psGn[l][:, :, :]).then_inc(S["gN"], 1)

                def subtract(b, l):
                    dve.wait_ge(S["gN"], b + 1)
                    dve.tensor_tensor(out=d[l][:, :, :], in0=indb[l][:, :, :], in1=gN[l][:, :, :], op=ALU.subtract)\
                        .then_inc(S["d"], 1)

                def to_sigmoid(b, l):
                    dve.wait_ge(S["w"], b + 1 + LANES)
                    dve.tensor_scalar(out=wt[l][:, :], in0=wt[l][:, :], scalar1=0.5, scalar2=0.5, op0=ALU.mult,
                                      op1=ALU.add).then_inc(S["w1"], 1)

                def weigh(b, l):
                    dve.wait_ge(S["w1"], b + 1)
                    dve.tensor_tensor(out=d[l][:, :, :], in0=d[l][:, :, :],
                                      in1=wt[l][:, :].unsqueeze(2).broadcast_to([P, NT, D]),
                                      op=ALU.mult).then_inc(S["d2"], 1)

                def add_g(b, l):
                    dve.wait_ge(S["d2"], b + 1)
                    dve.tensor_tensor(out=d[l][:, :, :], in0=d[l][:, :, :], in1=gN[l][:, :, :], op=ALU.add)\
                        .then_inc(S["d3"], 1)

                def add_x(b, l):
                    dve.wait_ge(S["d3"], b + 1 + LANES)
                    dve.tensor_tensor(out=X[:, :, b, :], in0=X[:, :, b, :], in1=d[l][:, :, :], op=ALU.add)\
                        .then_inc(S["x"], 1)

                each_lane(dve, [copy_g, subtract, to_sigmoid, weigh, add_g, add_x])


def layer0(nc, w, c, X):
    with ExitStack() as ctx:
        m = Mem(nc, ctx)
        IND = m.sb("IND", [P, NT, B, D])
        st = dict(c)
        with ExitStack() as inner:
            mi = Mem(nc, inner)
            adjT = mi.sb("adjT0", [P, NT, N])
            l0_industry(nc, w, st, adjT, IND)
        st["fcW"] = m.sb("fcW", [D, P])
        st["fcb"] = m.sb("fcb", [P, 1])
        st["av"] = m.sb("av", [P, 2])
        gT = m.sb("gT", [D, B, N])
        st["hT"] = m.sb("hT", [P, B, N])
        st["BS"] = m.sb("BS", [P, B, N], F16)
        st["CS"] = m.sb("CS", [P, B, N], F16)
        st["aggP"] = m.sb("aggP", [P, B, E // 2])
        l0_prepare(nc, w, X, st)
        l0_edges(nc, st, gT)
        l0_combine(nc, st, X, IND, gT)



TAB = HID + 3 + D
BIAS, SCALE_P, SCALE_N, WOUT = HID, HID + 1, HID + 2, HID + 3


def l1_prepare(nc, w, c, X, st):
    with ExitStack() as ctx:
        m = Mem(nc, ctx)
        WhT = m.sb("WhT", [P, HEADS, 2, D])
        Ms = m.sb("Ms", [P, HEADS, D])
        bh = m.sb("bh", [P, HEADS])
        top = m.sb("top", [P, 4, HEADS])
        psM = m.ps("psM", [P, HEADS, D])
        psX = [m.ps(f"psX{i}", [P, N], F16) for i in range(2)]
        loaded = m.sem("l1_loaded")
        S = {k: m.sem("l1p_" + k) for k in ("x_hi", "x_lo", "m_ps", "m_abs", "m_max", "pow2", "inv", "scale", "ms",
                                            "m_hi", "m_lo", "mask", "xt_ps", "xt_act", "xt_dve")}
        XP, M12, tab = st["XP"], st["M12"], st["tab"]
        with nc.Block() as block:

            @block.sync
            def _(sp):
                for k in range(2):
                    sp.dma_start(WhT[:, :, k, :], w["WhT"]).then_inc(loaded, 16)
                    sp.dma_start(tab[k * D:k * D + D, :, 0:HID], w["Wh"]).then_inc(loaded, 16)
                sp.dma_start(tab[:, :, WOUT:WOUT + D], w["Wout"]).then_inc(loaded, 16)
                sp.dma_start(bh[:, :], w["bh"]).then_inc(loaded, 16)

            @block.vector
            def _(dve):
                x = X[:, :, :, :].rearrange("p t b f -> p (t b) f")
                xp = XP[:, :, :, :].rearrange("p t b f -> p (t b) f")
                dve.tensor_scalar(out=xp[:, :, 0:D], in0=x, scalar1=SPLIT, scalar2=None, op0=ALU.mult)\
                    .then_inc(S["x_hi"], 1)
                dve.wait_ge(S["x_hi"], 1)
                dve.scalar_tensor_tensor(out=xp[:, :, D:2 * D], in0=x, scalar=SPLIT, in1=xp[:, :, 0:D],
                                         op0=ALU.mult, op1=ALU.subtract).then_inc(S["x_lo"], 1)
                dve.wait_ge(S["m_abs"], 1)
                dve.tensor_reduce(out=top[:, 0, :], in_=Ms[:, :, :], axis=AX.X, op=ALU.max).then_inc(S["m_abs"], 1)
                dve.wait_ge(S["m_max"], 1)
                dve.tensor_scalar(out=top[:, 1, :], in0=top[:, 1, :], scalar1=2.0 ** -100, scalar2=None, op0=ALU.max)\
                    .then_inc(S["pow2"], 1)
                dve.wait_ge(S["pow2"], 1)
                dve.tensor_scalar(out=top[:, 2, :].bitcast(I32), in0=top[:, 1, :].bitcast(I32), scalar1=0x7F800000,
                                  scalar2=None, op0=ALU.bitwise_and).then_inc(S["pow2"], 1)
                dve.wait_ge(S["pow2"], 2)
                dve.reciprocal(top[:, 3, :], top[:, 2, :]).then_inc(S["inv"], 1)
                dve.wait_ge(loaded, 16 * 6)
                dve.tensor_copy(tab[:, :, BIAS], bh[:, :]).then_inc(S["scale"], 1)
                dve.tensor_scalar(out=tab[:, :, SCALE_P], in0=top[:, 2, :], scalar1=2.0 ** -20, scalar2=None,
                                  op0=ALU.mult).then_inc(S["scale"], 1)
                dve.tensor_scalar(out=tab[:, :, SCALE_N], in0=top[:, 2, :], scalar1=-(2.0 ** -20), scalar2=None,
                                  op0=ALU.mult).then_inc(S["scale"], 1)
                dve.wait_ge(S["inv"], 1)
                dve.tensor_scalar(out=top[:, 3, :], in0=top[:, 3, :], scalar1=256.0, scalar2=None, op0=ALU.mult)\
                    .then_inc(S["inv"], 1)
                dve.wait_ge(S["inv"], 2)
                dve.tensor_tensor(out=Ms[:, :, :], in0=psM[:, :, :],
                                  in1=top[:, 3, :].unsqueeze(2).broadcast_to([P, HEADS, D]), op=ALU.mult)\
                    .then_inc(S["ms"], 1)
                dve.wait_ge(S["ms"], 1)
                dve.tensor_copy(M12[:, :, :], Ms[:, :, :]).then_inc(S["m_hi"], 1)
                dve.wait_ge(S["m_hi"], 1)
                dve.tensor_tensor(out=M12[D:P, :, :], in0=Ms[D:P, :, :], in1=M12[D:P, :, :], op=ALU.subtract)\
                    .then_inc(S["m_lo"], 1)
                for b in range(B):
                    dve.wait_ge(S["xt_ps"], b + 1)
                    dve.tensor_copy(st["XT2"][D:P, b, :], psX[b % 2][D:P, :]).then_inc(S["xt_dve"], 1)
                    dve.tensor_copy(st["XT2"][0:D, b, :], psX[b % 2][D:P, :]).then_inc(S["xt_dve"], 1)

            @block.gpsimd
            def _(pool):
                pool.memset(st["H2"][:, :, :, :], 0.0).then_inc(S["mask"], 1)
                pool.wait_ge(S["m_abs"], 2)
                pool.partition_all_reduce(top[:, 1, :], top[:, 0, :], P, bass.bass_isa.ReduceOp.max)\
                    .then_inc(S["m_max"], 1)

            @block.tensor
            def _(pe):
                pe.wait_ge(loaded, 16 * 6)
                for h in range(HEADS):
                    last = pe.matmul(psM[:, h, :], WhT[:, h, :, :].rearrange("p k f -> p (k f)"), WhT[:, h, 0, :],
                                     start=True, stop=True)
                last.then_inc(S["m_ps"], 1)
                pe.wait_ge(S["x_lo"], 1)
                for b in range(B):
                    if b >= 2:
                        pe.wait_ge(S["xt_act"], 2 * (b - 1))
                        pe.wait_ge(S["xt_dve"], 2 * (b - 1))
                    for t in range(NT):
                        last = pe.transpose(psX[b % 2][:, cols(t)], XP[:, t, b, :], c["ident16"][:, :])
                    last.then_inc(S["xt_ps"], 1)

            @block.scalar
            def _(act):
                act.wait_ge(S["m_ps"], 1)
                act.activation(Ms[:, :, :], psM[:, :, :], ACT.Abs).then_inc(S["m_abs"], 1)
                for b in range(B):
                    act.wait_ge(S["xt_ps"], b + 1)
                    act.activation(st["XT1"][D:P, b, :], psX[b % 2][0:D, :], ACT.Copy).then_inc(S["xt_act"], 1)
                    act.activation(st["XT1"][0:D, b, :], psX[b % 2][0:D, :], ACT.Copy).then_inc(S["xt_act"], 1)


def l1_heads(nc, c, st):
    U = B * HEADS
    with ExitStack() as ctx:
        m = Mem(nc, ctx)
        XT1, XT2, XP, M12, H2, tab, ident = (st[k] for k in ("XT1", "XT2", "XP", "M12", "H2", "tab", "ident"))
        neg = c["neg"]
        TQ = [m.sb(f"TQ{q}", [P, TAB]) for q in range(2)]
        GT = [m.sb(f"GT{q}", [P, N], F16) for q in range(2)]
        gg = m.sb("gg", [P, NT, P], F16)
        Z = m.sb("Z1", [P, 4, N])
        mx = m.sb("mx1", [P, 4])
        nb = m.sb("nb1", [P, 4])
        rs = [m.sb(f"rs{q}", [P, NT]) for q in range(2)]
        rinv = m.sb("rinv", [P, 4])
        EH = [m.sb(f"EH{k}", [P, NT, HALF], F16) for k in range(2)]
        EL = [m.sb(f"EL{k}", [P, NT, HALF], F16) for k in range(2)]
        Rs = m.sb("Rs", [P, HALF])
        OT = m.sb("OT", [P, HALF])
        yb = m.sb("yb", [P, HALF])
        yr = m.sb("yr", [P, HALF])
        psS = [m.ps(f"psS{i}", [P, N]) for i in range(2)]
        psE = [m.ps(f"psE{i}", [P, HALF]) for i in range(2)]
        psA = m.ps("psAtt", [P, HALF])
        psB = m.ps("psBank", [P, HALF])
        psB16 = psB[:, :].bitcast(F16)
        S = {k: m.sem("l1_" + k) for k in (
            "table", "g_ps", "g_hi", "g_lo", "gt_ps", "gt", "scores", "masked", "bias", "exps", "transposed", "hi", "lo",
            "o_ps", "rinv", "r_ps", "r_copied", "o_scaled", "y_ps", "y_biased", "y", "h2_ps", "h2")}

        def bh(u):
            return (u // HEADS, u % HEADS)

        with nc.Block() as block:

            @block.gpsimd
            def _(pool):
                def stage(u, q):
                    pool.tensor_copy(TQ[q][:, :], tab[:, u % HEADS, :]).then_inc(S["table"], 1)

                def unit(u, q, first=False, last=False):
                    if not first:
                        pool.wait_ge(S["h2_ps"], 2 * u)
                    if not last:
                        stage(u + 1, 1 - q)

                stage(0, 0)
                unit(0, 0, first=True)
                with pool.Fori(0, U // 2 - 1) as i:
                    unit(2 * i + 1, 1)
                    unit(2 * i + 2, 0)

            @block.tensor
            def _(pe):
                def g_product(u):
                    b, h = bh(u)
                    for t in range(NT):
                        pe.matmul(psB[:, cols(t, D)], XT1[:, b, cols(t)], M12[:, h, :], start=True, stop=False)
                        last = pe.matmul(psB[:, cols(t, D)], XT2[:, b, cols(t)], M12[:, h, :], start=False, stop=True)
                    last.then_inc(S["g_ps"], 1)

                def g_transpose(u):
                    pe.wait_ge(S["g_lo"], u + 1)
                    for t in range(NT):
                        last = pe.transpose(psB16[:, cols(t)], gg[:, t, :], c["ident16"][:, :])
                    last.then_inc(S["gt_ps"], 1)

                def scores(u, q, t):
                    b, _ = bh(u)
                    for xt, first in ((XT1, True), (XT2, False)):
                        for hf in range(2):
                            last = pe.matmul(psS[t % 2][:, cols(hf, HALF)], GT[q][:, cols(t)], xt[:, b, cols(hf, HALF)],
                                             start=first, stop=not first)
                    last.then_inc(S["scores"], 1)

                def transpose(u, t, first=False):
                    g = NT * u + t
                    pe.wait_ge(S["exps"], g + 1)
                    for k in range(2):
                        if not (first and t == 0):
                            pe.wait_ge(S["lo"], 2 * g - 1 + k)
                        for j in range(4):
                            last = pe.transpose(psE[k][:, cols(j)], Z[:, t % 4, cols(4 * k + j)], ident[:, :])
                        last.then_inc(S["transposed"], 1)

                def attend(u, half, j0):
                    b, _ = bh(u)
                    for j in range(j0, j0 + 4):
                        pe.matmul(psA[:, :], XP[:, j, b, :], EH[half][:, j, :], start=(j == 0), stop=False)
                        last = pe.matmul(psA[:, :], XP[:, j, b, :], EL[half][:, j, :], start=False, stop=(j == NT - 1))
                    if j0:
                        last.then_inc(S["o_ps"], 1)

                def spread_sums(i):
                    pe.wait_ge(S["rinv"], i + 1)
                    for t in range(4):
                        last = pe.matmul(psB[:, cols(t)], rinv[:, t:t + 1].broadcast_to([P, P]), ident[:, :],
                                         start=True, stop=True)
                    last.then_inc(S["r_ps"], 1)

                def times_w(i, q):
                    pe.wait_ge(S["o_scaled"], i + 1)
                    pe.matmul(psA[:, :], TQ[q][:, 0:HID], OT[:, :], start=True, stop=True).then_inc(S["y_ps"], 1)

                def times_wout(i, q):
                    pe.wait_ge(S["y"], i + 1)
                    for t in range(4):
                        last = pe.matmul(psB[:, cols(t, D)], yr[:, cols(t)], TQ[q][:, WOUT:WOUT + D],
                                         start=True, stop=True)
                    last.then_inc(S["h2_ps"], 1)

                def unit(u, q, first=False, last=False):
                    for t in range(NT):
                        if t < NT - 2:
                            pe.wait_ge(S["masked"], NT * u + t + 1)
                            scores(u, q, t + 2)
                        elif not last:
                            if t == NT - 2:
                                pe.wait_ge(S["gt"], u + 2)
                            pe.wait_ge(S["masked"], NT * u + t + 1)
                            scores(u + 1, 1 - q, t - NT + 2)
                        transpose(u, t, first)
                        if t == 0 and not first:
                            pe.wait_ge(S["lo"], 16 * u)
                            pe.wait_ge(S["y_biased"], 2 * u - 1)
                            attend(u - 1, 1, 0)
                            times_wout(2 * u - 2, 1 - q)
                        if t == 1:
                            if not first:
                                attend(u - 1, 1, 4)
                                pe.wait_ge(S["h2"], 2 * u - 1)
                            if not last:
                                g_product(u + 1)
                        if t == 2 and not first:
                            if not last:
                                pe.wait_ge(S["g_lo"], u + 2)
                            else:
                                pe.wait_ge(S["h2"], 2 * u - 1)
                            spread_sums(2 * u - 1)
                        if t == 3:
                            if not first:
                                times_w(2 * u - 1, 1 - q)
                                pe.wait_ge(S["r_copied"], 2 * u)
                            if not last:
                                g_transpose(u + 1)
                        if t == 4 and not first:
                            if not last:
                                pe.wait_ge(S["gt"], u + 2)
                            times_wout(2 * u - 1, 1 - q)
                        if t == 5:
                            if not first:
                                pe.wait_ge(S["y_biased"], 2 * u)
                            pe.wait_ge(S["lo"], 16 * u + 8)
                            attend(u, 0, 0)
                        if t == 6:
                            attend(u, 0, 4)
                            if not first:
                                pe.wait_ge(S["h2"], 2 * u)
                            else:
                                pe.wait_ge(S["gt"], u + 2)
                            spread_sums(2 * u)
                        if t == 7:
                            times_w(2 * u, q)

                g_product(0)
                g_transpose(0)
                pe.wait_ge(S["gt"], 1)
                scores(0, 0, 0)
                scores(0, 0, 1)
                unit(0, 0, first=True)
                with pe.Fori(0, U // 2 - 1) as i:
                    unit(2 * i + 1, 1)
                    unit(2 * i + 2, 0)
                unit(U - 1, 1, last=True)
                times_wout(2 * U - 2, 1)
                pe.wait_ge(S["lo"], 16 * U)
                attend(U - 1, 1, 0)
                attend(U - 1, 1, 4)
                pe.wait_ge(S["h2"], 2 * U - 1)
                spread_sums(2 * U - 1)
                times_w(2 * U - 1, 1)
                times_wout(2 * U - 1, 1)

            @block.scalar
            def _(act):
                def exps(u, q, t):
                    act.wait_ge(S["bias"], NT * u + t + 1)
                    act.activation(Z[:, t % 4, :], Z[:, t % 4, :], ACT.Exp, bias=nb[:, t % 4:t % 4 + 1],
                                   scale=TQ[q][:, SCALE_P:SCALE_P + 1], accum_out=rs[q][:, t:t + 1])\
                        .then_inc(S["exps"], 1)

                def high(u, t, first=False):
                    g = NT * u + t
                    half = t // 4
                    if t % 4 == 0 and not first:
                        act.wait_ge(S["o_ps"], 2 * u + half - 1)
                    for k in range(2):
                        act.wait_ge(S["transposed"], 2 * g + k + 1)
                        act.activation(EH[half][:, 4 * k:4 * k + 4, cols(t % 4)],
                                       psE[k][:, :].rearrange("p (j n) -> p j n", n=P), ACT.Copy).then_inc(S["hi"], 1)

                def g_high(u):
                    act.wait_ge(S["g_ps"], u + 1)
                    act.activation(gg[:, :, 0:D], psB[:, :].rearrange("p (t f) -> p t f", f=D), ACT.Copy,
                                   scale=1.0 / SPLIT).then_inc(S["g_hi"], 1)

                def g_copy(u, q):
                    act.wait_ge(S["gt_ps"], u + 1)
                    act.activation(GT[q][:, :], psB16, ACT.Copy).then_inc(S["gt"], 1)

                def copy_sums(i):
                    act.wait_ge(S["r_ps"], i + 1)
                    act.activation(Rs[:, :], psB[:, :], ACT.Copy, scale=1.0 / SPLIT).then_inc(S["r_copied"], 1)

                def add_bias(i, q):
                    act.wait_ge(S["y_ps"], i + 1)
                    act.activation(yb[:, :], psA[:, :], ACT.Identity, bias=TQ[q][:, BIAS:BIAS + 1])\
                        .then_inc(S["y_biased"], 1)

                def unit(u, q, first=False, last=False):
                    for t in range(NT):
                        if t < NT - 1:
                            exps(u, q, t + 1)
                        elif not last:
                            exps(u + 1, 1 - q, 0)
                        high(u, t, first)
                        if t == 1 and not last:
                            g_high(u + 1)
                        if t == 2 and not first:
                            copy_sums(2 * u - 1)
                        if t == 3:
                            if not first:
                                add_bias(2 * u - 1, 1 - q)
                            if not last:
                                g_copy(u + 1, 1 - q)
                        if t == 6:
                            copy_sums(2 * u)
                        if t == 7:
                            add_bias(2 * u, q)

                g_high(0)
                g_copy(0, 0)
                exps(0, 0, 0)
                unit(0, 0, first=True)
                with act.Fori(0, U // 2 - 1) as i:
                    unit(2 * i + 1, 1)
                    unit(2 * i + 2, 0)
                unit(U - 1, 1, last=True)
                copy_sums(2 * U - 1)
                add_bias(2 * U - 1, 1)

            @block.vector
            def _(dve):
                def mask(u, q, t):
                    g = NT * u + t
                    dve.wait_ge(S["scores"], g + 1)
                    apart(dve, c)
                    dve.tensor_tensor_reduce(out=Z[:, t % 4, :], in0=psS[t % 2][:, :], in1=neg[:, t, :], scale=1.0,
                                             scalar=LOWEST, op0=ALU.add, op1=ALU.max,
                                             accum_out=mx[:, t % 4:t % 4 + 1]).then_inc(S["masked"], 1)
                    if t == 0:
                        dve.wait_ge(S["table"], u + 1)
                    dve.wait_ge(S["masked"], g + 1)
                    dve.tensor_scalar(out=nb[:, t % 4:t % 4 + 1], in0=mx[:, t % 4:t % 4 + 1],
                                      scalar1=TQ[q][:, SCALE_N:SCALE_N + 1], scalar2=LN_PEAK,
                                      op0=ALU.mult, op1=ALU.add).then_inc(S["bias"], 1)

                def low(u, t):
                    g = NT * u + t
                    half = t // 4
                    for k in range(2):
                        dve.wait_ge(S["hi"], 2 * g + k + 1)
                        dve.tensor_tensor(out=EL[half][:, 4 * k:4 * k + 4, cols(t % 4)],
                                          in0=psE[k][:, :].rearrange("p (j n) -> p j n", n=P),
                                          in1=EH[half][:, 4 * k:4 * k + 4, cols(t % 4)],
                                          op=ALU.subtract).then_inc(S["lo"], 1)

                def g_low(u):
                    dve.wait_ge(S["g_hi"], u + 1)
                    dve.scalar_tensor_tensor(out=gg[:, :, D:P], in0=psB[:, :].rearrange("p (t f) -> p t f", f=D),
                                             scalar=1.0 / SPLIT, in1=gg[:, :, 0:D], op0=ALU.mult, op1=ALU.subtract)\
                        .then_inc(S["g_lo"], 1)

                def invert(i, q, half):
                    dve.wait_ge(S["exps"], 4 * i + 4)
                    dve.reciprocal(rinv[:, :], rs[q][:, 4 * half:4 * half + 4]).then_inc(S["rinv"], 1)

                def scale(i):
                    dve.wait_ge(S["r_copied"], i + 1)
                    dve.wait_ge(S["o_ps"], i + 1)
                    dve.tensor_tensor(out=OT[:, :], in0=psA[:, :], in1=Rs[:, :], op=ALU.mult).then_inc(S["o_scaled"], 1)

                def lrelu(i):
                    dve.wait_ge(S["y_biased"], i + 1)
                    dve.scalar_tensor_tensor(out=yr[:, :], in0=yb[:, :], scalar=0.01, in1=yb[:, :],
                                             op0=ALU.mult, op1=ALU.max).then_inc(S["y"], 1)

                def add_h2(i, u, half):
                    b = u // HEADS
                    dst = H2[:, 4 * half:4 * half + 4, b, :]
                    dve.wait_ge(S["h2_ps"], i + 1)
                    dve.tensor_tensor(out=dst, in0=dst, in1=psB[:, 0:4 * D].rearrange("p (t f) -> p t f", f=D),
                                      op=ALU.add).then_inc(S["h2"], 1)

                def unit(u, q, first=False, last=False):
                    for t in range(NT):
                        if t < NT - 2:
                            mask(u, q, t + 2)
                        elif not last:
                            mask(u + 1, 1 - q, t - NT + 2)
                        low(u, t)
                        if t == 0 and not first:
                            add_h2(2 * u - 2, u - 1, 0)
                            invert(2 * u - 1, 1 - q, 1)
                        if t == 1 and not last:
                            g_low(u + 1)
                        if t == 2 and not first:
                            scale(2 * u - 1)
                        if t == 3 and not first:
                            lrelu(2 * u - 1)
                        if t == 4 and not first:
                            add_h2(2 * u - 1, u - 1, 1)
                        if t == 5:
                            invert(2 * u, q, 0)
                        if t == 6:
                            scale(2 * u)
                        if t == 7:
                            lrelu(2 * u)

                g_low(0)
                mask(0, 0, 0)
                mask(0, 0, 1)
                unit(0, 0, first=True)
                with dve.Fori(0, U // 2 - 1) as i:
                    unit(2 * i + 1, 1)
                    unit(2 * i + 2, 0)
                unit(U - 1, 1, last=True)
                add_h2(2 * U - 2, U - 1, 0)
                invert(2 * U - 1, 1, 1)
                scale(2 * U - 1)
                lrelu(2 * U - 1)
                add_h2(2 * U - 1, U - 1, 1)


def attention(nc, c, X, kind, src, wts):
    dot = kind == "dot"
    AHEAD = 2 if dot else 3
    with ExitStack() as ctx:
        m = Mem(nc, ctx, kind + "_")
        neg, ident = c["neg"], c["ident"]
        Xb = [m.sb(f"Xb{q}", [P, NT, D]) for q in range(2)]
        Tb = [m.sb(f"Tb{q}", [D, N]) for q in range(2)]
        Hb = Xb if dot else [m.sb(f"Hb{q}", [P, NT, D]) for q in range(2)]
        Z = m.sb("Z2", [P, 4, N])
        Z1 = None if dot else m.sb("Z1s", [P, 2, N])
        Z2 = None if dot else m.sb("Z2s", [P, 2, N])
        mx = m.sb("mx2", [P, 4])
        na = m.sb("na2", [P, 4])
        nm = m.sb("nm2", [P, 4])
        nb = m.sb("nb2", [P, 4, 2])
        rs = [m.sb(f"rs2{q}", [P, NT]) for q in range(2)]
        ri = m.sb("ri2", [P, NT])
        e1 = [m.sb(f"e1{q}", [P, NT, 2]) for q in range(2)]
        ET = m.sb("ET", [P, 2, NT, P])
        o = m.sb("o2", [P, NT, D])
        oe = m.sb("o2e", [P, NT, D])
        o2 = m.sb("o2b", [P, NT, D])
        psS = [m.ps(f"psT{i}", [P, N]) for i in range(2)]
        psE = [m.ps(f"psU{i}", [P, HALF]) for i in range(2)]
        psO = m.ps("psO", [P, NT, D])
        psV = m.ps("psV", [P, HALF])
        S = {k: m.sem("at_" + k) for k in (
            "staged", "t_ps", "t", "v_ps", "v", "e1_ps", "e1", "e2_ps", "scores", "masked", "na", "nm", "bias", "exps",
            "joined", "transposed", "ev0", "ev1", "o_ps", "rinv", "o1", "o2", "oexp", "o3", "x")}
        weights_ready = S["exps"] if dot else S["joined"]

        def phases(eng, unit):
            unit(0, 0, first=True)
            with eng.Fori(0, B // 2 - 1) as i:
                unit(2 * i + 1, 1)
                unit(2 * i + 2, 0)
            unit(B - 1, 1, last=True)

        with nc.Block() as block:

            @block.gpsimd
            def _(pool):
                def stage(b, q):
                    pool.tensor_copy(Xb[q][:, :, :], src[:, :, b, :]).then_inc(S["staged"], 1)

                def add_x(b):
                    pool.wait_ge(S["o3"], b + 1)
                    pool.tensor_tensor(out=X[:, :, b, :], in0=X[:, :, b, :], in1=o2[:, :, :], op=ALU.add)\
                        .then_inc(S["x"], 1)

                def unit(b, q, first=False, last=False):
                    if not first:
                        if dot:
                            pool.wait_ge(S["o_ps"], NT * b)
                        else:
                            pool.wait_ge(S["t_ps"], 2 * b)
                    if not last:
                        stage(b + 1, 1 - q)
                    if not first:
                        add_x(b - 1)

                pool.sem_inc(S["x"], FREE)
                stage(0, 0)
                phases(pool, unit)
                add_x(B - 1)

            @block.tensor
            def _(pe):
                def keep_warm(count):
                    for _ in range(count):
                        pe.matmul(psE[0][:, :], c["ident16"][:, :], c["ident16"][:, :].unsqueeze(1).broadcast_to([P, 4, P]),
                                  start=True, stop=True)

                def prepare_x(b, q, half, first=False):
                    if half == 0:
                        pe.wait_ge(S["staged"], b + 1)
                    if not first or half:
                        if half == 0 and not dot:
                            pe.wait_ge(S["e1"], 2 * b)
                        else:
                            pe.wait_ge(S["t"], 2 * b + half)
                        apart(pe, c)
                    for t in range(4):
                        last = pe.transpose(psV[0:D, cols(t)], Xb[q][:, 4 * half + t, :], ident[:, :])
                    last.then_inc(S["t_ps"], 1)

                def prepare_v(b, q):
                    pe.wait_ge(S["t"], 2 * b + 2)
                    for t in range(NT):
                        last = pe.matmul(psV[:, cols(t, D)], Tb[q][:, cols(t)], wts["W3T"][:, :], start=True, stop=True)
                    last.then_inc(S["v_ps"], 1)

                def prepare_e(b, q, early=False):
                    pe.wait_ge(S["v"], b + 1)
                    for t in range(NT):
                        last = pe.matmul(psV[:, t:t + 1], Tb[q][:, cols(t)], wts["A"][0][:, 0:1], start=True, stop=True)
                    last.then_inc(S["e1_ps"], 1)
                    if not early:
                        pe.wait_ge(S["masked"], NT * (b - 1))
                    for hf in range(2):
                        last = pe.matmul(psS[q][:, cols(hf, HALF)], wts["A"][1][:, :], Tb[q][:, cols(hf, HALF)],
                                         start=True, stop=True)
                    last.then_inc(S["e2_ps"], 1)

                def scores(q, t):
                    for hf in range(2):
                        last = pe.matmul(psS[t % 2][:, cols(hf, HALF)], Tb[q][:, cols(t)], Tb[q][:, cols(hf, HALF)],
                                         start=True, stop=True)
                    last.then_inc(S["scores"], 1)

                def attend(b, q, t, early=False):
                    g = NT * b + t
                    pe.wait_ge(S["ev0"], g + 1)
                    pe.wait_ge(S["ev1"], g + 1)
                    if t == 0 and not early:
                        pe.wait_ge(S["o1"], b)
                    for j in range(NT):
                        last = pe.matmul(psO[:, t, :], ET[:, t % 2, j, :], Hb[q][:, j, :],
                                         start=(j == 0), stop=(j == NT - 1))
                    last.then_inc(S["o_ps"], 1)

                def unit(b, q, first=False, last=False):
                    for t in range(NT):
                        g = NT * b + t
                        if dot:
                            if t + 2 < NT:
                                pe.wait_ge(S["masked"], g + 1)
                                scores(q, t + 2)
                            elif not last:
                                if t + 2 == NT:
                                    pe.wait_ge(S["t"], 2 * b + 4)
                                pe.wait_ge(S["masked"], g + 1)
                                scores(1 - q, t + 2 - NT)
                        if t == 0 and not first:
                            attend(b - 1, 1 - q, NT - 1)
                        if not dot:
                            if not (first and t == 0):
                                pe.wait_ge(S["ev0"], g)
                            keep_warm(KEEP)
                        pe.wait_ge(weights_ready, g + 1)
                        for k in range(2):
                            if not (first and t == 0):
                                pe.wait_ge(S[f"ev{k}"], g)
                            for j in range(4):
                                end = pe.transpose(psE[k][:, cols(j)], Z[:, t % 4, cols(4 * k + j)], ident[:, :])
                            end.then_inc(S["transposed"], 1)
                        if t:
                            attend(b, q, t - 1, first)
                        if not last:
                            if t in (1, 2):
                                prepare_x(b + 1, 1 - q, t - 1)
                            if t == 3 and not dot:
                                prepare_v(b + 1, 1 - q)
                            if t == 4 and not dot:
                                prepare_e(b + 1, 1 - q, first)

                prepare_x(0, 0, 0, True)
                prepare_x(0, 0, 1, True)
                if dot:
                    pe.wait_ge(S["t"], 2)
                    scores(0, 0)
                    scores(0, 1)
                else:
                    prepare_v(0, 0)
                    prepare_e(0, 0, True)
                phases(pe, unit)
                attend(B - 1, 1, NT - 1)

            @block.scalar
            def _(act):
                def copy_t(b, q, half):
                    act.wait_ge(S["t_ps"], 2 * b + half + 1)
                    act.activation(Tb[q][:, cols(half, HALF)], psV[0:D, :], ACT.Copy).then_inc(S["t"], 1)

                def copy_v(b, q):
                    act.wait_ge(S["v_ps"], b + 1)
                    act.activation(Hb[q][:, :, :], psV[:, :].rearrange("p (t f) -> p t f", f=D), ACT.Copy)\
                        .then_inc(S["v"], 1)

                def exps(b, q, t, early=False):
                    g = NT * b + t
                    r = t % 4
                    act.wait_ge(S["bias"], g + 1)
                    if dot:
                        act.activation(Z[:, r, :], Z[:, r, :], ACT.Exp, bias=nb[:, r, 0:1],
                                       accum_out=rs[q][:, t:t + 1]).then_inc(S["exps"], 1)
                        return
                    if not early:
                        act.wait_ge(S["joined"], g - 1)
                        apart(act, c)
                    act.activation(Z1[:, t % 2, :], Z[:, r, :], ACT.Exp, bias=nb[:, r, 0:1])
                    act.activation(Z2[:, t % 2, :], Z[:, r, :], ACT.Exp, bias=nb[:, r, 1:2], scale=0.2)\
                        .then_inc(S["exps"], 1)

                def exp_o(b):
                    act.wait_ge(S["o1"], b + 1)
                    act.activation(oe[:, :, :], o[:, :, :], ACT.Exp).then_inc(S["oexp"], 1)

                def unit(b, q, first=False, last=False):
                    for t in range(NT):
                        g = NT * b + t
                        ahead = t + AHEAD - 1
                        if ahead < NT:
                            exps(b, q, ahead)
                        elif not last:
                            exps(b + 1, 1 - q, ahead - NT)
                        act.wait_ge(S["transposed"], 2 * g + 1)
                        if not (first and t < 2):
                            act.wait_ge(S["o_ps"], g - 1)
                        act.activation(ET[:, t % 2, 0:4, :], psE[0][:, :].rearrange("p (j n) -> p j n", n=P), ACT.Copy)\
                            .then_inc(S["ev0"], 1)
                        if t in (1, 2) and not last:
                            copy_t(b + 1, 1 - q, t - 1)
                        if t == 3 and not last and not dot:
                            copy_v(b + 1, 1 - q)
                        if t == 1 and not first and not dot:
                            exp_o(b - 1)

                copy_t(0, 0, 0)
                copy_t(0, 0, 1)
                if not dot:
                    copy_v(0, 0)
                for t in range(AHEAD - 1):
                    exps(0, 0, t, early=True)
                phases(act, unit)
                if not dot:
                    exp_o(B - 1)

            @block.vector
            def _(dve):
                def copy_e1(b, q):
                    dve.wait_ge(S["e1_ps"], b + 1)
                    dve.tensor_copy(e1[q][:, :, 0], psV[:, 0:NT]).then_inc(S["e1"], 1)
                    dve.tensor_scalar(out=e1[q][:, :, 1], in0=psV[:, 0:NT], scalar1=0.2, scalar2=None, op0=ALU.mult)\
                        .then_inc(S["e1"], 1)

                def mask(b, q, t):
                    g = NT * b + t
                    r = slice(t % 4, t % 4 + 1)
                    if dot:
                        dve.wait_ge(S["scores"], g + 1)
                    elif t == 0:
                        dve.wait_ge(S["e2_ps"], b + 1)
                    apart(dve, c)
                    dve.tensor_tensor_reduce(out=Z[:, t % 4, :], in0=psS[t % 2 if dot else q][:, :],
                                             in1=neg[:, t, :], scale=1.0, scalar=LOWEST, op0=ALU.add, op1=ALU.max,
                                             accum_out=mx[:, r]).then_inc(S["masked"], 1)
                    if dot:
                        dve.wait_ge(S["masked"], g + 1)
                        dve.tensor_scalar(out=nb[:, t % 4, 0:1], in0=mx[:, r], scalar1=-1.0, scalar2=None, op0=ALU.mult)\
                            .then_inc(S["bias"], 1)

                def bias_1(b, q, t):
                    g = NT * b + t
                    r = slice(t % 4, t % 4 + 1)
                    dve.wait_ge(S["masked"], g + 1)
                    if t == 0:
                        dve.wait_ge(S["e1"], 2 * b + 2)
                        apart(dve, c)
                    dve.tensor_scalar(out=na[:, r], in0=mx[:, r], scalar1=e1[q][:, t, 0:1], scalar2=-1.0,
                                      op0=ALU.add, op1=ALU.mult).then_inc(S["na"], 1)

                def bias_2(b, q, t):
                    r = slice(t % 4, t % 4 + 1)
                    dve.wait_ge(S["na"], NT * b + t + 1)
                    dve.scalar_tensor_tensor(out=nm[:, r], in0=na[:, r], scalar=0.2, in1=na[:, r],
                                             op0=ALU.mult, op1=ALU.min).then_inc(S["nm"], 1)

                def bias_3(b, q, t):
                    dve.wait_ge(S["nm"], NT * b + t + 1)
                    dve.tensor_scalar(out=nb[:, t % 4, :], in0=e1[q][:, t, :], scalar1=nm[:, t % 4:t % 4 + 1],
                                      scalar2=None, op0=ALU.add).then_inc(S["bias"], 1)

                def join(b, q, t):
                    g = NT * b + t
                    dve.wait_ge(S["exps"], g + 1)
                    dve.scalar_tensor_tensor(out=Z[:, t % 4, :], in0=Z1[:, t % 2, :], scalar=1.0, in1=Z2[:, t % 2, :],
                                             op0=ALU.mult, op1=ALU.max,
                                             accum_out=rs[q][:, t:t + 1]).then_inc(S["joined"], 1)

                def normalise(b, q):
                    dve.wait_ge(weights_ready, NT * b + NT)
                    dve.reciprocal(ri[:, :], rs[q][:, :]).then_inc(S["rinv"], 1)
                    dve.wait_ge(S["rinv"], b + 1)
                    dve.wait_ge(S["o_ps"], NT * b + NT)
                    dve.tensor_tensor(out=o[:, :, :], in0=psO[:, :, :],
                                      in1=ri[:, :].unsqueeze(2).broadcast_to([P, NT, D]), op=ALU.mult)\
                        .then_inc(S["o1"], 1)

                def finish(b):
                    if dot:
                        dve.wait_ge(S["o1"], b + 1)
                        dve.tensor_tensor(out=oe[:, :, :], in0=o[:, :, :],
                                          in1=wts["bout"][:, :].unsqueeze(1).broadcast_to([P, NT, D]), op=ALU.add)\
                            .then_inc(S["o2"], 1)
                    else:
                        dve.wait_ge(S["oexp"], b + 1)
                        dve.tensor_scalar(out=oe[:, :, :], in0=oe[:, :, :], scalar1=1.0, scalar2=-1.0, op0=ALU.min,
                                          op1=ALU.add).then_inc(S["o2"], 1)
                    dve.wait_ge(S["o2"], b + 1)
                    dve.wait_ge(S["x"], b + FREE)
                    apart(dve, c)
                    if dot:
                        dve.scalar_tensor_tensor(out=o2[:, :, :], in0=oe[:, :, :], scalar=0.01, in1=oe[:, :, :],
                                                 op0=ALU.mult, op1=ALU.max).then_inc(S["o3"], 1)
                    else:
                        dve.scalar_tensor_tensor(out=o2[:, :, :], in0=o[:, :, :], scalar=0.0, in1=oe[:, :, :],
                                                 op0=ALU.max, op1=ALU.add).then_inc(S["o3"], 1)

                def later(b, q, t, ahead, last=False):
                    t = t + ahead
                    return (b, q, t) if t < NT else None if last else (b + 1, 1 - q, t - NT)

                def unit(b, q, first=False, last=False):
                    for t in range(NT):
                        g = NT * b + t
                        new, before, joining = (later(b, q, t, k, last) for k in (AHEAD, AHEAD - 1, 1))
                        if new:
                            mask(*new)
                        if not dot:
                            if before:
                                bias_3(*before)
                            if joining:
                                join(*joining)
                            if new:
                                bias_1(*new)
                        if t == 0 and not first:
                            normalise(b - 1, 1 - q)
                        dve.wait_ge(S["transposed"], 2 * g + 2)
                        if not (first and t < 2):
                            dve.wait_ge(S["o_ps"], g - 1)
                        dve.tensor_copy(ET[:, t % 2, 4:8, :], psE[1][:, :].rearrange("p (j n) -> p j n", n=P))\
                            .then_inc(S["ev1"], 1)
                        if not dot and new:
                            bias_2(*new)
                        if t == 4 and not last and not dot:
                            copy_e1(b + 1, 1 - q)
                        if t == 2 and not first:
                            finish(b - 1)

                if not dot:
                    copy_e1(0, 0)
                for t in range(AHEAD):
                    mask(0, 0, t)
                    if not dot:
                        bias_1(0, 0, t)
                        bias_2(0, 0, t)
                        if t < AHEAD - 1:
                            bias_3(0, 0, t)
                if not dot:
                    join(0, 0, 0)
                phases(dve, unit)
                normalise(B - 1, 1)
                finish(B - 1)


def layer1(nc, w, c, X):
    with ExitStack() as ctx:
        m = Mem(nc, ctx)
        H2 = m.sb("H2", [P, NT, B, D])
        bout = m.sb("bout", [P, D])
        with ExitStack() as inner:
            mi = Mem(nc, inner)
            st = dict(c, H2=H2, XT1=mi.sb("XT1", [P, B, N], F16), XT2=mi.sb("XT2", [P, B, N], F16),
                      XP=mi.sb("XP", [P, NT, B, 2 * D], F16), M12=mi.sb("M12", [P, HEADS, D], F16),
                      tab=mi.sb("tab", [P, HEADS, TAB]))
            l1_prepare(nc, w, c, X, st)
            l1_heads(nc, c, st)
        load(nc, [(bout[:, :], w["bout"].partition_broadcast(P))], "bout")
        attention(nc, c, X, "dot", H2, {"bout": bout})



def layer2(nc, w, c, X):
    STEPS, PAIRS = 3, B // 2
    with ExitStack() as ctx:
        m = Mem(nc, ctx)
        adjT = m.sb("adjT2", [P, NT, N])
        V = m.sb("V", [P, NT, B, D])
        VT = m.sb("VT", [P, PAIRS, N])
        W1a, W1b, W2 = (m.sb(k, [P, P]) for k in ("W1a", "W1b", "W2b"))
        b1, b2 = m.sb("b1", [P, 1]), m.sb("b2", [P, 1])
        b2r = m.sb("b2r", [P, 2, D])
        EF = m.sb("EF", [P, N])
        HT = m.sb("HT", [P, N])
        psE, psH, psT, psN = (m.ps(k, [P, N]) for k in ("psE2", "psH2", "psT2", "psN2"))
        zeroed, copied, loaded = m.sem("l2_zeroed"), m.sem("l2_copied"), m.sem("l2_loaded")
        adj_loaded = m.sem("l2_adj_loaded")
        S = {k: m.sem("l2_" + k) for k in ("vt0_ps", "vt0", "eff_ps", "eff", "h_ps", "h", "v_ps", "vt", "v")}
        with nc.Block() as block:

            @block.gpsimd
            def _(pool):
                for k in (W1a, W1b, W2):
                    pool.memset(k[:, :], 0.0).then_inc(zeroed, 1)

            @block.sync
            def _(sp):
                sp.dma_start(adjT[:, :, :], w["adjT"]).then_inc(adj_loaded, 16)
                sp.wait_ge(zeroed, 3)
                sp.wait_ge(copied, 1)
                n = 0
                for k in range(2):
                    blk = slice(k * D, k * D + D)
                    for dst, src in ((W1a[blk, blk], w["W1T"][0:D, :]), (W1b[blk, blk], w["W1T"][D:2 * D, :]),
                                     (W2[blk, blk], w["W2T"]), (b1[blk, :], w["b1"]), (b2[blk, :], w["b2"]),
                                     (b2r[:, k, :], w["b2row"].partition_broadcast(P))):
                        sp.dma_start(dst, src).then_inc(loaded, 16)
                        n += 1
                for b in range(B):
                    sp.dma_start(V[0:1, 0, b, :], w["iv"]).then_inc(loaded, 16)
                    n += 1
                assert n == 20

            @block.vector
            def _(dve):
                dve.sem_inc(S["v"], FREE)
                dve.tensor_copy(V[:, :, :, :], X[:, :, :, :]).then_inc(copied, 1)
                dve.wait_ge(loaded, 16 * 20)
                for p in range(PAIRS):
                    dve.wait_ge(S["vt0_ps"], p + 1)
                    dve.tensor_copy(VT[:, p, :], (psE, psH, psT, psN)[p][:, :]).then_inc(S["vt0"], 1)
                with dve.Fori(0, STEPS) as s:
                    for p in range(PAIRS):
                        i = PAIRS * s + p
                        dve.wait_ge(S["v_ps"], i + 1 + FREE)
                        dve.tensor_scalar(out=VT[:, p, :], in0=psT[:, :], scalar1=b2[:, 0:1], scalar2=None, op0=ALU.add)\
                            .then_inc(S["vt"], 1)
                        dve.tensor_tensor(out=V[:, :, 2 * p:2 * p + 2, :].rearrange("p t b f -> p t (b f)"),
                                          in0=psN[:, :].rearrange("p (t c) -> p t c", c=P),
                                          in1=b2r[:, :, :].rearrange("p b f -> p (b f)").unsqueeze(1)
                                          .broadcast_to([P, NT, P]), op=ALU.add).then_inc(S["v"], 1)
                dve.wait_ge(S["v"], STEPS * PAIRS + FREE)
                dve.tensor_tensor(out=X[:, :, :, :].rearrange("p t b f -> p (t b f)"),
                                  in0=X[:, :, :, :].rearrange("p t b f -> p (t b f)"),
                                  in1=V[:, :, :, :].rearrange("p t b f -> p (t b f)"), op=ALU.add).then_inc(copied, 1)

            @block.tensor
            def _(pe):
                pe.sem_inc(S["v_ps"], FREE)
                pe.wait_ge(loaded, 16 * 20)
                for p in range(PAIRS):
                    for t in range(NT):
                        last = pe.transpose((psE, psH, psT, psN)[p][:, cols(t)],
                                            V[:, t, 2 * p:2 * p + 2, :].rearrange("p b f -> p (b f)"), c["ident"][:, :])
                    last.then_inc(S["vt0_ps"], 1)
                pe.wait_ge(adj_loaded, 16)
                pe.wait_ge(S["vt0"], PAIRS)

                def effects(s, p):
                    i = PAIRS * s + p
                    pe.wait_ge(S["eff"], i + FREE)
                    for j in range(NT):
                        for hf in range(2):
                            last = pe.matmul(psE[:, cols(hf, HALF)],
                                             V[:, j, 2 * p:2 * p + 2, :].rearrange("p b f -> p (b f)"),
                                             adjT[:, j, cols(hf, HALF)], start=(j == 0), stop=(j == NT - 1))
                    last.then_inc(S["eff_ps"], 1)

                def update(s, p):
                    i = PAIRS * s + p
                    pe.wait_ge(S["eff"], i + 1 + FREE)
                    for hf in range(2):
                        pe.matmul(psH[:, cols(hf, HALF)], W1a[:, :], VT[:, p, cols(hf, HALF)], start=True, stop=False)
                        last = pe.matmul(psH[:, cols(hf, HALF)], W1b[:, :], EF[:, cols(hf, HALF)], start=False, stop=True)
                    last.then_inc(S["h_ps"], 1)

                def output(s, p):
                    i = PAIRS * s + p
                    pe.wait_ge(S["h"], i + 1)
                    pe.wait_ge(S["v"], i + FREE)
                    for hf in range(2):
                        pe.matmul(psT[:, cols(hf, HALF)], W2[:, :], HT[:, cols(hf, HALF)], start=True, stop=True)
                    for t in range(NT):
                        last = pe.matmul(psN[:, cols(t)], HT[:, cols(t)], W2[:, :], start=True, stop=True)
                    last.then_inc(S["v_ps"], 1)

                with pe.Fori(0, STEPS) as s:
                    pe.wait_ge(S["v"], PAIRS * s + FREE)
                    effects(s, 0)
                    for p in range(PAIRS):
                        update(s, p)
                        if p + 1 < PAIRS:
                            effects(s, p + 1)
                        output(s, p)

            @block.scalar
            def _(act):
                act.sem_inc(S["eff"], FREE)
                with act.Fori(0, STEPS) as s:
                    for p in range(PAIRS):
                        i = PAIRS * s + p
                        act.wait_ge(S["eff_ps"], i + 1)
                        act.activation(EF[:, :], psE[:, :], ACT.Copy).then_inc(S["eff"], 1)
                        act.wait_ge(S["h_ps"], i + 1)
                        act.wait_ge(S["v_ps"], i + FREE)
                        act.activation(HT[:, :], psH[:, :], ACT.Relu, bias=b1[:, 0:1]).then_inc(S["h"], 1)



def layer3(nc, w, c, X):
    with ExitStack() as ctx:
        m = Mem(nc, ctx)
        W3T, W3 = m.sb("W3T", [D, D]), m.sb("W3", [D, D])
        a3 = m.sb("a3", [D, 2])
        a3b = m.sb("a3b", [D, 2, P])
        A = [m.sb(f"A{k}", [D, P]) for k in range(2)]
        with ExitStack() as inner:
            mi = Mem(nc, inner)
            psA = mi.ps("psA3", [D, 2, P])
            loaded, ones, rep, a_ps, done = (mi.sem("l3_" + k) for k in ("loaded", "ones", "rep", "a_ps", "a"))
            with nc.Block() as block:

                @block.sync
                def _(sp):
                    for dst, src in ((W3T[:, :], w["W3T"]), (W3[:, :], w["W3"]), (a3[:, :], w["a3"])):
                        sp.dma_start(dst, src).then_inc(loaded, 16)

                @block.vector
                def _(dve):
                    dve.memset(a3b[:, :, :], 1.0).then_inc(ones, 1)
                    dve.wait_ge(ones, 1)
                    dve.wait_ge(loaded, 48)
                    for k in range(2):
                        dve.tensor_scalar(out=a3b[:, k, :], in0=a3b[:, k, :], scalar1=a3[:, k:k + 1], scalar2=None,
                                          op0=ALU.mult).then_inc(rep, 1)
                    dve.wait_ge(a_ps, 1)
                    for k in range(2):
                        dve.tensor_copy(A[k][:, :], psA[:, k, :]).then_inc(done, 1)

                @block.tensor
                def _(pe):
                    pe.wait_ge(rep, 2)
                    for k in range(2):
                        last = pe.matmul(psA[:, k, :], W3[:, :], a3b[:, k, :], start=True, stop=True)
                    last.then_inc(a_ps, 1)

        attention(nc, c, X, "add", X, {"W3T": W3T, "A": A})


LAYERS = {0: layer0, 1: layer1, 2: layer2, 3: layer3}


def build(nc, w, out, layers=(0, 1, 2, 3)):
    with ExitStack() as ctx:
        m = Mem(nc, ctx)
        X = m.sb("X", [P, NT, B, D])
        c = {"ident": m.sb("ident", [P, P]), "ident16": m.sb("ident16", [P, P], F16),
             "built": m.sem("ident_built"), "passed": m.sem("passed"),
             "neg": m.sb("neg", [P, NT, N], BF16)}
        make_constants(nc, c)
        load(nc, [(X[:, :, :, :], w["x"])], "x")
        for n in layers:
            LAYERS[n](nc, w, c, X)
            layer_norm(nc, X, f"_{n}")
        stored = m.sem("stored")
        with nc.Block() as block:

            @block.sync
            def _(sp):
                sp.dma_start(out, X[:, :, :, :]).then_inc(stored, 16)
                sp.wait_ge(stored, 16)


def host_layout(v):
    x, adj, H = v["x"], v["adj"], v["L0_gnn_H"]
    tiles = lambda a: a.reshape(NT, P, *a.shape[1:])
    return {
        "x": tiles(x.transpose(1, 0, 2)).transpose(1, 0, 2, 3),
        "xT": x.transpose(2, 0, 1),
        "adj": tiles(adj).transpose(1, 0, 2),
        "adjT": tiles(adj.T).transpose(1, 0, 2),
        "H": tiles(H).transpose(1, 0, 2),
        "HT": H.T,
        "W0": v["L0_gnn_W"], "W0T": v["L0_gnn_W"].T, "Wind": v["L0_gnn_W_ind"],
        "a_node": v["L0_gnn_a_node"][:, None], "a_gn": v["L0_gnn_a_gn"][:, None], "a_ge": v["L0_gnn_a_ge"][:, None],
        "fcW": v["L0_gnn_fcW"], "fcb": v["L0_gnn_fcb"][:, None], "av": v["L0_gnn_av"][:, None],
        "Wh": v["L1_gnn_Wh"].transpose(1, 0, 2),
        "WhT": v["L1_gnn_Wh"].transpose(2, 0, 1),
        "bh": v["L1_gnn_bh"].T,
        "Wout": v["L1_gnn_W_out"].reshape(HEADS, HID, D).transpose(1, 0, 2),
        "bout": v["L1_gnn_b_out"][None, :],
        "iv": v["L2_gnn_intervention_value"],
        "W1T": v["L2_gnn_W1"].T, "b1": v["L2_gnn_b1"][:, None],
        "W2T": v["L2_gnn_W2"].T, "b2": v["L2_gnn_b2"][:, None], "b2row": v["L2_gnn_b2"][None, :],
        "W3": v["L3_gnn_W"], "W3T": v["L3_gnn_W"].T, "a3": v["L3_gnn_a"].reshape(2, D).T,
    }


def kernel(**inputs):
    import concourse.bacc as bacc
    from concourse.bass_utils import run_bass_kernel_spmd

    nc = bacc.Bacc("TRN2", target_bir_lowering=False, num_devices=1)
    arrays, w = {}, {}
    for name, a in host_layout({k: np.asarray(v) for k, v in inputs.items()}).items():
        a = np.ascontiguousarray(a)
        arrays["in_" + name] = a
        w[name] = nc.dram_tensor("in_" + name, a.shape, mybir.dt.from_np(a.dtype), kind="ExternalInput").ap()
    out = nc.dram_tensor("out_x", [P, NT, B, D], F32, kind="ExternalOutput").ap()
    build(nc, w, out)
    r = run_bass_kernel_spmd(nc, [arrays], core_ids=[0])
    got = np.asarray(r.results[0]["out_x"])
    return np.ascontiguousarray(got.transpose(2, 1, 0, 3).reshape(B, N, D))
```

```python
from contextlib import ExitStack

import numpy as np

import concourse.bass as bass
from concourse import mybir

F32 = mybir.dt.float32
F16 = mybir.dt.float16
BF16 = mybir.dt.bfloat16
I32 = mybir.dt.int32
ACT = mybir.ActivationFunctionType
ALU = mybir.AluOpType
AX = mybir.AxisListType

P = 128
B, N, D = 8, 1024, 64
NT = N // P
HEADS, HID = 8, 128
E = 64
HALF = 512
NEG = -1.0e30
LOWEST = -3.0e38
SPLIT = 4096.0
LN_PEAK = 10.397207708
SUM_SCALE = 2.0 ** 24
EPS = 1e-5
FREE = 1


class Mem:

    def __init__(self, nc, ctx, tag=""):
        self.nc, self.ctx, self.tag, self.sems = nc, ctx, tag, []

    def sb(self, name, shape, dt=F32):
        return self.ctx.enter_context(self.nc.sbuf_tensor(self.tag + name, shape, dt))

    def ps(self, name, shape, dt=F32):
        return self.ctx.enter_context(self.nc.psum_tensor(self.tag + name, shape, dt))

    def sem(self, name):
        if not self.sems:
            self.ctx.callback(self.clear)
        self.sems.append(self.nc.alloc_semaphore(self.tag + name))
        return self.sems[-1]

    def clear(self):
        self.nc.clear_and_free_semaphores(self.sems)
        self.nc.all_engine_barrier()


def cols(i, width=P):
    return slice(i * width, (i + 1) * width)


def apart(eng, c):
    eng.sem_inc(c["passed"], 1)


def make_constants(nc, c):
    with ExitStack() as ctx:
        m = Mem(nc, ctx)
        zeroed = m.sem("ident_zeroed")
        built = c["built"]
        with nc.Block() as block:

            @block.gpsimd
            def _(pool):
                pool.memset(c["ident"][:, :], 0.0).then_inc(zeroed, 1)
                pool.wait_ge(zeroed, 1)
                pool.affine_select(out=c["ident"][:, :], in_=c["ident"][:, :], compare_op=ALU.not_equal, fill=1.0,
                                   base=0, pattern=[[-1, P]], channel_multiplier=1).then_inc(built, 1)
                pool.wait_ge(built, 1)
                pool.tensor_copy(c["ident16"][:, :], c["ident"][:, :]).then_inc(built, 1)
                pool.wait_ge(built, 2)


def layer_norm(nc, X, tag, pairs=(), out=None):
    CH = 4
    with ExitStack() as ctx:
        m = Mem(nc, ctx)
        G = NT * B // CH
        GD = G // 2
        sq = m.sb("sq" + tag, [P, CH, G, D])
        mean = m.sb("mean" + tag, [P, CH, G])
        var = m.sb("var" + tag, [P, CH, G])
        std = m.sb("std" + tag, [P, CH, G])
        S = {k: m.sem("ln_" + k + tag) for k in ("sum", "mean", "centred", "centred_pool", "squared", "square_sum",
                                                 "var", "std", "rstd", "done", "done_pool", "stored")}
        loaded = m.sem("ln_loaded" + tag)
        x = X[:, :, :, :].rearrange("p t b f -> p (t b) f")

        def wide(v, k, part):
            g = part.stop - part.start
            return v[:, k, part].unsqueeze(2).broadcast_to([P, g, D])

        def rows(k, part):
            return x[:, k * G + part.start:k * G + part.stop, :]

        DVE, POOL = slice(0, GD), slice(GD, G)
        with nc.Block() as block:

            @block.sync
            def _(sp):
                for dst, src in pairs:
                    sp.dma_start(dst, src).then_inc(loaded, 16)
                if pairs:
                    sp.wait_ge(loaded, 16 * len(pairs))
                if out is not None:
                    tiles = NT // CH
                    for k in range(CH):
                        sp.wait_ge(S["done"], k + 1)
                        sp.wait_ge(S["done_pool"], k + 1)
                        part = slice(k * tiles, k * tiles + tiles)
                        sp.dma_start(out[:, part, :, :], X[:, part, :, :]).then_inc(S["stored"], 16)
                    sp.wait_ge(S["stored"], 16 * CH)

            @block.vector
            def _(dve):
                def centre(k):
                    dve.tensor_reduce(out=std[:, k, :], in_=rows(k, slice(0, G)), axis=AX.X, op=ALU.add)\
                        .then_inc(S["sum"], 1)
                    dve.wait_ge(S["sum"], k + 1)
                    dve.tensor_scalar(out=mean[:, k, :], in0=std[:, k, :], scalar1=1.0 / D, scalar2=None,
                                      op0=ALU.mult).then_inc(S["mean"], 1)
                    dve.wait_ge(S["mean"], k + 1)
                    dve.tensor_tensor(out=rows(k, DVE), in0=rows(k, DVE), in1=wide(mean, k, DVE),
                                      op=ALU.subtract).then_inc(S["centred"], 1)

                def variance(k):
                    dve.wait_ge(S["squared"], k + 1)
                    dve.tensor_reduce(out=var[:, k, :], in_=sq[:, k, :, :], axis=AX.X, op=ALU.add)\
                        .then_inc(S["square_sum"], 1)
                    dve.wait_ge(S["square_sum"], k + 1)
                    dve.tensor_scalar(out=var[:, k, :], in0=var[:, k, :], scalar1=1.0 / D, scalar2=EPS,
                                      op0=ALU.mult, op1=ALU.add).then_inc(S["var"], 1)

                def invert(k):
                    dve.wait_ge(S["std"], k + 1)
                    dve.reciprocal(var[:, k, :], std[:, k, :]).then_inc(S["rstd"], 1)

                def scale(k):
                    dve.wait_ge(S["rstd"], k + 1)
                    dve.tensor_tensor(out=rows(k, DVE), in0=rows(k, DVE), in1=wide(var, k, DVE),
                                      op=ALU.mult).then_inc(S["done"], 1)

                for k in range(CH + 2):
                    if k < CH:
                        centre(k)
                    if k >= 2:
                        invert(k - 2)
                    if 1 <= k <= CH:
                        variance(k - 1)
                    if k >= 2:
                        scale(k - 2)
                dve.wait_ge(S["done"], CH)

            @block.gpsimd
            def _(pool):
                def centre(k):
                    pool.wait_ge(S["mean"], k + 1)
                    pool.tensor_tensor(out=rows(k, POOL), in0=rows(k, POOL), in1=wide(mean, k, POOL),
                                       op=ALU.subtract).then_inc(S["centred_pool"], 1)

                def scale(k):
                    pool.wait_ge(S["rstd"], k + 1)
                    pool.tensor_tensor(out=rows(k, POOL), in0=rows(k, POOL), in1=wide(var, k, POOL),
                                       op=ALU.mult).then_inc(S["done_pool"], 1)

                for k in range(CH + 2):
                    if k < CH:
                        centre(k)
                    if k >= 2:
                        scale(k - 2)
                pool.wait_ge(S["done_pool"], CH)

            @block.scalar
            def _(act):
                for k in range(CH + 1):
                    if k < CH:
                        act.wait_ge(S["centred"], k + 1)
                        act.wait_ge(S["centred_pool"], k + 1)
                        act.activation(sq[:, k, :, :], rows(k, slice(0, G)), ACT.Square).then_inc(S["squared"], 1)
                    if k:
                        act.wait_ge(S["var"], k)
                        act.activation(std[:, k - 1, :], var[:, k - 1, :], ACT.Sqrt).then_inc(S["std"], 1)



def l0_prepare(nc, w, X, st):
    LANES = 2
    with ExitStack() as ctx:
        m = Mem(nc, ctx)
        W2 = m.sb("W2", [D, 2 * D])
        WT2 = m.sb("WT2", [D, 2 * D])
        wvec = m.sb("wvec", [D, 3])
        ones = m.sb("ones0", [P, P])
        avec = m.sb("avec", [D, 2, P])
        Lnode = m.sb("Lnode", [D, P])
        Lgate = m.sb("Lgate", [D, P])
        hT_neg = m.sb("hT_neg", [P, N])
        h_neg = m.sb("h_neg", [P, NT, E])
        avb = m.sb("avb", [P, P])

        def lanes(name, shape):
            return [m.sb(f"{name}{l}", shape) for l in range(LANES)]

        xb_ = lanes("xT_batch", [D, N])
        lg_ = lanes("lg", [P, N])
        al_ = lanes("al", [P, N])
        alT_ = lanes("alT", [P, NT, E])
        hN_ = lanes("hN", [P, NT, 2 * D])
        small_ = lanes("small0", [P, 8])
        agT_ = lanes("agT", [P, 2, E])
        ex_ = lanes("ex", [P, E])
        he_ = lanes("he", [P, E])
        Tse_ = lanes("Tse", [P, E])
        cst_ = lanes("cst", [P, 2, NT])
        psN_ = [m.ps(f"psN{l}", [P, N]) for l in range(LANES)]
        psP_ = [m.ps(f"psP{l}", [P, N]) for l in range(LANES)]

        def each_lane(eng, steps, ahead=()):
            def pair(b, last=False):
                for step in steps:
                    if step in ahead and last:
                        continue
                    for l in range(LANES):
                        step(b + l + (LANES if step in ahead else 0), l)

            for step in ahead:
                for l in range(LANES):
                    step(l, l)
            with eng.Fori(0, B // LANES - 1) as i:
                pair(LANES * i)
            pair(B - LANES, last=True)

        loaded = m.sem("l0_loaded")
        xb_loaded = [m.sem(f"l0_xb_loaded{l}") for l in range(LANES)]
        pro = {k: m.sem("l0_" + k) for k in ("avec", "L_ps", "masks", "avb")}
        S = {k: m.sem("l0_" + k) for k in (
            "projected", "projected_n", "projected_c", "projected_g", "ht_copied", "slope", "lrelu",
            "h_copied", "masked", "nmax", "alpha_exp", "alpha_inv", "alpha", "alphaT_ps",
            "alphaT", "agg_ps", "agg", "agg_exp", "agg_relu", "he", "edge_ps", "q", "Tse", "beta_t", "beta32",
            "beta_hi", "beta", "se_ps", "c_lg", "c_max", "c_sub", "c_exp", "c_sum", "c_inv", "c_inv2", "c_ready",
            "cT_ps", "cT_hi", "batch")}
        with nc.Block() as block:

            @block.sync
            def _(sp):
                n = 0
                for dst, src in ((W2[:, 0:D], w["W0"]), (W2[:, D:2 * D], w["W0"]),
                                 (WT2[:, 0:D], w["W0T"]), (WT2[:, D:2 * D], w["W0T"]),
                                 (wvec[:, 0:1], w["a_node"]), (wvec[:, 1:2], w["a_gn"]), (wvec[:, 2:3], w["a_ge"]),
                                 (hT_neg[0:E, :], w["HT"]), (hT_neg[E:P, :], w["HT"]),
                                 (h_neg[:, :, :], w["H"]), (st["fcW"][:, :], w["fcW"]), (st["fcb"][:, :], w["fcb"]),
                                 (st["av"][:, 0:1], w["av"])):
                    sp.dma_start(dst, src).then_inc(loaded, 16)
                    n += 1
                assert n == 13

                def load_x(b, l):
                    sp.wait_ge(S["projected_g"], b + 1)
                    sp.dma_start(xb_[l][:, :], w["xT"][:, bass.ds(b, 1), :].squeeze(1))\
                        .then_inc(xb_loaded[l], 16)

                each_lane(sp, [load_x])

            @block.vector
            def _(dve):
                dve.sem_inc(S["batch"], LANES)
                dve.memset(ones[:, :], 1.0).then_inc(pro["avb"], 1)
                dve.wait_ge(loaded, 16 * 13)
                dve.wait_ge(pro["avb"], 1)
                dve.tensor_scalar(out=avec[:, 0, :], in0=ones[0:D, :], scalar1=wvec[:, 0:1], scalar2=None,
                                  op0=ALU.mult).then_inc(pro["avec"], 1)
                dve.tensor_scalar(out=avec[:, 1, :], in0=ones[0:D, :], scalar1=wvec[:, 1:2], scalar2=None,
                                  op0=ALU.mult).then_inc(pro["avec"], 1)
                dve.tensor_scalar(out=avb[:, :], in0=ones[:, :], scalar1=st["av"][:, 0:1], scalar2=None,
                                  op0=ALU.mult).then_inc(pro["avb"], 1)
                dve.tensor_scalar(out=hT_neg[:, :], in0=hT_neg[:, :], scalar1=0.0, scalar2=NEG,
                                  op0=ALU.is_le, op1=ALU.mult).then_inc(pro["masks"], 1)
                dve.tensor_scalar(out=h_neg[:, :, :], in0=h_neg[:, :, :], scalar1=0.0, scalar2=NEG,
                                  op0=ALU.is_le, op1=ALU.mult).then_inc(pro["masks"], 1)
                dve.wait_ge(pro["L_ps"], 1)
                dve.tensor_copy(Lnode[:, :], psN_[0][0:D, 0:P]).then_inc(pro["masks"], 1)
                dve.tensor_copy(Lgate[:, :], psN_[0][0:D, P:2 * P]).then_inc(pro["masks"], 1)
                dve.wait_ge(pro["masks"], 4)

                def mask_nodes(b, l):
                    dve.wait_ge(S["slope"], b + 1)
                    dve.tensor_tensor(out=lg_[l][:, :], in0=psN_[l][:, :], in1=lg_[l][:, :], op=ALU.max)\
                        .then_inc(S["lrelu"], 1)
                    dve.wait_ge(S["lrelu"], b + 1)
                    apart(dve, st)
                    dve.tensor_tensor_reduce(out=al_[l][:, :], in0=lg_[l][:, :], in1=hT_neg[:, :], scale=1.0,
                                             scalar=LOWEST, op0=ALU.add, op1=ALU.max, accum_out=small_[l][:, 0:1])\
                        .then_inc(S["masked"], 1)
                    dve.wait_ge(S["masked"], b + 1)
                    dve.tensor_scalar(out=small_[l][:, 1:2], in0=small_[l][:, 0:1], scalar1=-1.0, scalar2=None,
                                      op0=ALU.mult).then_inc(S["nmax"], 1)

                def alpha(b, l):
                    dve.wait_ge(S["alpha_exp"], b + 1)
                    dve.reciprocal(small_[l][:, 3:4], small_[l][:, 2:3]).then_inc(S["alpha_inv"], 1)
                    dve.wait_ge(S["alpha_inv"], b + 1)
                    dve.tensor_scalar(out=al_[l][:, :], in0=al_[l][:, :], scalar1=small_[l][:, 3:4], scalar2=None,
                                      op0=ALU.mult).then_inc(S["alpha"], 1)

                def agg(b, l):
                    dve.wait_ge(S["agg_ps"], b + 1)
                    dve.tensor_copy(agT_[l][:, 0, :], psN_[l][:, HALF:HALF + E]).then_inc(S["agg"], 1)
                    dve.tensor_copy(agT_[l][:, 1, :], psN_[l][:, HALF:HALF + E]).then_inc(S["agg"], 1)
                    pairs = psN_[l][:, HALF:HALF + E].rearrange("p (j i) -> p j i", i=2)
                    dve.tensor_copy(st["aggP"][0:D, bass.ds(b, 1), :], pairs[0:D, :, 0].unsqueeze(1))\
                        .then_inc(S["agg"], 1)
                    dve.tensor_copy(st["aggP"][D:P, bass.ds(b, 1), :], pairs[D:P, :, 1].unsqueeze(1))\
                        .then_inc(S["agg"], 1)

                def edge_elu(b, l):
                    dve.wait_ge(S["agg"], 4 * b + 4)
                    dve.tensor_scalar(out=he_[l][:, :], in0=agT_[l][:, 0, :], scalar1=0.0, scalar2=None,
                                      op0=ALU.max).then_inc(S["agg_relu"], 1)
                    dve.wait_ge(S["agg_relu"], b + 1)
                    dve.wait_ge(S["agg_exp"], b + 1)
                    dve.scalar_tensor_tensor(out=he_[l][:, :], in0=ex_[l][:, :], scalar=-1.0, in1=he_[l][:, :],
                                             op0=ALU.add, op1=ALU.min).then_inc(S["he"], 1)

                def beta(b, l):
                    dve.wait_ge(S["beta_t"], b + 1 + LANES)
                    dve.tensor_scalar(out=al_[l][:, :], in0=al_[l][:, :], scalar1=SPLIT / 2, scalar2=SPLIT / 2,
                                      op0=ALU.mult, op1=ALU.add).then_inc(S["beta32"], 1)
                    dve.wait_ge(S["beta32"], b + 1)
                    bs = st["BS"][:, bass.ds(b, 1), :].squeeze(1)
                    dve.tensor_copy(bs, al_[l][:, :]).then_inc(S["beta_hi"], 1)
                    dve.wait_ge(S["beta_hi"], b + 1)
                    bs_lo = st["BS"][E:P, bass.ds(b, 1), :].squeeze(1)
                    dve.tensor_tensor(out=bs_lo, in0=al_[l][E:P, :], in1=bs_lo, op=ALU.subtract).then_inc(S["beta"], 1)

                def coef_logits(b, l):
                    dve.wait_ge(S["se_ps"], b + 1)
                    dve.tensor_tensor(out=alT_[l][:, :, :], in0=h_neg[:, :, :],
                                      in1=psN_[l][:, 0:E].unsqueeze(1).broadcast_to([P, NT, E]),
                                      op=ALU.add).then_inc(S["c_lg"], 1)
                    dve.wait_ge(S["c_lg"], b + 1)
                    dve.tensor_reduce(out=cst_[l][:, 0, :], in_=alT_[l][:, :, :], axis=AX.X, op=ALU.max)\
                        .then_inc(S["c_max"], 1)
                    dve.wait_ge(S["c_max"], b + 1)
                    dve.tensor_tensor(out=alT_[l][:, :, :], in0=alT_[l][:, :, :],
                                      in1=cst_[l][:, 0, :].unsqueeze(2).broadcast_to([P, NT, E]),
                                      op=ALU.subtract).then_inc(S["c_sub"], 1)

                def coef_scale(b, l):
                    dve.wait_ge(S["c_exp"], b + 1)
                    dve.tensor_reduce(out=cst_[l][:, 0, :], in_=alT_[l][:, :, :], axis=AX.X, op=ALU.add)\
                        .then_inc(S["c_sum"], 1)
                    dve.wait_ge(S["c_sum"], b + 1)
                    dve.reciprocal(cst_[l][:, 1, :], cst_[l][:, 0, :]).then_inc(S["c_inv"], 1)
                    dve.wait_ge(S["c_inv"], b + 1)
                    dve.tensor_scalar(out=cst_[l][:, 1, :], in0=cst_[l][:, 1, :], scalar1=SPLIT, scalar2=None,
                                      op0=ALU.mult).then_inc(S["c_inv2"], 1)
                    dve.wait_ge(S["c_inv2"], b + 1)
                    twice = lg_[l][:, :].rearrange("p (t k e) -> p t k e", k=2, e=E)
                    for k in range(2):
                        dve.tensor_tensor(out=twice[:, :, k, :], in0=alT_[l][:, :, :],
                                          in1=cst_[l][:, 1, :].unsqueeze(2).broadcast_to([P, NT, E]),
                                          op=ALU.mult).then_inc(S["c_ready"], 1)

                def coef_low(b, l):
                    dve.wait_ge(S["cT_hi"], b + 1)
                    cs_lo = st["CS"][E:P, bass.ds(b, 1), :].squeeze(1)
                    dve.tensor_tensor(out=cs_lo, in0=psN_[l][E:P, :], in1=cs_lo, op=ALU.subtract).then_inc(S["batch"], 1)

                each_lane(dve, [mask_nodes, alpha, agg, edge_elu, beta, coef_logits, coef_scale, coef_low])

            @block.scalar
            def _(act):
                act.sem_inc(S["beta_t"], LANES)

                def slope(b, l):
                    act.wait_ge(S["projected_n"], b + 1)
                    act.activation(lg_[l][:, :], psN_[l][:, :], ACT.Copy, scale=0.2).then_inc(S["slope"], 1)

                def copy_ht(b, l):
                    act.wait_ge(S["projected"], b + 1)
                    act.activation(st["hT"][:, bass.ds(b, 1), :].squeeze(1), psP_[l][:, :], ACT.Copy)\
                        .then_inc(S["ht_copied"], 1)

                def copy_h(b, l):
                    act.wait_ge(S["projected_c"], b + 1)
                    act.activation(hN_[l][:, :, :], psP_[l][:, :].rearrange("p (t f) -> p t f", f=2 * D), ACT.Copy)\
                        .then_inc(S["h_copied"], 1)

                def alpha(b, l):
                    act.wait_ge(S["nmax"], b + 1)
                    act.activation(al_[l][:, :], al_[l][:, :], ACT.Exp, bias=small_[l][:, 1:2],
                                   accum_out=small_[l][:, 2:3])\
                        .then_inc(S["alpha_exp"], 1)

                def copy_alpha(b, l):
                    act.wait_ge(S["alphaT_ps"], b + 1)
                    act.activation(alT_[l][:, :, :], psN_[l][:, 0:HALF].rearrange("p (t e) -> p t e", e=E), ACT.Copy)\
                        .then_inc(S["alphaT"], 1)

                def edge_exp(b, l):
                    act.wait_ge(S["agg"], 4 * b + 4)
                    act.activation(ex_[l][:, :], agT_[l][:, 0, :], ACT.Exp).then_inc(S["agg_exp"], 1)

                def edge_tanh(b, l):
                    act.wait_ge(S["edge_ps"], b + 1)
                    act.activation(small_[l][:, 4:5], psN_[l][:, 0:1], ACT.Copy, scale=0.5).then_inc(S["q"], 1)
                    act.activation(Tse_[l][:, :], psN_[l][:, E:2 * E], ACT.Tanh, bias=st["fcb"][:, 0:1])\
                        .then_inc(S["Tse"], 1)

                def beta(b, l):
                    act.wait_ge(S["q"], b + 1)
                    act.wait_ge(S["projected_g"], b + 1 + LANES)
                    act.activation(al_[l][:, :], psP_[l][:, :], ACT.Tanh, bias=small_[l][:, 4:5], scale=0.5)\
                        .then_inc(S["beta_t"], 1)

                def coef_exp(b, l):
                    act.wait_ge(S["c_sub"], b + 1)
                    act.activation(alT_[l][:, :, :], alT_[l][:, :, :], ACT.Exp).then_inc(S["c_exp"], 1)

                def coef_high(b, l):
                    act.wait_ge(S["cT_ps"], b + 1)
                    act.activation(st["CS"][:, bass.ds(b, 1), :].squeeze(1), psN_[l][:, :], ACT.Copy)\
                        .then_inc(S["cT_hi"], 1)

                each_lane(act, [slope, alpha, copy_alpha, edge_exp, edge_tanh, beta, copy_ht, coef_exp, copy_h, coef_high],
                          ahead=(copy_ht, copy_h))

            @block.tensor
            def _(pe):
                pe.sem_inc(S["projected_g"], LANES)
                ident = st["ident"]
                pe.wait_ge(pro["avec"], 2)
                for k in range(2):
                    last = pe.matmul(psN_[0][0:D, cols(k)], WT2[:, 0:D], avec[:, k, :], start=True, stop=True)
                last.then_inc(pro["L_ps"], 1)
                pe.wait_ge(pro["masks"], 4)
                pe.wait_ge(pro["avb"], 2)

                def project_nodes(b, l):
                    pe.wait_ge(S["batch"], b + 1)
                    for hf in range(2):
                        last = pe.matmul(psN_[l][:, cols(hf, HALF)], Lnode[:, :], xb_[l][:, cols(hf, HALF)],
                                         start=True, stop=True)
                    last.then_inc(S["projected_n"], 1)

                def project_ht(b, l):
                    pe.wait_ge(S["beta_t"], b + 1)
                    pe.wait_ge(xb_loaded[l], 8 * (b - l) + 16)
                    for hf in range(2):
                        last = pe.matmul(psP_[l][:, cols(hf, HALF)], W2[:, :], xb_[l][:, cols(hf, HALF)],
                                         start=True, stop=True)
                    last.then_inc(S["projected"], 1)

                def project_h(b, l):
                    pe.wait_ge(S["ht_copied"], b + 1)
                    for t in range(NT):
                        last = pe.matmul(psP_[l][:, cols(t)], xb_[l][:, cols(t)], W2[:, :], start=True, stop=True)
                    last.then_inc(S["projected_c"], 1)

                def project_gate(b, l):
                    pe.wait_ge(S["h_copied"], b + 1)
                    for hf in range(2):
                        last = pe.matmul(psP_[l][:, cols(hf, HALF)], Lgate[:, :], xb_[l][:, cols(hf, HALF)],
                                         start=True, stop=True)
                    last.then_inc(S["projected_g"], 1)

                def alpha(b, l):
                    pe.wait_ge(S["alpha"], b + 1)
                    apart(pe, st)
                    for t in range(NT):
                        last = pe.transpose(psN_[l][:, cols(t, E)], al_[l][0:E, cols(t)], ident[0:E, 0:E])
                    last.then_inc(S["alphaT_ps"], 1)

                def agg(b, l):
                    pe.wait_ge(S["alphaT"], b + 1)
                    for t in range(NT):
                        last = pe.matmul(psN_[l][:, HALF:HALF + E], hN_[l][:, t, :], alT_[l][:, t, :],
                                         start=(t == 0), stop=(t == NT - 1))
                    last.then_inc(S["agg_ps"], 1)

                def edge(b, l):
                    pe.wait_ge(S["he"], b + 1)
                    pe.matmul(psN_[l][:, 0:1], agT_[l][0:D, :, :], wvec[:, 2:3], start=True, stop=True)
                    pe.matmul(psN_[l][:, E:2 * E], st["fcW"][:, :], he_[l][0:D, :], start=True, stop=True)\
                        .then_inc(S["edge_ps"], 1)

                def edge_score(b, l):
                    pe.wait_ge(S["Tse"], b + 1)
                    pe.matmul(psN_[l][:, 0:E], avb[:, :], Tse_[l][:, :], start=True, stop=True).then_inc(S["se_ps"], 1)

                def coefs(b, l):
                    pe.wait_ge(S["c_ready"], 2 * b + 2)
                    for t in range(NT):
                        last = pe.transpose(psN_[l][:, cols(t)], lg_[l][:, cols(t)], ident[:, :])
                    last.then_inc(S["cT_ps"], 1)

                each_lane(pe, [project_nodes, project_gate, alpha, agg, edge, edge_score, project_ht, project_h, coefs],
                          ahead=(project_ht, project_h))


def l0_industry(nc, w, st, adjT, IND):
    PARTS = 4
    with ExitStack() as ctx:
        m = Mem(nc, ctx)
        xT = m.sb("xTi", [D, B, N])
        Wi = m.sb("Wi", [D, D])
        Y = m.sb("Yi", [P, NT, B, D])
        adj = m.sb("adjn", [P, 2, N])
        deg = m.sb("deg", [P, NT])
        rdeg = m.sb("rdeg", [P, NT])
        psY = [m.ps(f"psY{i}", [P, NT, D]) for i in range(2)]
        psI = [m.ps(f"psI{i}", [P, B, D]) for i in range(2)]
        w_loaded, x_loaded = m.sem("ind_w_loaded"), [m.sem(f"ind_x_loaded{k}") for k in range(PARTS)]
        adj_loaded = [m.sem("adjrow_loaded0"), m.sem("adjrow_loaded1")]
        adjT_loaded = m.sem("adjT_loaded")
        y_ps, y_ready, ind_ps, ind_ready = (m.sem("ind_" + k) for k in ("y_ps", "y", "ps", "ready"))
        deg_part, deg_ready = m.sem("deg_part"), m.sem("deg_ready")
        with nc.Block() as block:

            @block.sync
            def _(sp):
                sp.dma_start(Wi[:, :], w["Wind"]).then_inc(w_loaded, 16)
                for k in range(PARTS):
                    sp.dma_start(xT[:, cols(k, B // PARTS), :], w["xT"][:, cols(k, B // PARTS), :])\
                        .then_inc(x_loaded[k], 16)
                sp.dma_start(adjT[:, :, :], w["adjT"]).then_inc(adjT_loaded, 16)
                for t in range(NT):
                    if t >= 2:
                        sp.wait_ge(deg_part, 2 * t - 2)
                    sp.dma_start(adj[:, t % 2, :], w["adj"][:, t, :]).then_inc(adj_loaded[t % 2], 16)

            @block.vector
            def _(dve):
                for t in range(NT):
                    dve.wait_ge(adj_loaded[t % 2], 16 * (t // 2 + 1))
                    dve.tensor_scalar(out=st["neg"][:, t, :], in0=adj[:, t % 2, :], scalar1=0.0, scalar2=NEG,
                                      op0=ALU.is_equal, op1=ALU.mult).then_inc(deg_part, 1)
                    dve.tensor_reduce(out=deg[:, t:t + 1], in_=adj[:, t % 2, :], axis=AX.X, op=ALU.add)\
                        .then_inc(deg_part, 1)
                dve.wait_ge(deg_part, 2 * NT)
                dve.tensor_scalar(out=deg[:, :], in0=deg[:, :], scalar1=1.0, scalar2=None, op0=ALU.max)\
                    .then_inc(deg_part, 1)
                dve.wait_ge(deg_part, 2 * NT + 1)
                dve.reciprocal(rdeg[:, :], deg[:, :]).then_inc(deg_ready, 1)

            @block.tensor
            def _(pe):
                pe.wait_ge(w_loaded, 16)
                for b in range(B):
                    if b % (B // PARTS) == 0:
                        pe.wait_ge(x_loaded[b * PARTS // B], 16)
                    if b >= 2:
                        pe.wait_ge(y_ready, b - 1)
                    for t in range(NT):
                        last = pe.matmul(psY[b % 2][:, t, :], xT[:, b, cols(t)], Wi[:, :], start=True, stop=True)
                    last.then_inc(y_ps, 1)
                pe.wait_ge(adjT_loaded, 16)
                pe.wait_ge(y_ready, B)
                for t in range(NT):
                    if t >= 2:
                        pe.wait_ge(ind_ready, t - 1)
                    for j in range(NT):
                        last = pe.matmul(psI[t % 2][:, :, :], adjT[:, j, cols(t)], Y[:, j, :, :],
                                         start=(j == 0), stop=(j == NT - 1))
                    last.then_inc(ind_ps, 1)

            @block.scalar
            def _(act):
                for b in range(B):
                    act.wait_ge(y_ps, b + 1)
                    act.activation(Y[:, :, b, :], psY[b % 2][:, :, :], ACT.Copy).then_inc(y_ready, 1)
                act.wait_ge(deg_ready, 1)
                for t in range(NT):
                    act.wait_ge(ind_ps, t + 1)
                    act.activation(IND[:, t, :, :], psI[t % 2][:, :, :], ACT.Copy, scale=rdeg[:, t:t + 1])\
                        .then_inc(ind_ready, 1)


def l0_edges(nc, st, gT, y):
    J = E // 2
    RING = 4
    G = J // RING
    with ExitStack() as ctx:
        m = Mem(nc, ctx)
        SEL = m.sb("SEL", [P, E, D], F16)
        SUM = m.sb("SUM", [P, D])
        v = m.sb("v", [P, RING, N])
        ex = m.sb("exv", [P, RING, N])
        cc = m.sb("cc", [P, RING - 1, N])
        psB = [m.ps(f"psB{i}", [P, N]) for i in range(2)]
        psC = m.ps("psCe", [P, N])
        psA = m.ps("psA", [D, N])
        sel = m.sem("sel_step")
        S = {k: m.sem("edge_" + k) for k in ("beta", "coef", "c_copied", "v", "exp", "relu", "elu", "y_dve", "y_pool",
                                             "summed", "g")}

        def place(b, g, k):
            if not isinstance(g, int):
                return b, RING * g + k, RING // 2 * g + k // 2
            j = RING * g + k
            if j < 0:
                b, j = b - 1, j + J
            elif j >= J:
                b, j = b + 1, j - J
            return b, j, j // 2

        def count(b, g, k):
            b, j, _ = place(b, g, k)
            return J * b + j + 1

        def weighed(b, g, k):
            if not isinstance(g, int):
                b, g, k = b, g + k // RING, k % RING
            else:
                b, g, k = b + (RING * g + k) // J, (g + k // RING) % G, k % RING
            if k == 0:
                return S["y_dve"], G * b + g + 1
            return S["y_pool"], (RING - 1) * (G * b + g) + k

        def phases(eng, step):
            def batch(b, first=False, last=False):
                for k in range(RING):
                    step(b, 0, k, k if first else RING)
                with eng.Fori(1, G - 1) as g:
                    for k in range(RING):
                        step(b, g, k, RING)
                for k in range(RING):
                    step(b, G - 1, k, RING, last=last)

            batch(0, first=True)
            with eng.Fori(1, B - 1) as b:
                batch(b)
            batch(B - 1, last=True)

        with nc.Block() as block:

            @block.gpsimd
            def _(pool):
                pool.memset(SEL[:, :, :], 0.0).then_inc(sel, 1)
                pool.memset(SUM[:, :], 0.0).then_inc(sel, 1)
                pool.wait_ge(sel, 2)
                for k in range(2):
                    pool.affine_select(out=SEL[:, :, :], in_=SEL[:, :, :], compare_op=ALU.not_equal, fill=1.0 / SPLIT,
                                       base=-E * k, pattern=[[-1, E], [0, D]], channel_multiplier=1).then_inc(sel, 1)
                    pool.affine_select(out=SUM[:, :], in_=SUM[:, :], compare_op=ALU.not_equal, fill=1.0,
                                       base=-D * k, pattern=[[-1, D]], channel_multiplier=1).then_inc(sel, 1)
                    pool.wait_ge(sel, 4 + 2 * k)

                def weigh(g, k, first=False):
                    pool.wait_ge(S["elu"], RING * g + k + 1)
                    pool.wait_ge(S["c_copied"], (RING - 1) * g + k)
                    if not first:
                        pool.wait_ge(S["summed"], RING * (g - 1) + k + 1)
                    pool.tensor_tensor(out=y[:, k, :], in0=ex[:, k, :], in1=cc[:, k - 1, :], op=ALU.mult)\
                        .then_inc(S["y_pool"], 1)

                for k in range(1, RING):
                    weigh(0, k, True)
                with pool.Fori(1, B * G) as g:
                    for k in range(1, RING):
                        weigh(g, k)

            @block.tensor
            def _(pe):
                pe.wait_ge(sel, 6)

                def gates(b, g, k):
                    b, j, _ = place(b, g, k)
                    for hf in range(2):
                        last = pe.matmul(psB[k % 2][:, cols(hf, HALF)], SEL[:, bass.ds(2 * j, 2), :],
                                         st["BS"][:, b, cols(hf, HALF)], start=True, stop=True)
                    last.then_inc(S["beta"], 1)

                def coefs(b, g, k):
                    b, j, _ = place(b, g, k)
                    for hf in range(2):
                        last = pe.matmul(psC[:, cols(hf, HALF)], SEL[:, bass.ds(2 * j, 2), :],
                                         st["CS"][:, b, cols(hf, HALF)], start=True, stop=True)
                    last.then_inc(S["coef"], 1)

                def add_up(b, g, k):
                    _, j, _ = place(b, g, k)
                    pe.wait_ge(*weighed(b, g, k))
                    first, final = (isinstance(j, int) and j == x for x in (0, J - 1))
                    for hf in range(2):
                        last = pe.matmul(psA[:, cols(hf, HALF)], SUM[:, :], y[:, k % RING, cols(hf, HALF)],
                                         start=first, stop=final)
                    last.then_inc(S["summed"], 1)

                def step(b, g, k, s, last=False):
                    if not (last and k >= 1):
                        pe.wait_ge(S["v"], count(b, g, k + 1))
                        gates(b, g, k + 3)
                    if k == 1:
                        pe.wait_ge(*weighed(b, g, 0))
                    elif s > 0:
                        pe.wait_ge(S["c_copied"], weighed(b, g, k - 1)[1])
                    coefs(b, g, k)
                    if s >= 3:
                        if isinstance(g, int) and g == 0 and k == 3 and s == RING:
                            pe.wait_ge(S["g"], b)
                        add_up(b, g, k - 3)

                gates(0, 0, 0)
                gates(0, 0, 1)
                pe.wait_ge(S["v"], 1)
                gates(0, 0, 2)
                phases(pe, step)
                for k in (1, 2, 3):
                    add_up(B - 1, G - 1, k)

            @block.vector
            def _(dve):
                def gate(b, g, k, early=False):
                    dve.wait_ge(S["beta"], count(b, g, k))
                    if not early:
                        dve.wait_ge(S["elu"], count(b, g, k - RING))
                    b, j, _ = place(b, g, k)
                    dve.scalar_tensor_tensor(out=v[:, k % RING, :], in0=st["hT"][:, b, :],
                                             scalar=st["aggP"][:, b, bass.ds(j, 1)], in1=psB[k % 2][:, :],
                                             op0=ALU.subtract, op1=ALU.mult).then_inc(S["v"], 1)

                def elu(b, g, k):
                    dve.wait_ge(S["relu"], count(b, g, k))
                    dve.scalar_tensor_tensor(out=ex[:, k, :], in0=ex[:, k, :], scalar=-1.0, in1=v[:, k, :],
                                             op0=ALU.add, op1=ALU.min).then_inc(S["elu"], 1)

                def weigh(b, g, k, s):
                    dve.wait_ge(S["elu"], count(b, g, k))
                    dve.wait_ge(S["coef"], count(b, g, k))
                    if s >= RING:
                        dve.wait_ge(S["summed"], count(b, g, k - RING))
                    dve.tensor_tensor(out=y[:, k, :], in0=ex[:, k, :], in1=psC[:, :], op=ALU.mult)\
                        .then_inc(S["y_dve"], 1)

                def step(b, g, k, s, last=False):
                    if k == 1:
                        weigh(b, g, 0, s)
                    if not (last and k >= 2):
                        gate(b, g, k + 2, early=s < 2)
                    elu(b, g, k)

                gate(0, 0, 0, True)
                gate(0, 0, 1, True)
                phases(dve, step)

            @block.scalar
            def _(act):
                def exps(b, g, k, early=False):
                    act.wait_ge(S["v"], count(b, g, k))
                    if not early:
                        act.wait_ge(*weighed(b, g, k - RING))
                    bb, j, _ = place(b, g, k)
                    agg = st["aggP"][:, bb, bass.ds(j, 1)]
                    act.activation(ex[:, k % RING, :], v[:, k % RING, :], ACT.Exp, bias=agg).then_inc(S["exp"], 1)
                    act.activation(v[:, k % RING, :], v[:, k % RING, :], ACT.Relu, bias=agg).then_inc(S["relu"], 1)

                def copy_sum(b):
                    act.wait_ge(S["summed"], J * b + J)
                    apart(act, st)
                    act.activation(gT[:, bass.ds(b, 1), :].squeeze(1), psA[:, :], ACT.Copy).then_inc(S["g"], 1)

                def copy_coefs(b, g, k):
                    act.wait_ge(S["coef"], count(b, g, k))
                    act.activation(cc[:, k % RING - 1, :], psC[:, :], ACT.Copy).then_inc(S["c_copied"], 1)

                def step(b, g, k, s, last=False):
                    if k != 1 and s > 0:
                        copy_coefs(b, g, k - 1)
                    if not (last and k == 3):
                        exps(b, g, k + 1, early=s < 3)
                    if isinstance(g, int) and g == 0 and k == 2 and s == RING:
                        copy_sum(b - 1)

                exps(0, 0, 0, early=True)
                phases(act, step)
                copy_coefs(B - 1, G - 1, 3)
                copy_sum(B - 1)


def l0_combine(nc, w, st, X, IND, gT):
    LANES = 2
    with ExitStack() as ctx:
        m = Mem(nc, ctx)

        def lanes(name, shape):
            return [m.sb(f"{name}{l}", shape) for l in range(LANES)]

        indb = lanes("indb", [P, NT, D])
        gb = lanes("gb", [D, N])
        indT = lanes("indT", [D, N])
        T1 = lanes("T1", [P, N])
        T2 = lanes("T2", [P, N])
        gN = lanes("gN", [P, NT, D])
        d = lanes("dmix", [P, NT, D])
        wt = lanes("wt", [P, NT])
        psF = [m.ps(f"psF{l}", [P, N]) for l in range(LANES)]
        psGn = [m.ps(f"psGn{l}", [P, NT, D]) for l in range(LANES)]
        psD = [m.ps(f"psD{l}", [P, NT]) for l in range(LANES)]
        S = {k: m.sem("comb_" + k) for k in ("ind", "g", "tr", "indT", "fc1", "fc2", "tanh1", "tanh2", "t", "diff", "w", "w1",
                                             "gN", "d", "d2", "d3", "x")}

        def each_lane(eng, steps):
            with eng.Fori(0, B // LANES) as i:
                for step in steps:
                    for l in range(LANES):
                        step(LANES * i + l, l)

        x_loaded = m.sem("comb_x_loaded")
        with nc.Block() as block:

            @block.sync
            def _(sp):
                sp.dma_start(X[:, :, :, :], w["x"]).then_inc(x_loaded, 16)

            @block.tensor
            def _(pe):
                def fc(l, src):
                    for hf in range(2):
                        last = pe.matmul(psF[l][:, cols(hf, HALF)], st["fcW"][:, :], src[:, cols(hf, HALF)],
                                         start=True, stop=True)
                    return last

                def turn(b, l):
                    pe.wait_ge(S["ind"], b + 1)
                    pe.wait_ge(S["g"], b + 1)
                    pe.wait_ge(S["tanh2"], b + 1)
                    apart(pe, st)
                    for t in range(NT):
                        pe.transpose(psF[l][0:D, cols(t)], indb[l][:, t, :], st["ident"][:, :])
                        last = pe.transpose(psGn[l][:, t, :], gb[l][:, cols(t)], st["ident"][0:D, 0:D])
                    last.then_inc(S["tr"], 1)

                def fc_industry(b, l):
                    pe.wait_ge(S["indT"], b + 1)
                    fc(l, indT[l]).then_inc(S["fc1"], 1)

                def fc_g(b, l):
                    pe.wait_ge(S["tanh1"], b + 1)
                    fc(l, gb[l]).then_inc(S["fc2"], 1)

                def difference(b, l):
                    pe.wait_ge(S["t"], b + 1)
                    pe.wait_ge(S["w"], b + 1)
                    for t in range(NT):
                        last = pe.matmul(psD[l][:, t:t + 1], T1[l][:, cols(t)], st["av"][:, 0:1], start=True, stop=True)
                    last.then_inc(S["diff"], 1)

                each_lane(pe, [turn, fc_industry, fc_g, difference])

            @block.scalar
            def _(act):
                act.sem_inc(S["tanh2"], LANES)
                act.sem_inc(S["w"], LANES)

                def stage_g(b, l):
                    act.activation(gb[l][:, :], gT[:, b, :], ACT.Copy).then_inc(S["g"], 1)

                def copy_industry(b, l):
                    act.wait_ge(S["tr"], b + 1)
                    act.activation(indT[l][:, :], psF[l][0:D, :], ACT.Copy).then_inc(S["indT"], 1)

                def tanh_industry(b, l):
                    act.wait_ge(S["fc1"], b + 1)
                    act.activation(T1[l][:, :], psF[l][:, :], ACT.Tanh, bias=st["fcb"][:, 0:1]).then_inc(S["tanh1"], 1)

                def tanh_g(b, l):
                    act.wait_ge(S["fc2"], b + 1)
                    act.activation(T2[l][:, :], psF[l][:, :], ACT.Tanh, bias=st["fcb"][:, 0:1]).then_inc(S["tanh2"], 1)

                def weight(b, l):
                    act.wait_ge(S["diff"], b + 1)
                    act.activation(wt[l][:, :], psD[l][:, :], ACT.Tanh, scale=0.5).then_inc(S["w"], 1)

                each_lane(act, [stage_g, copy_industry, tanh_industry, tanh_g, weight])

            @block.vector
            def _(dve):
                def stage_industry(b, l):
                    dve.tensor_copy(indb[l][:, :, :], IND[:, :, b, :]).then_inc(S["ind"], 1)

                def copy_g(b, l):
                    dve.wait_ge(S["tr"], b + 1)
                    dve.tensor_copy(gN[l][:, :, :], psGn[l][:, :, :]).then_inc(S["gN"], 1)

                def subtract(b, l):
                    dve.wait_ge(S["gN"], b + 1)
                    dve.tensor_tensor(out=d[l][:, :, :], in0=indb[l][:, :, :], in1=gN[l][:, :, :], op=ALU.subtract)\
                        .then_inc(S["d"], 1)

                def subtract_tanh(b, l):
                    dve.wait_ge(S["tanh2"], b + 1 + LANES)
                    dve.tensor_tensor(out=T1[l][:, :], in0=T1[l][:, :], in1=T2[l][:, :], op=ALU.subtract)\
                        .then_inc(S["t"], 1)

                def to_sigmoid(b, l):
                    dve.wait_ge(S["w"], b + 1 + LANES)
                    dve.tensor_scalar(out=wt[l][:, :], in0=wt[l][:, :], scalar1=0.5, scalar2=0.5, op0=ALU.mult,
                                      op1=ALU.add).then_inc(S["w1"], 1)

                def weigh(b, l):
                    dve.wait_ge(S["w1"], b + 1)
                    dve.tensor_tensor(out=d[l][:, :, :], in0=d[l][:, :, :],
                                      in1=wt[l][:, :].unsqueeze(2).broadcast_to([P, NT, D]),
                                      op=ALU.mult).then_inc(S["d2"], 1)

                def add_g(b, l):
                    dve.wait_ge(S["d2"], b + 1)
                    dve.tensor_tensor(out=d[l][:, :, :], in0=d[l][:, :, :], in1=gN[l][:, :, :], op=ALU.add)\
                        .then_inc(S["d3"], 1)

                def add_x(b, l):
                    dve.wait_ge(x_loaded, 16)
                    dve.wait_ge(S["d3"], b + 1)
                    dve.tensor_tensor(out=X[:, :, b, :], in0=X[:, :, b, :], in1=d[l][:, :, :], op=ALU.add)\
                        .then_inc(S["x"], 1)

                each_lane(dve, [stage_industry, copy_g, subtract, subtract_tanh, to_sigmoid, weigh, add_g, add_x])


def layer0(nc, w, c, X):
    with ExitStack() as ctx:
        m = Mem(nc, ctx)
        IND = m.sb("IND", [P, NT, B, D])
        st = dict(c)
        with ExitStack() as inner:
            mi = Mem(nc, inner)
            adjT = mi.sb("adjT0", [P, NT, N])
            l0_industry(nc, w, st, adjT, IND)
        st["fcW"] = m.sb("fcW", [D, P])
        st["fcb"] = m.sb("fcb", [P, 1])
        st["av"] = m.sb("av", [P, 1])
        gT = m.sb("gT", [D, B, N])
        st["hT"] = m.sb("hT", [P, B, N])
        st["BS"] = m.sb("BS", [P, B, N], F16)
        st["CS"] = m.sb("CS", [P, B, N], F16)
        st["aggP"] = m.sb("aggP", [P, B, E // 2])
        l0_prepare(nc, w, X, st)
        l0_edges(nc, st, gT, X[:, :, :, :].rearrange("p (k t) b f -> p k (t b f)", k=4))
        l0_combine(nc, w, st, X, IND, gT)



TAB = HID + 3 + D
BIAS, SCALE_P, SCALE_N, WOUT = HID, HID + 1, HID + 2, HID + 3


def l1_prepare(nc, w, c, X, st):
    with ExitStack() as ctx:
        m = Mem(nc, ctx)
        WhT, bh = w["l1"]["WhT"], w["l1"]["bh"]
        Ms = m.sb("Ms", [P, HEADS, D])
        top = m.sb("top", [P, 4, HEADS])
        psM = m.ps("psM", [P, HEADS, D])
        psX = [m.ps(f"psX{i}", [P, N], F16) for i in range(2)]
        S = {k: m.sem("l1p_" + k) for k in ("x_hi", "x_lo", "m_ps", "m_abs", "m_max", "pow2", "inv", "scale", "ms",
                                            "m_hi", "m_lo", "mask", "xt_ps", "xt_act", "xt_dve")}
        XP, M12, tab = st["XP"], st["M12"], st["tab"]
        with nc.Block() as block:

            @block.vector
            def _(dve):
                x = X[:, :, :, :].rearrange("p t b f -> p (t b) f")
                xp = XP[:, :, :, :].rearrange("p t b f -> p (t b) f")
                dve.tensor_scalar(out=xp[:, :, 0:D], in0=x, scalar1=SPLIT, scalar2=None, op0=ALU.mult)\
                    .then_inc(S["x_hi"], 1)
                dve.wait_ge(S["x_hi"], 1)
                dve.scalar_tensor_tensor(out=xp[:, :, D:2 * D], in0=x, scalar=SPLIT, in1=xp[:, :, 0:D],
                                         op0=ALU.mult, op1=ALU.subtract).then_inc(S["x_lo"], 1)
                dve.wait_ge(S["m_abs"], 1)
                dve.tensor_reduce(out=top[:, 0, :], in_=Ms[:, :, :], axis=AX.X, op=ALU.max).then_inc(S["m_abs"], 1)
                dve.wait_ge(S["m_max"], 1)
                dve.tensor_scalar(out=top[:, 1, :], in0=top[:, 1, :], scalar1=2.0 ** -40, scalar2=None, op0=ALU.max)\
                    .then_inc(S["pow2"], 1)
                dve.wait_ge(S["pow2"], 1)
                dve.tensor_scalar(out=top[:, 2, :].bitcast(I32), in0=top[:, 1, :].bitcast(I32), scalar1=0x7F800000,
                                  scalar2=None, op0=ALU.bitwise_and).then_inc(S["pow2"], 1)
                dve.wait_ge(S["pow2"], 2)
                dve.reciprocal(top[:, 3, :], top[:, 2, :]).then_inc(S["inv"], 1)
                dve.tensor_copy(tab[:, :, BIAS], bh[:, :]).then_inc(S["scale"], 1)
                dve.tensor_scalar(out=tab[:, :, SCALE_P], in0=top[:, 2, :], scalar1=2.0 ** -20, scalar2=None,
                                  op0=ALU.mult).then_inc(S["scale"], 1)
                dve.tensor_scalar(out=tab[:, :, SCALE_N], in0=top[:, 2, :], scalar1=-(2.0 ** -20), scalar2=None,
                                  op0=ALU.mult).then_inc(S["scale"], 1)
                dve.wait_ge(S["inv"], 1)
                dve.tensor_scalar(out=top[:, 3, :], in0=top[:, 3, :], scalar1=256.0, scalar2=None, op0=ALU.mult)\
                    .then_inc(S["inv"], 1)
                dve.wait_ge(S["inv"], 2)
                dve.tensor_tensor(out=Ms[:, :, :], in0=psM[:, :, :],
                                  in1=top[:, 3, :].unsqueeze(2).broadcast_to([P, HEADS, D]), op=ALU.mult)\
                    .then_inc(S["ms"], 1)
                dve.wait_ge(S["ms"], 1)
                dve.tensor_copy(M12[:, :, :], Ms[:, :, :]).then_inc(S["m_hi"], 1)
                dve.wait_ge(S["m_hi"], 1)
                dve.tensor_tensor(out=M12[D:P, :, :], in0=Ms[D:P, :, :], in1=M12[D:P, :, :], op=ALU.subtract)\
                    .then_inc(S["m_lo"], 1)
                for b in range(B):
                    dve.wait_ge(S["xt_ps"], b + 1)
                    dve.tensor_copy(st["XT2"][D:P, b, :], psX[b % 2][D:P, :]).then_inc(S["xt_dve"], 1)
                    dve.tensor_copy(st["XT2"][0:D, b, :], psX[b % 2][D:P, :]).then_inc(S["xt_dve"], 1)

            @block.gpsimd
            def _(pool):
                pool.memset(st["H2"][:, :, :, :], 0.0).then_inc(S["mask"], 1)
                pool.wait_ge(S["m_abs"], 2)
                pool.partition_all_reduce(top[:, 1, :], top[:, 0, :], P, bass.bass_isa.ReduceOp.max)\
                    .then_inc(S["m_max"], 1)

            @block.tensor
            def _(pe):
                for h in range(HEADS):
                    last = pe.matmul(psM[:, h, :], WhT[:, h, :, :].rearrange("p k f -> p (k f)"), WhT[:, h, 0, :],
                                     start=True, stop=True)
                last.then_inc(S["m_ps"], 1)
                pe.wait_ge(S["x_lo"], 1)
                for b in range(B):
                    if b >= 2:
                        pe.wait_ge(S["xt_act"], 2 * (b - 1))
                        pe.wait_ge(S["xt_dve"], 2 * (b - 1))
                    for t in range(NT):
                        last = pe.transpose(psX[b % 2][:, cols(t)], XP[:, t, b, :], c["ident16"][:, :])
                    last.then_inc(S["xt_ps"], 1)

            @block.scalar
            def _(act):
                act.wait_ge(S["m_ps"], 1)
                act.activation(Ms[:, :, :], psM[:, :, :], ACT.Abs).then_inc(S["m_abs"], 1)
                for b in range(B):
                    act.wait_ge(S["xt_ps"], b + 1)
                    act.activation(st["XT1"][D:P, b, :], psX[b % 2][0:D, :], ACT.Copy).then_inc(S["xt_act"], 1)
                    act.activation(st["XT1"][0:D, b, :], psX[b % 2][0:D, :], ACT.Copy).then_inc(S["xt_act"], 1)


def l1_heads(nc, c, st):
    U = B * HEADS
    with ExitStack() as ctx:
        m = Mem(nc, ctx)
        XT1, XT2, XP, M12, H2, tab, ident = (st[k] for k in ("XT1", "XT2", "XP", "M12", "H2", "tab", "ident"))
        neg = c["neg"]
        TQ = [m.sb(f"TQ{q}", [P, TAB]) for q in range(2)]
        GT = [m.sb(f"GT{q}", [P, N], F16) for q in range(2)]
        gg = m.sb("gg", [P, NT, P], F16)
        Z = m.sb("Z1", [P, 4, N])
        mx = m.sb("mx1", [P, 4])
        nb = m.sb("nb1", [P, 4])
        rs = [m.sb(f"rs{q}", [P, NT]) for q in range(2)]
        rinv = m.sb("rinv", [P, 4])
        r16 = m.sb("r16", [P, 2, 4], F16)
        EH = [m.sb(f"EH{k}", [P, NT, HALF], F16) for k in range(2)]
        EL = [m.sb(f"EL{k}", [P, NT, HALF], F16) for k in range(2)]
        Rs = m.sb("Rs", [P, HALF])
        OT = m.sb("OT", [P, HALF])
        yb = m.sb("yb", [P, HALF])
        yr = m.sb("yr", [P, HALF])
        psS = [m.ps(f"psS{i}", [P, N]) for i in range(2)]
        psE = [m.ps(f"psE{i}", [P, HALF]) for i in range(2)]
        psA = m.ps("psAtt", [P, HALF])
        psB = m.ps("psBank", [P, HALF])
        psB16 = psB[:, :].bitcast(F16)
        S = {k: m.sem("l1_" + k) for k in (
            "table", "g_ps", "g_hi", "g_lo", "gt_ps", "gt", "scores", "masked", "bias", "exps", "transposed", "hi", "lo",
            "o_ps", "rinv32", "rinv_hi", "rinv", "r_ps", "r_copied", "o_scaled", "y_ps", "y_biased", "y", "h2_ps", "h2")}

        def bh(u):
            return (u // HEADS, u % HEADS)

        with nc.Block() as block:

            @block.gpsimd
            def _(pool):
                def stage(u, q):
                    pool.tensor_copy(TQ[q][:, :], tab[:, u % HEADS, :]).then_inc(S["table"], 1)

                def unit(u, q, first=False, last=False):
                    if not first:
                        pool.wait_ge(S["h2_ps"], 2 * u)
                    if not last:
                        stage(u + 1, 1 - q)

                stage(0, 0)
                unit(0, 0, first=True)
                with pool.Fori(0, U // 2 - 1) as i:
                    unit(2 * i + 1, 1)
                    unit(2 * i + 2, 0)

            @block.tensor
            def _(pe):
                def g_product(u):
                    b, h = bh(u)
                    for t in range(NT):
                        pe.matmul(psB[:, cols(t, D)], XT1[:, b, cols(t)], M12[:, h, :], start=True, stop=False)
                        last = pe.matmul(psB[:, cols(t, D)], XT2[:, b, cols(t)], M12[:, h, :], start=False, stop=True)
                    last.then_inc(S["g_ps"], 1)

                def g_transpose(u):
                    pe.wait_ge(S["g_lo"], u + 1)
                    for t in range(NT):
                        last = pe.transpose(psB16[:, cols(t)], gg[:, t, :], c["ident16"][:, :])
                    last.then_inc(S["gt_ps"], 1)

                def scores(u, q, t):
                    b, _ = bh(u)
                    for xt, first in ((XT1, True), (XT2, False)):
                        for hf in range(2):
                            last = pe.matmul(psS[t % 2][:, cols(hf, HALF)], GT[q][:, cols(t)], xt[:, b, cols(hf, HALF)],
                                             start=first, stop=not first)
                    last.then_inc(S["scores"], 1)

                def transpose(u, t, first=False):
                    g = NT * u + t
                    pe.wait_ge(S["exps"], g + 1)
                    for k in range(2):
                        if not (first and t == 0):
                            pe.wait_ge(S["lo"], 2 * g - 1 + k)
                        for j in range(4):
                            last = pe.transpose(psE[k][:, cols(j)], Z[:, t % 4, cols(4 * k + j)], ident[:, :])
                        last.then_inc(S["transposed"], 1)

                def attend(u, half, j0):
                    b, _ = bh(u)
                    for j in range(j0, j0 + 4):
                        pe.matmul(psA[:, :], XP[:, j, b, :], EH[half][:, j, :], start=(j == 0), stop=False)
                        last = pe.matmul(psA[:, :], XP[:, j, b, :], EL[half][:, j, :], start=False, stop=(j == NT - 1))
                    if j0:
                        last.then_inc(S["o_ps"], 1)

                def spread_sums(i):
                    pe.wait_ge(S["rinv"], i + 1)
                    for t in range(4):
                        for k in range(2):
                            last = pe.matmul(psB[:, cols(t)], r16[:, k, t:t + 1].broadcast_to([P, P]),
                                             c["ident16"][:, :], start=(k == 0), stop=(k == 1))
                    last.then_inc(S["r_ps"], 1)

                def times_w(i, q):
                    pe.wait_ge(S["o_scaled"], i + 1)
                    pe.matmul(psA[:, :], TQ[q][:, 0:HID], OT[:, :], start=True, stop=True).then_inc(S["y_ps"], 1)

                def times_wout(i, q):
                    pe.wait_ge(S["y"], i + 1)
                    for t in range(4):
                        last = pe.matmul(psB[:, cols(t, D)], yr[:, cols(t)], TQ[q][:, WOUT:WOUT + D],
                                         start=True, stop=True)
                    last.then_inc(S["h2_ps"], 1)

                def unit(u, q, first=False, last=False):
                    for t in range(NT):
                        if t < NT - 2:
                            pe.wait_ge(S["masked"], NT * u + t + 1)
                            scores(u, q, t + 2)
                        elif not last:
                            if t == NT - 2:
                                pe.wait_ge(S["gt"], u + 2)
                            pe.wait_ge(S["masked"], NT * u + t + 1)
                            scores(u + 1, 1 - q, t - NT + 2)
                        transpose(u, t, first)
                        if t == 0 and not first:
                            pe.wait_ge(S["lo"], 16 * u)
                            pe.wait_ge(S["y_biased"], 2 * u - 1)
                            attend(u - 1, 1, 0)
                            times_wout(2 * u - 2, 1 - q)
                        if t == 1:
                            if not first:
                                attend(u - 1, 1, 4)
                                pe.wait_ge(S["h2"], 2 * u - 1)
                            if not last:
                                g_product(u + 1)
                        if t == 2 and not first:
                            if not last:
                                pe.wait_ge(S["g_lo"], u + 2)
                            else:
                                pe.wait_ge(S["h2"], 2 * u - 1)
                            spread_sums(2 * u - 1)
                        if t == 3:
                            if not first:
                                times_w(2 * u - 1, 1 - q)
                                pe.wait_ge(S["r_copied"], 2 * u)
                            if not last:
                                g_transpose(u + 1)
                        if t == 4 and not first:
                            if not last:
                                pe.wait_ge(S["gt"], u + 2)
                            times_wout(2 * u - 1, 1 - q)
                        if t == 5:
                            if not first:
                                pe.wait_ge(S["y_biased"], 2 * u)
                            pe.wait_ge(S["lo"], 16 * u + 8)
                            attend(u, 0, 0)
                        if t == 6:
                            attend(u, 0, 4)
                            if not first:
                                pe.wait_ge(S["h2"], 2 * u)
                            else:
                                pe.wait_ge(S["gt"], u + 2)
                            spread_sums(2 * u)
                        if t == 7:
                            times_w(2 * u, q)

                g_product(0)
                g_transpose(0)
                pe.wait_ge(S["gt"], 1)
                scores(0, 0, 0)
                scores(0, 0, 1)
                unit(0, 0, first=True)
                with pe.Fori(0, U // 2 - 1) as i:
                    unit(2 * i + 1, 1)
                    unit(2 * i + 2, 0)
                unit(U - 1, 1, last=True)
                times_wout(2 * U - 2, 1)
                pe.wait_ge(S["lo"], 16 * U)
                attend(U - 1, 1, 0)
                attend(U - 1, 1, 4)
                pe.wait_ge(S["h2"], 2 * U - 1)
                spread_sums(2 * U - 1)
                times_w(2 * U - 1, 1)
                times_wout(2 * U - 1, 1)

            @block.scalar
            def _(act):
                def exps(u, q, t):
                    act.wait_ge(S["bias"], NT * u + t + 1)
                    act.activation(Z[:, t % 4, :], Z[:, t % 4, :], ACT.Exp, bias=nb[:, t % 4:t % 4 + 1],
                                   scale=TQ[q][:, SCALE_P:SCALE_P + 1], accum_out=rs[q][:, t:t + 1])\
                        .then_inc(S["exps"], 1)

                def high(u, t, first=False):
                    g = NT * u + t
                    half = t // 4
                    if t % 4 == 0 and not first:
                        act.wait_ge(S["o_ps"], 2 * u + half - 1)
                    for k in range(2):
                        act.wait_ge(S["transposed"], 2 * g + k + 1)
                        act.activation(EH[half][:, 4 * k:4 * k + 4, cols(t % 4)],
                                       psE[k][:, :].rearrange("p (j n) -> p j n", n=P), ACT.Copy).then_inc(S["hi"], 1)

                def g_high(u):
                    act.wait_ge(S["g_ps"], u + 1)
                    act.activation(gg[:, :, 0:D], psB[:, :].rearrange("p (t f) -> p t f", f=D), ACT.Copy,
                                   scale=1.0 / SPLIT).then_inc(S["g_hi"], 1)

                def g_copy(u, q):
                    act.wait_ge(S["gt_ps"], u + 1)
                    act.activation(GT[q][:, :], psB16, ACT.Copy).then_inc(S["gt"], 1)

                def copy_sums(i):
                    act.wait_ge(S["r_ps"], i + 1)
                    act.activation(Rs[:, :], psB[:, :], ACT.Copy, scale=1.0 / (SPLIT * SUM_SCALE))\
                        .then_inc(S["r_copied"], 1)

                def add_bias(i, q):
                    act.wait_ge(S["y_ps"], i + 1)
                    act.activation(yb[:, :], psA[:, :], ACT.Identity, bias=TQ[q][:, BIAS:BIAS + 1])\
                        .then_inc(S["y_biased"], 1)

                def unit(u, q, first=False, last=False):
                    for t in range(NT):
                        if t < NT - 1:
                            exps(u, q, t + 1)
                        elif not last:
                            exps(u + 1, 1 - q, 0)
                        high(u, t, first)
                        if t == 1 and not last:
                            g_high(u + 1)
                        if t == 2 and not first:
                            copy_sums(2 * u - 1)
                        if t == 3:
                            if not first:
                                add_bias(2 * u - 1, 1 - q)
                            if not last:
                                g_copy(u + 1, 1 - q)
                        if t == 6:
                            copy_sums(2 * u)
                        if t == 7:
                            add_bias(2 * u, q)

                g_high(0)
                g_copy(0, 0)
                exps(0, 0, 0)
                unit(0, 0, first=True)
                with act.Fori(0, U // 2 - 1) as i:
                    unit(2 * i + 1, 1)
                    unit(2 * i + 2, 0)
                unit(U - 1, 1, last=True)
                copy_sums(2 * U - 1)
                add_bias(2 * U - 1, 1)

            @block.vector
            def _(dve):
                def mask(u, q, t):
                    g = NT * u + t
                    dve.wait_ge(S["scores"], g + 1)
                    apart(dve, c)
                    dve.tensor_tensor_reduce(out=Z[:, t % 4, :], in0=psS[t % 2][:, :], in1=neg[:, t, :], scale=1.0,
                                             scalar=LOWEST, op0=ALU.add, op1=ALU.max,
                                             accum_out=mx[:, t % 4:t % 4 + 1]).then_inc(S["masked"], 1)

                def bias(u, q, t):
                    if t == 0:
                        dve.wait_ge(S["table"], u + 1)
                    dve.wait_ge(S["masked"], NT * u + t + 1)
                    dve.tensor_scalar(out=nb[:, t % 4:t % 4 + 1], in0=mx[:, t % 4:t % 4 + 1],
                                      scalar1=TQ[q][:, SCALE_N:SCALE_N + 1], scalar2=LN_PEAK,
                                      op0=ALU.mult, op1=ALU.add).then_inc(S["bias"], 1)

                def low(u, t, between=None):
                    g = NT * u + t
                    half = t // 4
                    for k in range(2):
                        if k and between:
                            bias(*between)
                        dve.wait_ge(S["hi"], 2 * g + k + 1)
                        dve.tensor_tensor(out=EL[half][:, 4 * k:4 * k + 4, cols(t % 4)],
                                          in0=psE[k][:, :].rearrange("p (j n) -> p j n", n=P),
                                          in1=EH[half][:, 4 * k:4 * k + 4, cols(t % 4)],
                                          op=ALU.subtract).then_inc(S["lo"], 1)

                def g_low(u):
                    dve.wait_ge(S["g_hi"], u + 1)
                    dve.scalar_tensor_tensor(out=gg[:, :, D:P], in0=psB[:, :].rearrange("p (t f) -> p t f", f=D),
                                             scalar=1.0 / SPLIT, in1=gg[:, :, 0:D], op0=ALU.mult, op1=ALU.subtract)\
                        .then_inc(S["g_lo"], 1)

                def invert(i, q, half):
                    dve.wait_ge(S["exps"], 4 * i + 4)
                    dve.reciprocal(rinv[:, :], rs[q][:, 4 * half:4 * half + 4]).then_inc(S["rinv32"], 1)
                    dve.wait_ge(S["rinv32"], i + 1)
                    dve.tensor_scalar(out=r16[:, 0, :], in0=rinv[:, :], scalar1=SUM_SCALE, scalar2=None, op0=ALU.mult)\
                        .then_inc(S["rinv_hi"], 1)
                    dve.wait_ge(S["rinv_hi"], i + 1)
                    dve.scalar_tensor_tensor(out=r16[:, 1, :], in0=rinv[:, :], scalar=SUM_SCALE, in1=r16[:, 0, :],
                                             op0=ALU.mult, op1=ALU.subtract).then_inc(S["rinv"], 1)

                def scale(i):
                    dve.wait_ge(S["r_copied"], i + 1)
                    dve.wait_ge(S["o_ps"], i + 1)
                    dve.tensor_tensor(out=OT[:, :], in0=psA[:, :], in1=Rs[:, :], op=ALU.mult).then_inc(S["o_scaled"], 1)

                def lrelu(i):
                    dve.wait_ge(S["y_biased"], i + 1)
                    dve.scalar_tensor_tensor(out=yr[:, :], in0=yb[:, :], scalar=0.01, in1=yb[:, :],
                                             op0=ALU.mult, op1=ALU.max).then_inc(S["y"], 1)

                def add_h2(i, u, half):
                    b = u // HEADS
                    dst = H2[:, 4 * half:4 * half + 4, b, :]
                    dve.wait_ge(S["h2_ps"], i + 1)
                    dve.tensor_tensor(out=dst, in0=dst, in1=psB[:, 0:4 * D].rearrange("p (t f) -> p t f", f=D),
                                      op=ALU.add).then_inc(S["h2"], 1)

                def unit(u, q, first=False, last=False):
                    for t in range(NT):
                        new = (u, q, t + 2) if t < NT - 2 else None if last else (u + 1, 1 - q, t - NT + 2)
                        if new:
                            mask(*new)
                        low(u, t, new)
                        if t == 0 and not first:
                            add_h2(2 * u - 2, u - 1, 0)
                            invert(2 * u - 1, 1 - q, 1)
                        if t == 1 and not last:
                            g_low(u + 1)
                        if t == 2 and not first:
                            scale(2 * u - 1)
                        if t == 3 and not first:
                            lrelu(2 * u - 1)
                        if t == 4 and not first:
                            add_h2(2 * u - 1, u - 1, 1)
                        if t == 5:
                            invert(2 * u, q, 0)
                        if t == 6:
                            scale(2 * u)
                        if t == 7:
                            lrelu(2 * u)

                g_low(0)
                for t in range(2):
                    mask(0, 0, t)
                    bias(0, 0, t)
                unit(0, 0, first=True)
                with dve.Fori(0, U // 2 - 1) as i:
                    unit(2 * i + 1, 1)
                    unit(2 * i + 2, 0)
                unit(U - 1, 1, last=True)
                add_h2(2 * U - 2, U - 1, 0)
                invert(2 * U - 1, 1, 1)
                scale(2 * U - 1)
                lrelu(2 * U - 1)
                add_h2(2 * U - 1, U - 1, 1)


def l1_output(nc, c, X, H2, bout):
    with ExitStack() as ctx:
        m = Mem(nc, ctx, "out_")
        neg, ident = c["neg"], c["ident"]
        Z = m.sb("Z", [P, 4, N])
        part = m.sb("part", [P, 4])
        top = m.sb("top", [P, 4])
        sc = m.sb("sc", [P, 4])
        SUM = m.sb("SUM", [P, D])
        with nc.Block() as block:
            absd, part_max, all_max, step = (m.sem(k) for k in ("absd", "part_max", "all_max", "scale_step"))

            @block.scalar
            def _(act):
                h = H2[:, :, :, :].rearrange("p (k t) b f -> p k (t b f)", k=4)
                for k in range(4):
                    act.activation(Z[:, k, :], h[:, k, :], ACT.Abs).then_inc(absd, 1)

            @block.gpsimd
            def _(pool):
                pool.wait_ge(part_max, 5)
                pool.partition_all_reduce(top[:, 1:2], top[:, 0:1], P, bass.bass_isa.ReduceOp.max).then_inc(all_max, 1)

            @block.vector
            def _(dve):
                for k in range(4):
                    dve.wait_ge(absd, k + 1)
                    dve.tensor_reduce(out=part[:, k:k + 1], in_=Z[:, k, :], axis=AX.X, op=ALU.max).then_inc(part_max, 1)
                dve.wait_ge(part_max, 4)
                dve.tensor_reduce(out=top[:, 0:1], in_=part[:, :], axis=AX.X, op=ALU.max).then_inc(part_max, 1)
                dve.tensor_tensor(out=SUM[:, :], in0=ident[:, 0:D], in1=ident[:, D:P], op=ALU.add).then_inc(step, 1)
                dve.wait_ge(all_max, 1)
                dve.tensor_scalar(out=top[:, 2:3], in0=top[:, 1:2], scalar1=2.0 ** -20, scalar2=None, op0=ALU.max)\
                    .then_inc(step, 1)
                dve.wait_ge(step, 2)
                dve.tensor_scalar(out=top[:, 3:4].bitcast(I32), in0=top[:, 2:3].bitcast(I32), scalar1=0x7F800000,
                                  scalar2=None, op0=ALU.bitwise_and).then_inc(step, 1)
                dve.wait_ge(step, 3)
                dve.tensor_scalar(out=sc[:, 1:2], in0=top[:, 3:4], scalar1=2.0 ** -14, scalar2=None, op0=ALU.mult)\
                    .then_inc(step, 1)
                dve.wait_ge(step, 4)
                dve.reciprocal(sc[:, 0:1], sc[:, 1:2]).then_inc(step, 1)
                dve.tensor_tensor(out=sc[:, 2:3], in0=sc[:, 1:2], in1=sc[:, 1:2], op=ALU.mult).then_inc(step, 1)
                dve.tensor_scalar(out=SUM[:, :], in0=SUM[:, :], scalar1=sc[:, 1:2], scalar2=None, op0=ALU.mult)\
                    .then_inc(step, 1)
                dve.wait_ge(step, 7)
                dve.tensor_scalar(out=sc[:, 3:4], in0=sc[:, 2:3], scalar1=-1.0, scalar2=None, op0=ALU.mult)\
                    .then_inc(step, 1)
                dve.wait_ge(step, 8)

        HP = [m.sb(f"HP{q}", [P, NT, 2 * D], F16) for q in range(2)]
        XG = [m.sb(f"XG{q}", [P, N], F16) for q in range(2)]
        XA = [m.sb(f"XA{q}", [P, N], F16) for q in range(2)]
        XB = [m.sb(f"XB{q}", [P, N], F16) for q in range(2)]
        mx = m.sb("mx", [P, 4])
        nb = m.sb("nb", [P, 4])
        rs = [m.sb(f"rs{q}", [P, NT]) for q in range(2)]
        rinv = m.sb("rinv", [P, 4])
        EH = [m.sb(f"EH{k}", [P, NT, HALF], F16) for k in range(2)]
        EL = [m.sb(f"EL{k}", [P, NT, HALF], F16) for k in range(2)]
        OT = m.sb("OT", [P, HALF])
        o1, o2, o3 = (m.sb(k, [P, 4, D]) for k in ("o1", "o2", "o3"))
        psS = [m.ps(f"psS{i}", [P, N]) for i in range(2)]
        psE = [m.ps(f"psE{i}", [P, HALF]) for i in range(2)]
        psA = m.ps("psA", [P, HALF])
        psB = m.ps("psB", [P, HALF])
        psB16 = psB[:, :].bitcast(F16)
        S = {k: m.sem(k) for k in (
            "h_hi", "h_lo", "xt_ps", "xt", "xg", "scores", "masked", "bias", "exps", "transposed", "hi", "lo",
            "o_ps", "ot", "on_ps", "rinv", "o1", "o2", "o3", "x")}

        def phases(eng, unit):
            unit(0, 0, first=True)
            with eng.Fori(0, B // 2 - 1) as i:
                unit(2 * i + 1, 1)
                unit(2 * i + 2, 0)
            unit(B - 1, 1, last=True)

        with nc.Block() as block:

            @block.gpsimd
            def _(pool):
                def add_x(i, b, half):
                    pool.wait_ge(S["o3"], i + 1)
                    dst = X[:, 4 * half:4 * half + 4, b, :]
                    pool.tensor_tensor(out=dst, in0=dst, in1=o3[:, :, :], op=ALU.add).then_inc(S["x"], 1)

                def unit(b, q, first=False, last=False):
                    if not first:
                        add_x(2 * b - 2, b - 1, 0)
                        add_x(2 * b - 1, b - 1, 1)

                pool.sem_inc(S["x"], FREE)
                phases(pool, unit)
                add_x(2 * B - 2, B - 1, 0)
                add_x(2 * B - 1, B - 1, 1)

            @block.tensor
            def _(pe):
                def turn(b, q):
                    pe.wait_ge(S["h_lo"], b + 1)
                    for t in range(NT):
                        last = pe.transpose(psB16[:, cols(t)], HP[q][:, t, :], c["ident16"][:, :])
                    last.then_inc(S["xt_ps"], 1)

                def scores(q, t):
                    for xt, start in ((XA, True), (XB, False)):
                        for hf in range(2):
                            last = pe.matmul(psS[t % 2][:, cols(hf, HALF)], XG[q][:, cols(t)],
                                             xt[q][:, cols(hf, HALF)], start=start, stop=not start)
                    last.then_inc(S["scores"], 1)

                def attend(q, half, j0):
                    for j in range(j0, j0 + 4):
                        pe.matmul(psA[:, :], HP[q][:, j, :], EH[half][:, j, :], start=(j == 0), stop=False)
                        last = pe.matmul(psA[:, :], HP[q][:, j, :], EL[half][:, j, :], start=False, stop=(j == NT - 1))
                    if j0:
                        last.then_inc(S["o_ps"], 1)

                def turn_output(i):
                    pe.wait_ge(S["ot"], i + 1)
                    for t in range(4):
                        last = pe.matmul(psB[:, cols(t, D)], OT[:, cols(t)], SUM[:, :], start=True, stop=True)
                    last.then_inc(S["on_ps"], 1)

                def unit(b, q, first=False, last=False):
                    for t in range(NT):
                        g = NT * b + t
                        if t < NT - 2:
                            pe.wait_ge(S["masked"], g + 1)
                            scores(q, t + 2)
                        elif not last:
                            if t == NT - 2:
                                pe.wait_ge(S["xt"], 4 * b + 8)
                            pe.wait_ge(S["masked"], g + 1)
                            scores(1 - q, t - NT + 2)
                        pe.wait_ge(S["exps"], g + 1)
                        for k in range(2):
                            if not (first and t == 0):
                                pe.wait_ge(S["lo"], 2 * g - 1 + k)
                            for j in range(4):
                                end = pe.transpose(psE[k][:, cols(j)], Z[:, t % 4, cols(4 * k + j)], ident[:, :])
                            end.then_inc(S["transposed"], 1)
                        if not first:
                            if t == 0:
                                pe.wait_ge(S["lo"], 16 * b)
                                pe.wait_ge(S["ot"], 2 * b - 1)
                                attend(1 - q, 1, 0)
                            if t == 1:
                                attend(1 - q, 1, 4)
                            if t == 2:
                                pe.wait_ge(S["o1"], 2 * b - 1)
                                turn_output(2 * b - 1)
                        if t == 3 and not last:
                            if not first:
                                pe.wait_ge(S["o1"], 2 * b)
                            turn(b + 1, 1 - q)
                        if t == 5:
                            pe.wait_ge(S["lo"], 16 * b + 8)
                            if not first:
                                pe.wait_ge(S["ot"], 2 * b)
                            attend(q, 0, 0)
                        if t == 6:
                            attend(q, 0, 4)
                        if t == 7:
                            if not last:
                                pe.wait_ge(S["xg"], b + 2)
                            else:
                                pe.wait_ge(S["o1"], 2 * b)
                            turn_output(2 * b)

                turn(0, 0)
                pe.wait_ge(S["xt"], 4)
                scores(0, 0)
                scores(0, 1)
                phases(pe, unit)
                pe.wait_ge(S["lo"], 16 * B)
                pe.wait_ge(S["ot"], 2 * B - 1)
                attend(1, 1, 0)
                attend(1, 1, 4)
                pe.wait_ge(S["o1"], 2 * B - 1)
                turn_output(2 * B - 1)

            @block.scalar
            def _(act):
                def copy_turned(b, q):
                    act.wait_ge(S["xt_ps"], b + 1)
                    act.activation(XG[q][:, :], psB16, ACT.Copy).then_inc(S["xg"], 1)

                def exps(b, q, t):
                    act.wait_ge(S["bias"], NT * b + t + 1)
                    act.activation(Z[:, t % 4, :], Z[:, t % 4, :], ACT.Exp, bias=nb[:, t % 4:t % 4 + 1],
                                   scale=sc[:, 2:3], accum_out=rs[q][:, t:t + 1]).then_inc(S["exps"], 1)

                def high(b, t, first=False):
                    g = NT * b + t
                    half = t // 4
                    if t % 4 == 0 and not first:
                        act.wait_ge(S["o_ps"], 2 * b + half - 1)
                    for k in range(2):
                        act.wait_ge(S["transposed"], 2 * g + k + 1)
                        act.activation(EH[half][:, 4 * k:4 * k + 4, cols(t % 4)],
                                       psE[k][:, :].rearrange("p (j n) -> p j n", n=P), ACT.Copy).then_inc(S["hi"], 1)

                def copy_output(i, early=False):
                    act.wait_ge(S["o_ps"], i + 1)
                    if not early:
                        act.wait_ge(S["on_ps"], i)
                    act.activation(OT[:, :], psA[:, :], ACT.Copy).then_inc(S["ot"], 1)

                def unit(b, q, first=False, last=False):
                    for t in range(NT):
                        if t < NT - 1:
                            exps(b, q, t + 1)
                        elif not last:
                            exps(b + 1, 1 - q, 0)
                        high(b, t, first)
                        if t == 1 and not first:
                            copy_output(2 * b - 1)
                        if t == 3 and not last:
                            copy_turned(b + 1, 1 - q)
                        if t == 6:
                            copy_output(2 * b, first)

                copy_turned(0, 0)
                exps(0, 0, 0)
                phases(act, unit)
                copy_output(2 * B - 1)

            @block.vector
            def _(dve):
                def split(b, q):
                    h = H2[:, :, b, :]
                    dve.tensor_scalar(out=HP[q][:, :, 0:D], in0=h, scalar1=sc[:, 0:1], scalar2=None, op0=ALU.mult)\
                        .then_inc(S["h_hi"], 1)
                    dve.wait_ge(S["h_hi"], b + 1)
                    apart(dve, c)
                    dve.scalar_tensor_tensor(out=HP[q][:, :, D:2 * D], in0=h, scalar=sc[:, 0:1],
                                             in1=HP[q][:, :, 0:D], op0=ALU.mult, op1=ALU.subtract).then_inc(S["h_lo"], 1)

                def repeat(b, q, k):
                    if k == 0:
                        dve.wait_ge(S["xg"], b + 1)
                    for rows in (slice(0, D), slice(D, P)):
                        dve.tensor_copy((XA, XB)[k][q][rows, :], XG[q][k * D:k * D + D, :]).then_inc(S["xt"], 1)

                def mask(b, q, t):
                    g = NT * b + t
                    dve.wait_ge(S["scores"], g + 1)
                    apart(dve, c)
                    dve.tensor_tensor_reduce(out=Z[:, t % 4, :], in0=psS[t % 2][:, :], in1=neg[:, t, :], scale=1.0,
                                             scalar=LOWEST, op0=ALU.add, op1=ALU.max,
                                             accum_out=mx[:, t % 4:t % 4 + 1]).then_inc(S["masked"], 1)

                def bias(b, t):
                    dve.wait_ge(S["masked"], NT * b + t + 1)
                    dve.tensor_scalar(out=nb[:, t % 4:t % 4 + 1], in0=mx[:, t % 4:t % 4 + 1], scalar1=sc[:, 3:4],
                                      scalar2=LN_PEAK, op0=ALU.mult, op1=ALU.add).then_inc(S["bias"], 1)

                def low(b, t, between=None):
                    g = NT * b + t
                    half = t // 4
                    for k in range(2):
                        if k and between:
                            bias(between[0], between[2])
                        dve.wait_ge(S["hi"], 2 * g + k + 1)
                        dve.tensor_tensor(out=EL[half][:, 4 * k:4 * k + 4, cols(t % 4)],
                                          in0=psE[k][:, :].rearrange("p (j n) -> p j n", n=P),
                                          in1=EH[half][:, 4 * k:4 * k + 4, cols(t % 4)],
                                          op=ALU.subtract).then_inc(S["lo"], 1)

                def normalise(i, q, half):
                    dve.wait_ge(S["exps"], 4 * i + 4)
                    dve.reciprocal(rinv[:, :], rs[q][:, 4 * half:4 * half + 4]).then_inc(S["rinv"], 1)
                    dve.wait_ge(S["rinv"], i + 1)
                    dve.wait_ge(S["on_ps"], i + 1)
                    dve.tensor_tensor(out=o1[:, :, :], in0=psB[:, 0:4 * D].rearrange("p (t f) -> p t f", f=D),
                                      in1=rinv[:, :].unsqueeze(2).broadcast_to([P, 4, D]), op=ALU.mult)\
                        .then_inc(S["o1"], 1)

                def finish(i):
                    dve.wait_ge(S["o1"], i + 1)
                    dve.tensor_tensor(out=o2[:, :, :], in0=o1[:, :, :],
                                      in1=bout[:, :].unsqueeze(1).broadcast_to([P, 4, D]), op=ALU.add)\
                        .then_inc(S["o2"], 1)
                    dve.wait_ge(S["o2"], i + 1)
                    dve.wait_ge(S["x"], i + FREE)
                    apart(dve, c)
                    dve.scalar_tensor_tensor(out=o3[:, :, :], in0=o2[:, :, :], scalar=0.01, in1=o2[:, :, :],
                                             op0=ALU.mult, op1=ALU.max).then_inc(S["o3"], 1)

                def unit(b, q, first=False, last=False):
                    for t in range(NT):
                        new = (b, q, t + 2) if t < NT - 2 else None if last else (b + 1, 1 - q, t - NT + 2)
                        if new:
                            mask(*new)
                        low(b, t, new)
                        if t == 0 and not first:
                            finish(2 * b - 2)
                        if t == 2:
                            if not first:
                                normalise(2 * b - 1, 1 - q, 1)
                            if not last:
                                split(b + 1, 1 - q)
                        if t == 3 and not first:
                            finish(2 * b - 1)
                        if t == 4 and not last:
                            repeat(b + 1, 1 - q, 0)
                            repeat(b + 1, 1 - q, 1)
                        if t == 7:
                            normalise(2 * b, q, 0)

                split(0, 0)
                repeat(0, 0, 0)
                repeat(0, 0, 1)
                for t in range(2):
                    mask(0, 0, t)
                    bias(0, t)
                phases(dve, unit)
                finish(2 * B - 2)
                normalise(2 * B - 1, 1, 1)
                finish(2 * B - 1)


def layer1_weights(m, w):
    o = {"WhT": m.sb("WhT", [P, HEADS, 2, D]), "bh": m.sb("bh", [P, HEADS]), "bout": m.sb("bout", [P, D]),
         "tab": m.sb("tab", [P, HEADS, TAB])}
    pairs = [(o["tab"][:, :, WOUT:WOUT + D], w["Wout"]), (o["bh"][:, :], w["bh"]),
             (o["bout"][:, :], w["bout"].partition_broadcast(P))]
    for k in range(2):
        pairs += [(o["WhT"][:, :, k, :], w["WhT"]), (o["tab"][k * D:k * D + D, :, 0:HID], w["Wh"])]
    return o, pairs


def layer1(nc, w, c, X):
    with ExitStack() as ctx:
        m = Mem(nc, ctx)
        H2 = m.sb("H2", [P, NT, B, D])
        with ExitStack() as inner:
            mi = Mem(nc, inner)
            st = dict(c, H2=H2, XT1=mi.sb("XT1", [P, B, N], F16), XT2=mi.sb("XT2", [P, B, N], F16),
                      XP=mi.sb("XP", [P, NT, B, 2 * D], F16), M12=mi.sb("M12", [P, HEADS, D], F16),
                      tab=w["l1"]["tab"])
            l1_prepare(nc, w, c, X, st)
            l1_heads(nc, c, st)
        l1_output(nc, c, X, H2, w["l1"]["bout"])



def layer2_weights(m, w):
    o = {k: m.sb(k, shape) for k, shape in (("adjT2", [P, NT, N]), ("W1a", [P, P]), ("W1b", [P, P]), ("W2b", [P, P]),
                                            ("b1", [P, 1]), ("b2", [P, 1]), ("b2r", [P, 2, D]), ("iv", [1, B, D]))}
    pairs = [(o["iv"][:, b, :], w["iv"]) for b in range(B)]
    for k in range(2):
        blk = slice(k * D, k * D + D)
        pairs += [(o["W1a"][blk, blk], w["W1T"][0:D, :]), (o["W1b"][blk, blk], w["W1T"][D:2 * D, :]),
                  (o["W2b"][blk, blk], w["W2T"]), (o["b1"][blk, :], w["b1"]), (o["b2"][blk, :], w["b2"]),
                  (o["b2r"][:, k, :], w["b2row"].partition_broadcast(P))]
    return o, pairs + [(o["adjT2"][:, :, :], w["adjT"])]


def layer2(nc, w, c, X):
    STEPS, PAIRS = 3, B // 2
    with ExitStack() as ctx:
        m = Mem(nc, ctx)
        o = w["l2"]
        adjT, b1, b2, b2r = o["adjT2"], o["b1"], o["b2"], o["b2r"]
        W1a, W1b, W2 = o["W1a"], o["W1b"], o["W2b"]
        V = m.sb("V", [P, NT, B, D])
        VT = m.sb("VT", [P, PAIRS, N])
        EF = m.sb("EF", [P, N])
        HT = m.sb("HT", [P, N])
        psE, psH, psT, psN = (m.ps(k, [P, N]) for k in ("psE2", "psH2", "psT2", "psN2"))
        zeroed, copied, started = m.sem("l2_zeroed"), m.sem("l2_copied"), m.sem("l2_started")
        S = {k: m.sem("l2_" + k) for k in ("vt0_ps", "vt0", "eff_ps", "eff", "h_ps", "h", "v_ps", "vt", "v")}
        with nc.Block() as block:

            @block.gpsimd
            def _(pool):
                for n, k in enumerate((W1a, W1b, W2)):
                    pool.memset(k[0:D, D:P], 0.0).then_inc(zeroed, 1)
                    pool.wait_ge(zeroed, 2 * n + 1)
                    pool.memset(k[D:P, 0:D], 0.0).then_inc(zeroed, 1)
                    pool.wait_ge(zeroed, 2 * n + 2)

            @block.vector
            def _(dve):
                dve.sem_inc(S["v"], FREE)
                for p in range(PAIRS):
                    pair = slice(2 * p, 2 * p + 2)
                    dve.tensor_copy(V[:, :, pair, :], X[:, :, pair, :]).then_inc(copied, 1)
                    dve.wait_ge(copied, p + 1)
                    dve.tensor_copy(V[0:1, 0, pair, :], o["iv"][:, pair, :]).then_inc(started, 1)
                for p in range(PAIRS):
                    dve.wait_ge(S["vt0_ps"], p + 1)
                    dve.tensor_copy(VT[:, p, :], (psE, psH, psT, psN)[p][:, :]).then_inc(S["vt0"], 1)
                with dve.Fori(0, STEPS) as s:
                    for p in range(PAIRS):
                        i = PAIRS * s + p
                        dve.wait_ge(S["v_ps"], i + 1 + FREE)
                        dve.tensor_scalar(out=VT[:, p, :], in0=psT[:, :], scalar1=b2[:, 0:1], scalar2=None, op0=ALU.add)\
                            .then_inc(S["vt"], 1)
                        dve.tensor_tensor(out=V[:, :, 2 * p:2 * p + 2, :].rearrange("p t b f -> p t (b f)"),
                                          in0=psN[:, :].rearrange("p (t c) -> p t c", c=P),
                                          in1=b2r[:, :, :].rearrange("p b f -> p (b f)").unsqueeze(1)
                                          .broadcast_to([P, NT, P]), op=ALU.add).then_inc(S["v"], 1)
                dve.wait_ge(S["v"], STEPS * PAIRS + FREE)
                dve.tensor_tensor(out=X[:, :, :, :].rearrange("p t b f -> p (t b f)"),
                                  in0=X[:, :, :, :].rearrange("p t b f -> p (t b f)"),
                                  in1=V[:, :, :, :].rearrange("p t b f -> p (t b f)"), op=ALU.add).then_inc(copied, 1)

            @block.tensor
            def _(pe):
                pe.sem_inc(S["v_ps"], FREE)
                for p in range(PAIRS):
                    pe.wait_ge(started, p + 1)
                    for t in range(NT):
                        last = pe.transpose((psE, psH, psT, psN)[p][:, cols(t)],
                                            V[:, t, 2 * p:2 * p + 2, :].rearrange("p b f -> p (b f)"), c["ident"][:, :])
                    last.then_inc(S["vt0_ps"], 1)
                pe.wait_ge(S["vt0"], PAIRS)
                pe.wait_ge(zeroed, 6)

                def effects(s, p):
                    i = PAIRS * s + p
                    pe.wait_ge(S["eff"], i + FREE)
                    for j in range(NT):
                        for hf in range(2):
                            last = pe.matmul(psE[:, cols(hf, HALF)],
                                             V[:, j, 2 * p:2 * p + 2, :].rearrange("p b f -> p (b f)"),
                                             adjT[:, j, cols(hf, HALF)], start=(j == 0), stop=(j == NT - 1))
                    last.then_inc(S["eff_ps"], 1)

                def update(s, p):
                    i = PAIRS * s + p
                    pe.wait_ge(S["eff"], i + 1 + FREE)
                    for hf in range(2):
                        pe.matmul(psH[:, cols(hf, HALF)], W1a[:, :], VT[:, p, cols(hf, HALF)], start=True, stop=False)
                        last = pe.matmul(psH[:, cols(hf, HALF)], W1b[:, :], EF[:, cols(hf, HALF)], start=False, stop=True)
                    last.then_inc(S["h_ps"], 1)

                def output(s, p):
                    i = PAIRS * s + p
                    pe.wait_ge(S["h"], i + 1)
                    pe.wait_ge(S["v"], i + FREE)
                    for hf in range(2):
                        pe.matmul(psT[:, cols(hf, HALF)], W2[:, :], HT[:, cols(hf, HALF)], start=True, stop=True)
                    for t in range(NT):
                        last = pe.matmul(psN[:, cols(t)], HT[:, cols(t)], W2[:, :], start=True, stop=True)
                    last.then_inc(S["v_ps"], 1)

                with pe.Fori(0, STEPS) as s:
                    pe.wait_ge(S["v"], PAIRS * s + FREE)
                    effects(s, 0)
                    for p in range(PAIRS):
                        update(s, p)
                        if p + 1 < PAIRS:
                            effects(s, p + 1)
                        output(s, p)

            @block.scalar
            def _(act):
                act.sem_inc(S["eff"], FREE)
                with act.Fori(0, STEPS) as s:
                    for p in range(PAIRS):
                        i = PAIRS * s + p
                        act.wait_ge(S["eff_ps"], i + 1)
                        act.activation(EF[:, :], psE[:, :], ACT.Copy).then_inc(S["eff"], 1)
                        act.wait_ge(S["h_ps"], i + 1)
                        act.wait_ge(S["v_ps"], i + FREE)
                        act.activation(HT[:, :], psH[:, :], ACT.Relu, bias=b1[:, 0:1]).then_inc(S["h"], 1)



def l3_attention(nc, c, X, W3T, A):
    AHEAD = 3
    with ExitStack() as ctx:
        m = Mem(nc, ctx, "add_")
        neg, ident = c["neg"], c["ident"]
        Xb = [m.sb(f"Xb{q}", [P, NT, D]) for q in range(2)]
        Tb = [m.sb(f"Tb{q}", [D, N]) for q in range(2)]
        Hb = [m.sb(f"Hb{q}", [P, NT, D]) for q in range(2)]
        Z = m.sb("Z2", [P, 4, N])
        Z1 = m.sb("Z1s", [P, 2, N])
        Z2 = m.sb("Z2s", [P, 2, N])
        mx = m.sb("mx2", [P, 4])
        na = m.sb("na2", [P, 4])
        nm = m.sb("nm2", [P, 4])
        nb = m.sb("nb2", [P, 4, 2])
        rs = [m.sb(f"rs2{q}", [P, NT]) for q in range(2)]
        ri = m.sb("ri2", [P, NT])
        e1 = [m.sb(f"e1{q}", [P, NT, 2]) for q in range(2)]
        ET = m.sb("ET", [P, 2, NT, P])
        o = m.sb("o2", [P, NT, D])
        oe = m.sb("o2e", [P, NT, D])
        o2 = m.sb("o2b", [P, NT, D])
        psS = [m.ps(f"psT{i}", [P, N]) for i in range(2)]
        psE = [m.ps(f"psU{i}", [P, HALF]) for i in range(2)]
        psO = m.ps("psO", [P, NT, D])
        psV = m.ps("psV", [P, HALF])
        S = {k: m.sem("at_" + k) for k in (
            "staged", "t_ps", "t", "v_ps", "v", "e1_ps", "e1", "e2_ps", "masked", "na", "nm", "bias", "exps",
            "joined", "transposed", "ev0", "ev1", "o_ps", "rinv", "o1", "o2", "oexp", "o3", "x")}

        def phases(eng, unit):
            unit(0, 0, first=True)
            with eng.Fori(0, B // 2 - 1) as i:
                unit(2 * i + 1, 1)
                unit(2 * i + 2, 0)
            unit(B - 1, 1, last=True)

        with nc.Block() as block:

            @block.gpsimd
            def _(pool):
                def stage(b, q):
                    pool.tensor_copy(Xb[q][:, :, :], X[:, :, b, :]).then_inc(S["staged"], 1)

                def add_x(b):
                    pool.wait_ge(S["o3"], b + 1)
                    pool.tensor_tensor(out=X[:, :, b, :], in0=X[:, :, b, :], in1=o2[:, :, :], op=ALU.add)\
                        .then_inc(S["x"], 1)

                def unit(b, q, first=False, last=False):
                    if not first:
                        pool.wait_ge(S["t_ps"], 2 * b)
                    if not last:
                        stage(b + 1, 1 - q)
                    if not first:
                        add_x(b - 1)

                pool.sem_inc(S["x"], FREE)
                stage(0, 0)
                phases(pool, unit)
                add_x(B - 1)

            @block.tensor
            def _(pe):
                def prepare_x(b, q, half, first=False):
                    if half == 0:
                        pe.wait_ge(S["staged"], b + 1)
                    if not first or half:
                        if half == 0:
                            pe.wait_ge(S["e1"], 2 * b)
                        else:
                            pe.wait_ge(S["t"], 2 * b + half)
                        apart(pe, c)
                    for t in range(4):
                        last = pe.transpose(psV[0:D, cols(t)], Xb[q][:, 4 * half + t, :], ident[:, :])
                    last.then_inc(S["t_ps"], 1)

                def prepare_v(b, q):
                    pe.wait_ge(S["t"], 2 * b + 2)
                    for t in range(NT):
                        last = pe.matmul(psV[:, cols(t, D)], Tb[q][:, cols(t)], W3T[:, :], start=True, stop=True)
                    last.then_inc(S["v_ps"], 1)

                def prepare_e(b, q, early=False):
                    if not early:
                        pe.wait_ge(S["masked"], NT * (b - 1))
                    for hf in range(2):
                        last = pe.matmul(psS[q][:, cols(hf, HALF)], A[1][:, :], Tb[q][:, cols(hf, HALF)],
                                         start=True, stop=True)
                    last.then_inc(S["e2_ps"], 1)
                    pe.wait_ge(S["v"], b + 1)
                    for t in range(NT):
                        last = pe.matmul(psV[:, t:t + 1], Tb[q][:, cols(t)], A[0][:, 0:1], start=True, stop=True)
                    last.then_inc(S["e1_ps"], 1)

                def attend(b, q, t, early=False):
                    g = NT * b + t
                    pe.wait_ge(S["ev0"], g + 1)
                    pe.wait_ge(S["ev1"], g + 1)
                    if t == 0 and not early:
                        pe.wait_ge(S["o1"], b)
                    for j in range(NT):
                        last = pe.matmul(psO[:, t, :], ET[:, t % 2, j, :], Hb[q][:, j, :],
                                         start=(j == 0), stop=(j == NT - 1))
                    last.then_inc(S["o_ps"], 1)

                def unit(b, q, first=False, last=False):
                    for t in range(NT):
                        g = NT * b + t
                        if t == 0 and not first:
                            attend(b - 1, 1 - q, NT - 1)
                        pe.wait_ge(S["joined"], g + 1)
                        for k in range(2):
                            if not (first and t == 0):
                                pe.wait_ge(S[f"ev{k}"], g)
                            for j in range(4):
                                end = pe.transpose(psE[k][:, cols(j)], Z[:, t % 4, cols(4 * k + j)], ident[:, :])
                            end.then_inc(S["transposed"], 1)
                        if t:
                            attend(b, q, t - 1, first)
                        if not last:
                            if t in (1, 2):
                                prepare_x(b + 1, 1 - q, t - 1)
                            if t == 3:
                                prepare_v(b + 1, 1 - q)
                            if t == 4:
                                prepare_e(b + 1, 1 - q, first)

                prepare_x(0, 0, 0, True)
                prepare_x(0, 0, 1, True)
                prepare_v(0, 0)
                prepare_e(0, 0, True)
                phases(pe, unit)
                attend(B - 1, 1, NT - 1)

            @block.scalar
            def _(act):
                def copy_t(b, q, half):
                    act.wait_ge(S["t_ps"], 2 * b + half + 1)
                    act.activation(Tb[q][:, cols(half, HALF)], psV[0:D, :], ACT.Copy).then_inc(S["t"], 1)

                def copy_v(b, q):
                    act.wait_ge(S["v_ps"], b + 1)
                    act.activation(Hb[q][:, :, :], psV[:, :].rearrange("p (t f) -> p t f", f=D), ACT.Copy)\
                        .then_inc(S["v"], 1)

                def exps(b, q, t, early=False):
                    g = NT * b + t
                    r = t % 4
                    act.wait_ge(S["bias"], g + 1)
                    if not early:
                        act.wait_ge(S["joined"], g - 1)
                        apart(act, c)
                    act.activation(Z1[:, t % 2, :], Z[:, r, :], ACT.Exp, bias=nb[:, r, 0:1])
                    act.activation(Z2[:, t % 2, :], Z[:, r, :], ACT.Exp, bias=nb[:, r, 1:2], scale=0.2)\
                        .then_inc(S["exps"], 1)

                def exp_o(b):
                    act.wait_ge(S["o1"], b + 1)
                    act.activation(oe[:, :, :], o[:, :, :], ACT.Exp).then_inc(S["oexp"], 1)

                def unit(b, q, first=False, last=False):
                    for t in range(NT):
                        g = NT * b + t
                        ahead = t + AHEAD - 1
                        if ahead < NT:
                            exps(b, q, ahead)
                        elif not last:
                            exps(b + 1, 1 - q, ahead - NT)
                        act.wait_ge(S["transposed"], 2 * g + 1)
                        if not (first and t < 2):
                            act.wait_ge(S["o_ps"], g - 1)
                        act.activation(ET[:, t % 2, 0:4, :], psE[0][:, :].rearrange("p (j n) -> p j n", n=P), ACT.Copy)\
                            .then_inc(S["ev0"], 1)
                        if t in (1, 2) and not last:
                            copy_t(b + 1, 1 - q, t - 1)
                        if t == 3 and not last:
                            copy_v(b + 1, 1 - q)
                        if t == 1 and not first:
                            exp_o(b - 1)

                copy_t(0, 0, 0)
                copy_t(0, 0, 1)
                copy_v(0, 0)
                for t in range(AHEAD - 1):
                    exps(0, 0, t, early=True)
                phases(act, unit)
                exp_o(B - 1)

            @block.vector
            def _(dve):
                def copy_e1(b, q):
                    dve.wait_ge(S["e1_ps"], b + 1)
                    dve.tensor_copy(e1[q][:, :, 0], psV[:, 0:NT]).then_inc(S["e1"], 1)
                    dve.tensor_scalar(out=e1[q][:, :, 1], in0=psV[:, 0:NT], scalar1=0.2, scalar2=None, op0=ALU.mult)\
                        .then_inc(S["e1"], 1)

                def mask(b, q, t):
                    g = NT * b + t
                    r = slice(t % 4, t % 4 + 1)
                    if t == 0:
                        dve.wait_ge(S["e2_ps"], b + 1)
                    apart(dve, c)
                    dve.tensor_tensor_reduce(out=Z[:, t % 4, :], in0=psS[q][:, :],
                                             in1=neg[:, t, :], scale=1.0, scalar=LOWEST, op0=ALU.add, op1=ALU.max,
                                             accum_out=mx[:, r]).then_inc(S["masked"], 1)

                def bias_1(b, q, t):
                    g = NT * b + t
                    r = slice(t % 4, t % 4 + 1)
                    dve.wait_ge(S["masked"], g + 1)
                    if t == 0:
                        dve.wait_ge(S["e1"], 2 * b + 2)
                        apart(dve, c)
                    dve.tensor_scalar(out=na[:, r], in0=mx[:, r], scalar1=e1[q][:, t, 0:1], scalar2=-1.0,
                                      op0=ALU.add, op1=ALU.mult).then_inc(S["na"], 1)

                def bias_2(b, q, t):
                    r = slice(t % 4, t % 4 + 1)
                    dve.wait_ge(S["na"], NT * b + t + 1)
                    dve.scalar_tensor_tensor(out=nm[:, r], in0=na[:, r], scalar=0.2, in1=na[:, r],
                                             op0=ALU.mult, op1=ALU.min).then_inc(S["nm"], 1)

                def bias_3(b, q, t):
                    dve.wait_ge(S["nm"], NT * b + t + 1)
                    dve.tensor_scalar(out=nb[:, t % 4, :], in0=e1[q][:, t, :], scalar1=nm[:, t % 4:t % 4 + 1],
                                      scalar2=None, op0=ALU.add).then_inc(S["bias"], 1)

                def join(b, q, t):
                    g = NT * b + t
                    dve.wait_ge(S["exps"], g + 1)
                    dve.scalar_tensor_tensor(out=Z[:, t % 4, :], in0=Z1[:, t % 2, :], scalar=1.0, in1=Z2[:, t % 2, :],
                                             op0=ALU.mult, op1=ALU.max,
                                             accum_out=rs[q][:, t:t + 1]).then_inc(S["joined"], 1)

                def normalise(b, q):
                    dve.wait_ge(S["joined"], NT * b + NT)
                    dve.reciprocal(ri[:, :], rs[q][:, :]).then_inc(S["rinv"], 1)
                    dve.wait_ge(S["rinv"], b + 1)
                    dve.wait_ge(S["o_ps"], NT * b + NT)
                    dve.tensor_tensor(out=o[:, :, :], in0=psO[:, :, :],
                                      in1=ri[:, :].unsqueeze(2).broadcast_to([P, NT, D]), op=ALU.mult)\
                        .then_inc(S["o1"], 1)

                def finish(b):
                    dve.wait_ge(S["oexp"], b + 1)
                    dve.tensor_scalar(out=oe[:, :, :], in0=oe[:, :, :], scalar1=1.0, scalar2=-1.0, op0=ALU.min,
                                      op1=ALU.add).then_inc(S["o2"], 1)
                    dve.wait_ge(S["o2"], b + 1)
                    dve.wait_ge(S["x"], b + FREE)
                    apart(dve, c)
                    dve.scalar_tensor_tensor(out=o2[:, :, :], in0=o[:, :, :], scalar=0.0, in1=oe[:, :, :],
                                             op0=ALU.max, op1=ALU.add).then_inc(S["o3"], 1)

                def later(b, q, t, ahead, last=False):
                    t = t + ahead
                    return (b, q, t) if t < NT else None if last else (b + 1, 1 - q, t - NT)

                def unit(b, q, first=False, last=False):
                    for t in range(NT):
                        g = NT * b + t
                        new, before, joining = (later(b, q, t, k, last) for k in (AHEAD, AHEAD - 1, 1))
                        if new:
                            mask(*new)
                        if before:
                            bias_3(*before)
                        if joining:
                            join(*joining)
                        if t == NT - AHEAD and not last:
                            copy_e1(b + 1, 1 - q)
                        if new:
                            bias_1(*new)
                        if t == 0 and not first:
                            normalise(b - 1, 1 - q)
                        dve.wait_ge(S["transposed"], 2 * g + 2)
                        if not (first and t < 2):
                            dve.wait_ge(S["o_ps"], g - 1)
                        dve.tensor_copy(ET[:, t % 2, 4:8, :], psE[1][:, :].rearrange("p (j n) -> p j n", n=P))\
                            .then_inc(S["ev1"], 1)
                        if new:
                            bias_2(*new)
                        if t == 2 and not first:
                            finish(b - 1)

                copy_e1(0, 0)
                for t in range(AHEAD):
                    mask(0, 0, t)
                    bias_1(0, 0, t)
                    bias_2(0, 0, t)
                    if t < AHEAD - 1:
                        bias_3(0, 0, t)
                join(0, 0, 0)
                phases(dve, unit)
                normalise(B - 1, 1)
                finish(B - 1)


def layer3_weights(m, w):
    o = {"W3T": m.sb("W3T", [D, D]), "W3": m.sb("W3", [D, D]), "a3": m.sb("a3", [D, 2])}
    return o, [(o[k][:, :], w[k]) for k in o]


def layer3(nc, w, c, X):
    with ExitStack() as ctx:
        m = Mem(nc, ctx)
        W3T, W3, a3 = (w["l3"][k] for k in ("W3T", "W3", "a3"))
        a3b = m.sb("a3b", [D, 2, P])
        A = [m.sb(f"A{k}", [D, P]) for k in range(2)]
        with ExitStack() as inner:
            mi = Mem(nc, inner)
            psA = mi.ps("psA3", [D, 2, P])
            ones, rep, a_ps, done = (mi.sem("l3_" + k) for k in ("ones", "rep", "a_ps", "a"))
            with nc.Block() as block:

                @block.vector
                def _(dve):
                    dve.memset(a3b[:, :, :], 1.0).then_inc(ones, 1)
                    dve.wait_ge(ones, 1)
                    for k in range(2):
                        dve.tensor_scalar(out=a3b[:, k, :], in0=a3b[:, k, :], scalar1=a3[:, k:k + 1], scalar2=None,
                                          op0=ALU.mult).then_inc(rep, 1)
                    dve.wait_ge(a_ps, 1)
                    for k in range(2):
                        dve.tensor_copy(A[k][:, :], psA[:, k, :]).then_inc(done, 1)

                @block.tensor
                def _(pe):
                    pe.wait_ge(rep, 2)
                    for k in range(2):
                        last = pe.matmul(psA[:, k, :], W3[:, :], a3b[:, k, :], start=True, stop=True)
                    last.then_inc(a_ps, 1)

        l3_attention(nc, c, X, W3T, A)


LAYERS = {0: layer0, 1: layer1, 2: layer2, 3: layer3}
WEIGHTS = {1: layer1_weights, 2: layer2_weights, 3: layer3_weights}


def build(nc, w, out, layers=(0, 1, 2, 3)):
    with ExitStack() as ctx:
        m = Mem(nc, ctx)
        X = m.sb("X", [P, NT, B, D])
        c = {"ident": m.sb("ident", [P, P]), "ident16": m.sb("ident16", [P, P], F16),
             "built": m.sem("ident_built"), "passed": m.sem("passed"),
             "neg": m.sb("neg", [P, NT, N], BF16)}
        make_constants(nc, c)
        w = dict(w)
        LAYERS[layers[0]](nc, w, c, X)
        for last, n in zip(layers, layers[1:]):
            with ExitStack() as own:
                w[f"l{n}"], pairs = WEIGHTS[n](Mem(nc, own), w)
                layer_norm(nc, X, f"_{last}", pairs)
                LAYERS[n](nc, w, c, X)
        layer_norm(nc, X, f"_{layers[-1]}", out=out)


def host_layout(v):
    x, adj, H = v["x"], v["adj"], v["L0_gnn_H"]
    tiles = lambda a: a.reshape(NT, P, *a.shape[1:])
    return {
        "x": tiles(x.transpose(1, 0, 2)).transpose(1, 0, 2, 3),
        "xT": x.transpose(2, 0, 1),
        "adj": tiles(adj).transpose(1, 0, 2),
        "adjT": tiles(adj.T).transpose(1, 0, 2),
        "H": tiles(H).transpose(1, 0, 2),
        "HT": H.T,
        "W0": v["L0_gnn_W"], "W0T": v["L0_gnn_W"].T, "Wind": v["L0_gnn_W_ind"],
        "a_node": v["L0_gnn_a_node"][:, None], "a_gn": v["L0_gnn_a_gn"][:, None], "a_ge": v["L0_gnn_a_ge"][:, None],
        "fcW": v["L0_gnn_fcW"], "fcb": v["L0_gnn_fcb"][:, None], "av": v["L0_gnn_av"][:, None],
        "Wh": v["L1_gnn_Wh"].transpose(1, 0, 2),
        "WhT": v["L1_gnn_Wh"].transpose(2, 0, 1),
        "bh": v["L1_gnn_bh"].T,
        "Wout": v["L1_gnn_W_out"].reshape(HEADS, HID, D).transpose(1, 0, 2),
        "bout": v["L1_gnn_b_out"][None, :],
        "iv": v["L2_gnn_intervention_value"],
        "W1T": v["L2_gnn_W1"].T, "b1": v["L2_gnn_b1"][:, None],
        "W2T": v["L2_gnn_W2"].T, "b2": v["L2_gnn_b2"][:, None], "b2row": v["L2_gnn_b2"][None, :],
        "W3": v["L3_gnn_W"], "W3T": v["L3_gnn_W"].T, "a3": v["L3_gnn_a"].reshape(2, D).T,
    }


def kernel(**inputs):
    import concourse.bacc as bacc
    from concourse.bass_utils import run_bass_kernel_spmd

    nc = bacc.Bacc("TRN2", target_bir_lowering=False, num_devices=1)
    arrays, w = {}, {}
    for name, a in host_layout({k: np.asarray(v) for k, v in inputs.items()}).items():
        a = np.ascontiguousarray(a)
        arrays["in_" + name] = a
        w[name] = nc.dram_tensor("in_" + name, a.shape, mybir.dt.from_np(a.dtype), kind="ExternalInput").ap()
    out = nc.dram_tensor("out_x", [P, NT, B, D], F32, kind="ExternalOutput").ap()
    build(nc, w, out)
    r = run_bass_kernel_spmd(nc, [arrays], core_ids=[0])
    got = np.asarray(r.results[0]["out_x"])
    return np.ascontiguousarray(got.transpose(2, 1, 0, 3).reshape(B, N, D))
```
